# Optimizing a Trainium2 kernel written in Bass

```python
import numpy as np
import jax
import jax.numpy as jnp

def _softmax(x, axis=-1):
    return jax.nn.softmax(x, axis=axis)

def _gelu(x):
    return jax.nn.gelu(x, approximate=True)

def _silu(x):
    return jax.nn.silu(x)

def _sigmoid(x):
    return jax.nn.sigmoid(x)

def _layernorm(x, axis=-1, eps=1e-05):
    m = jnp.mean(x, axis=axis, keepdims=True)
    v = jnp.var(x, axis=axis, keepdims=True)
    return (x - m) / jnp.sqrt(v + eps)

def _scatter_add(tgt, idx, src, axis=0):
    return tgt.at[idx].add(src)

def _segment_sum(src, seg, n):
    return jax.ops.segment_sum(src, seg, n)
kernel_name = 'mk_gps_d1_gnn_r8_08d57d'

def setup_inputs(seed: int=0):
    np.random.seed(seed)
    _w = jnp.asarray

    def _rec_inputs():
        import jax
        import jax.numpy as jnp
        _gk = jax.random.key(seed)
        x = -8.776e-05 + 1 * jax.random.normal(jax.random.fold_in(_gk, 1), (1250, 512), jnp.float32)
        src = jax.random.randint(jax.random.fold_in(_gk, 2), (40000,), 0, 1250, jnp.int32)
        dst = jnp.minimum((1250 * jax.random.uniform(jax.random.fold_in(_gk, 3), (40000,)) ** 2.0).astype(jnp.int32), 9999)
        _o = jnp.argsort(dst, stable=True)
        src = src[_o]
        dst = dst[_o]
        edge_attr_128 = 0.000283511 + 1.00007 * jax.random.normal(jax.random.fold_in(_gk, 11), (40000, 128), jnp.float32)
        return (x, src, dst, edge_attr_128)
    x, src, dst, edge_attr_128 = _rec_inputs()

    def _L0_gnn_setup():
        import jax, jax.numpy as jnp
        import numpy as np
        N, E = (1250, 18750)
        HD, ED = (512, 128)
        BN_EPS = 1e-05
        key = jax.random.key(seed)
        ks = jax.random.split(key, 16)
        s = 0.02
        return {'h': jax.random.normal(ks[0], (N, HD), jnp.float32), 'edge_index': jax.random.randint(ks[1], (2, E), 0, N, jnp.int32), 'edge_attr': jax.random.normal(ks[2], (E, ED), jnp.float32), 'W1': jax.random.normal(ks[3], (HD, HD + ED), jnp.float32) * s, 'b1': jnp.zeros((HD,), jnp.float32), 'W2': jax.random.normal(ks[4], (HD, HD), jnp.float32) * s, 'b2': jnp.zeros((HD,), jnp.float32), 'W_ih': jax.random.normal(ks[5], (3 * HD, HD), jnp.float32) * s, 'W_hh': jax.random.normal(ks[6], (3 * HD, HD), jnp.float32) * s, 'b_ih': jnp.zeros((3 * HD,), jnp.float32), 'b_hh': jnp.zeros((3 * HD,), jnp.float32), 'gamma': jnp.ones((HD,), jnp.float32), 'beta': jnp.zeros((HD,), jnp.float32), 'run_mean': jnp.zeros((HD,), jnp.float32), 'run_var': jnp.ones((HD,), jnp.float32)}
    _L0_gnn_all = _L0_gnn_setup()
    _L0_gnn_in = {k: v for k, v in _L0_gnn_all.items() if k in ('W1', 'b1', 'W2', 'b2', 'W_ih', 'W_hh', 'b_ih', 'b_hh', 'gamma', 'beta', 'run_mean', 'run_var')}
    del _L0_gnn_all

    def _L0_mix_setup():
        import jax, jax.numpy as jnp
        import numpy as np
        B, S, DM = (4, 1024, 512)
        H = 8
        D = DM // H

        def _feature_map(t):
            return jax.nn.elu(t) + 1.0
        key = jax.random.key(seed)
        ks = jax.random.split(key, 9)
        s = 1.0 / np.sqrt(DM)
        x = jax.random.normal(ks[0], (B, S, DM), dtype=jnp.float32)
        Wq = jax.random.normal(ks[1], (DM, DM), dtype=jnp.float32) * s
        bq = jnp.zeros((DM,), dtype=jnp.float32)
        Wk = jax.random.normal(ks[2], (DM, DM), dtype=jnp.float32) * s
        bk = jnp.zeros((DM,), dtype=jnp.float32)
        Wv = jax.random.normal(ks[3], (DM, DM), dtype=jnp.float32) * s
        bv = jnp.zeros((DM,), dtype=jnp.float32)
        Wp = jax.random.normal(ks[4], (DM, DM), dtype=jnp.float32) * s
        bp = jnp.zeros((DM,), dtype=jnp.float32)
        return {'x': x, 'Wq': Wq, 'bq': bq, 'Wk': Wk, 'bk': bk, 'Wv': Wv, 'bv': bv, 'Wp': Wp, 'bp': bp}
    _L0_mix_all = _L0_mix_setup()
    _L0_mix_in = {k: v for k, v in _L0_mix_all.items() if k in ('Wq', 'bq', 'Wk', 'bk', 'Wv', 'bv', 'Wp', 'bp')}
    del _L0_mix_all

    def _L0_ffn_setup():
        import jax, jax.numpy as jnp
        import numpy as np
        B, S, D, H, E = (4, 1024, 512, 256, 8)
        key = jax.random.key(seed)
        ks = jax.random.split(key, 7)
        scale = 1.0 / np.sqrt(D)
        return {'x': jax.random.normal(ks[0], (B, S, D), dtype=jnp.float32), 'Wg': jax.random.normal(ks[1], (D, E), dtype=jnp.float32) * scale, 'bg': jnp.zeros((E,), dtype=jnp.float32), 'W1': jax.random.normal(ks[2], (E, D, H), dtype=jnp.float32) * scale, 'b1': jnp.zeros((E, H), dtype=jnp.float32), 'W2': jax.random.normal(ks[3], (E, H, D), dtype=jnp.float32) * (1.0 / np.sqrt(H)), 'b2': jnp.zeros((E, D), dtype=jnp.float32)}
    _L0_ffn_all = _L0_ffn_setup()
    _L0_ffn_in = {k: v for k, v in _L0_ffn_all.items() if k in ('Wg', 'bg', 'W1', 'b1', 'W2', 'b2')}
    del _L0_ffn_all
    return {'x': x, 'src': src, 'dst': dst, 'edge_attr_128': edge_attr_128, 'L0_gnn_W1': _L0_gnn_in['W1'], 'L0_gnn_b1': _L0_gnn_in['b1'], 'L0_gnn_W2': _L0_gnn_in['W2'], 'L0_gnn_b2': _L0_gnn_in['b2'], 'L0_gnn_W_ih': _L0_gnn_in['W_ih'], 'L0_gnn_W_hh': _L0_gnn_in['W_hh'], 'L0_gnn_b_ih': _L0_gnn_in['b_ih'], 'L0_gnn_b_hh': _L0_gnn_in['b_hh'], 'L0_gnn_gamma': _L0_gnn_in['gamma'], 'L0_gnn_beta': _L0_gnn_in['beta'], 'L0_gnn_run_mean': _L0_gnn_in['run_mean'], 'L0_gnn_run_var': _L0_gnn_in['run_var'], 'L0_mix_Wq': _L0_mix_in['Wq'], 'L0_mix_bq': _L0_mix_in['bq'], 'L0_mix_Wk': _L0_mix_in['Wk'], 'L0_mix_bk': _L0_mix_in['bk'], 'L0_mix_Wv': _L0_mix_in['Wv'], 'L0_mix_bv': _L0_mix_in['bv'], 'L0_mix_Wp': _L0_mix_in['Wp'], 'L0_mix_bp': _L0_mix_in['bp'], 'L0_ffn_Wg': _L0_ffn_in['Wg'], 'L0_ffn_bg': _L0_ffn_in['bg'], 'L0_ffn_W1': _L0_ffn_in['W1'], 'L0_ffn_b1': _L0_ffn_in['b1'], 'L0_ffn_W2': _L0_ffn_in['W2'], 'L0_ffn_b2': _L0_ffn_in['b2']}

def reference(x, src, dst, edge_attr_128, L0_gnn_W1, L0_gnn_b1, L0_gnn_W2, L0_gnn_b2, L0_gnn_W_ih, L0_gnn_W_hh, L0_gnn_b_ih, L0_gnn_b_hh, L0_gnn_gamma, L0_gnn_beta, L0_gnn_run_mean, L0_gnn_run_var, L0_mix_Wq, L0_mix_bq, L0_mix_Wk, L0_mix_bk, L0_mix_Wv, L0_mix_bv, L0_mix_Wp, L0_mix_bp, L0_ffn_Wg, L0_ffn_bg, L0_ffn_W1, L0_ffn_b1, L0_ffn_W2, L0_ffn_b2):
    import jax
    import jax.numpy as jnp

    def _L0_gnn_ref(h, edge_index, edge_attr, W1, b1, W2, b2, W_ih, W_hh, b_ih, b_hh, gamma, beta, run_mean, run_var):
        import jax, jax.numpy as jnp
        import numpy as np
        N, E = (1250, 18750)
        HD, ED = (512, 128)
        BN_EPS = 1e-05
        src, dst = (edge_index[0], edge_index[1])
        m_in = jnp.concatenate([h[src], edge_attr], axis=1)
        m = jax.nn.relu(m_in @ W1.T + b1) @ W2.T + b2
        agg = jax.ops.segment_sum(m, dst, num_segments=h.shape[0])
        gi = agg @ W_ih.T + b_ih
        gh = h @ W_hh.T + b_hh
        i_r, i_z, i_n = jnp.split(gi, 3, axis=1)
        h_r, h_z, h_n = jnp.split(gh, 3, axis=1)
        r = jax.nn.sigmoid(i_r + h_r)
        z = jax.nn.sigmoid(i_z + h_z)
        n = jnp.tanh(i_n + r * h_n)
        h_new = (1.0 - z) * n + z * h
        bn = gamma * (h_new - run_mean) * jax.lax.rsqrt(run_var + BN_EPS) + beta
        return h + bn

    def _L0_mix_ref(x, Wq, bq, Wk, bk, Wv, bv, Wp, bp):
        import jax, jax.numpy as jnp
        import numpy as np
        B, S, DM = (4, 1024, 512)
        H = 8
        D = DM // H

        def _feature_map(t):
            return jax.nn.elu(t) + 1.0
        b, s, _ = x.shape
        q = _feature_map(x @ Wq + bq).reshape(b, s, H, D)
        k = _feature_map(x @ Wk + bk).reshape(b, s, H, D)
        v = (x @ Wv + bv).reshape(b, s, H, D)
        kv = jnp.einsum('bshd,bshe->bhde', k, v)
        z = 1.0 / jnp.einsum('bshd,bhd->bsh', q, k.sum(axis=1))
        out = jnp.einsum('bshd,bhde,bsh->bshe', q, kv, z)
        out = out.reshape(b, s, H * D)
        return out @ Wp + bp

    def _L0_ffn_ref(x, Wg, bg, W1, b1, W2, b2):
        import jax, jax.numpy as jnp
        import numpy as np
        B, S, D, H, E = (4, 1024, 512, 256, 8)
        b, s, d = x.shape
        xf = x.reshape(-1, d)
        logits = xf @ Wg + bg
        scores = jax.nn.softmax(logits, axis=-1)
        top_s, top_i = jax.lax.top_k(scores, 1)
        idx = top_i[:, 0]
        sc = top_s[:, 0]
        n_experts = Wg.shape[1]
        out = jnp.zeros_like(xf)
        for e in range(n_experts):
            h = jax.nn.relu(xf @ W1[e] + b1[e]) @ W2[e] + b2[e]
            out = jnp.where((idx == e)[:, None], h, out)
        out = out * sc[:, None]
        return out.reshape(b, s, d)
    edge_index = jnp.stack([src, dst])
    xn = _layernorm(x, axis=-1)
    x = x + _L0_gnn_ref(xn, edge_index, edge_attr_128, L0_gnn_W1, L0_gnn_b1, L0_gnn_W2, L0_gnn_b2, L0_gnn_W_ih, L0_gnn_W_hh, L0_gnn_b_ih, L0_gnn_b_hh, L0_gnn_gamma, L0_gnn_beta, L0_gnn_run_mean, L0_gnn_run_var) + _L0_mix_ref(xn[None], L0_mix_Wq, L0_mix_bq, L0_mix_Wk, L0_mix_bk, L0_mix_Wv, L0_mix_bv, L0_mix_Wp, L0_mix_bp)[0]
    x = x + _L0_ffn_ref(_layernorm(x, axis=-1)[None], L0_ffn_Wg, L0_ffn_bg, L0_ffn_W1, L0_ffn_b1, L0_ffn_W2, L0_ffn_b2)[0]
    return x

_drawn_inputs = setup_inputs


def setup_inputs(seed=0):
    import zlib

    import numpy as np

    out = dict(_drawn_inputs(seed))
    spreads = {'L0_gnn_b1': (0.0, 0.1),
     'L0_gnn_b2': (0.0, 0.1),
     'L0_gnn_b_ih': (0.0, 0.389),
     'L0_gnn_b_hh': (0.0, 0.556),
     'L0_gnn_gamma': (1.0, 0.2),
     'L0_gnn_beta': (0.0, 0.1),
     'L0_gnn_run_mean': (0.0, 0.1),
     'L0_gnn_run_var': (1.0, 0.2),
     'L0_mix_bq': (0.0, 0.8),
     'L0_mix_bk': (0.0, 0.8),
     'L0_mix_bv': (0.0, 0.1),
     'L0_mix_bp': (0.0, 0.1),
     'L0_ffn_bg': (0.0, 0.385),
     'L0_ffn_b1': (0.0, 0.754),
     'L0_ffn_b2': (0.0, 0.524)}
    factors = {'L0_mix_Wq': 8.0, 'L0_mix_Wk': 8.0, 'L0_mix_Wv': 4.158}
    for name, (base, spread) in spreads.items():
        noise = np.random.default_rng([zlib.crc32(name.encode()), seed]).standard_normal(out[name].shape)
        drawn = base * np.exp(spread * noise) if base else spread * noise
        out[name] = jnp.asarray(drawn.astype(out[name].dtype))
    for name, factor in factors.items():
        out[name] = (out[name] * factor).astype(out[name].dtype)
    return out
```

```python
from contextlib import ExitStack

import concourse.bass as bass
from concourse import mybir

F32 = mybir.dt.float32
F32R = mybir.dt.float32r
I32 = mybir.dt.int32
ALU = mybir.AluOpType
ACT = mybir.ActivationFunctionType
AX_X = mybir.AxisListType.X

N, D, E, ED = 1250, 512, 40000, 128
TP = 125
NT = N // TP
KC = D // 128
TG = 4
EG = TP * TG
NG = E // EG
HEADS, DH = 8, 64
NX, HX = 8, 256
TS = 128
NST = (N + NX * (TS - 1)) // TS
NSLOT = NST * TS
EPS = 1e-5
SLICES = [(0, 418), (418, 416), (834, 416)]
TWO_PASS = (0, 2)
SCALE_X0 = 256


class Counter:

    def __init__(self, sem):
        self.sem, self.n = sem, 0

    def link(self, eng, ins):
        ins.then_inc(self.sem, 1)
        self.n += 1
        eng.wait_ge(self.sem, self.n)


def rows_dma(eng, dst, src, sem):
    eng.dma_start(dst[0:112], src[0:112]).then_inc(sem, 16)
    eng.dma_start(dst[112:TP], src[112:TP]).then_inc(sem, 16)


def build(nc, x_nodes, x_feat, src_cols, dst_cols, dst_groups, edge_blocks, w1a, w1b, wk, wv, wq, wp, w2,
          gate_blocks, wg, we1, we2, b1, bk, bv, b2, cols, bg, be1, be2, proj, slot_in, slot_out, out):
    with ExitStack() as ctx:
        def sb(name, shape, dt=F32, at=ctx):
            return at.enter_context(nc.sbuf_tensor(name, shape, dt))

        def sem(name):
            return ctx.enter_context(nc.semaphore(name))

        bank = [ctx.enter_context(nc.psum_tensor(f"bank{i}", [128, 512], F32)) for i in range(8)]

        base = sb("base", [128, KC, N])
        xn = sb("xn", [128, KC, N])
        nodes = sb("nodes", [TP, NT, D])
        ident = sb("ident", [128, 128])
        ones = sb("ones", [128, 128])
        bc = sb("bc", [128, 12, KC])
        COL = {n: bc[:, i, :] for i, n in enumerate(
            ["bq", "bp", "bir", "biz", "bin", "bhr", "bhz", "bhn", "gamma", "beta", "mean", "var"])}
        gscale = sb("gscale", [128, KC])
        gshift = sb("gshift", [128, KC])
        brz = sb("brz", [128, 2, KC])
        word = sb("word", [1, NG], I32)
        further = sb("further", [1, NG * 4], I32)
        dst_rel = sb("dst_rel", [TP, NG * TG])
        dst_f = sb("dst_f", [TP, NG * TG])
        deg = sb("deg", [TP, NT, 2])
        stat = sb("stat", [TP, NT, 6])
        mv = sb("mv", [TP, NT, 2])
        rstd = sb("rstd", [TP, NT])
        tmp_s = sb("tmp_s", [TP, NT])
        tmp_t = sb("tmp_t", [TP, NT])
        tmp_c = sb("tmp_c", [128, 3, KC])

        dve_chain, act_chain, pool_chain = (Counter(sem(n)) for n in ("dve_chain", "act_chain", "pool_chain"))
        epsc = sb("epsc", [128, 1])
        pool_step = sb("pool_step", [1, 2])
        zeros = sb("zeros", [128, 128])

        def newton_rsqrt(dve, r, v, a, b):
            L = dve_chain.link
            L(dve, nc.vector.reciprocal(a, r))
            L(dve, nc.vector.tensor_tensor(b, a, a, ALU.mult))
            L(dve, nc.vector.tensor_tensor(b, b, v, ALU.mult))
            L(dve, nc.vector.tensor_scalar(b, b, -0.5, 1.5, ALU.mult, ALU.add))
            L(dve, nc.vector.tensor_tensor(r, a, b, ALU.mult))

        split = ExitStack()
        xh = sb("xh", [128, KC, N], F32R, split)
        xl = sb("xl", [128, KC, N], F32R, split)

        s1 = ExitStack()
        dstg_i = sb("dstg_i", [NG, EG], I32, s1)
        dstg = sb("dstg", [NG, EG], F32, s1)
        dstc_i = sb("dstc_i", [TP, NG * TG], I32, s1)
        mm = sb("mm", [NG, 2], F32, s1)
        win = sb("win", [NG, 2], F32, s1)
        extra = sb("extra", [NG, 1], F32, s1)
        upper = sb("upper", [NG, NG], F32, s1)
        diag = sb("diag", [NG, NG], F32, s1)
        rows = sb("rows", [1, 3, NG], F32, s1)
        r1 = sb("r1", [1, NG], F32, s1)
        x_loaded = [sem(f"x_loaded{h}") for h in range(2)]
        dst_loaded, cols_loaded, feat_loaded = (sem(n) for n in ("dst_loaded", "cols_loaded", "feat_loaded"))
        consts_made, stats_made, std_made, centred, turned, turned_used, high1 = (sem(n) for n in (
            "consts_made", "stats_made", "std_made", "centred", "turned", "turned_used", "high1"))
        win_made, rows_ready, diag_made, spread_ready, table_zeroed = (sem(n) for n in (
            "win_made", "rows_ready", "diag_made", "spread_ready", "table_zeroed"))
        zeros_made = sem("zeros_made")

        with nc.Block() as block:
            @block.sync
            def _(sp):
                for h in range(2):
                    rows_dma(sp, nodes[:, 5 * h:5 * h + 5, :],
                             x_nodes.rearrange("(t p) f -> p t f", p=TP)[:, 5 * h:5 * h + 5, :], x_loaded[h])
                sp.dma_start(dstg_i[:, :], dst_groups).then_inc(dst_loaded, 16)
                sp.dma_start(dstc_i[:, :], dst_cols).then_inc(dst_loaded, 16)
                sp.dma_start(bc[:, :, :], cols).then_inc(cols_loaded, 16)
                sp.dma_start(base[:, :, :], x_feat.rearrange("(k p) n -> p k n", p=128)).then_inc(feat_loaded, 16)
                sp.wait_ge(zeros_made, 1)
                for i in range(NST):
                    sp.dma_start(slot_in[i * TS:(i + 1) * TS, :].rearrange("p (a f) -> p a f", f=128),
                                 zeros[:, :].unsqueeze(1).to_broadcast([TS, D // 128, 128])).then_inc(table_zeroed, 16)

            @block.gpsimd
            def _(pool):
                nc.gpsimd.memset(zeros[:, :], 0.0).then_inc(zeros_made, 1)
                pool_chain.link(pool, nc.gpsimd.memset(ones[:, :], 1.0))
                pool_chain.link(pool, nc.gpsimd.memset(epsc[:, :], EPS))
                nc.gpsimd.affine_select(out=ident[:, :], in_=ones[:, :], compare_op=ALU.is_equal, fill=0.0,
                                        base=0, pattern=[[-1, 128]], channel_multiplier=1).then_inc(consts_made, 1)
                nc.gpsimd.affine_select(out=upper[:, :], in_=ones[0:NG, 0:NG], compare_op=ALU.is_gt, fill=0.0,
                                        base=0, pattern=[[1, NG]], channel_multiplier=-1).then_inc(consts_made, 1)

            @block.scalar
            def _(act):
                act.wait_ge(stats_made, 1)
                act.wait_ge(consts_made, 2)
                nc.scalar.activation(rstd[:, :], mv[:, :, 1], ACT.Sqrt, bias=epsc[0:TP, :]).then_inc(std_made, 1)
                act.wait_ge(cols_loaded, 16)
                nc.scalar.activation(gscale[:, :], COL["var"], ACT.Sqrt, bias=epsc[:, :]).then_inc(std_made, 1)
                for t in range(NT):
                    act.wait_ge(turned, t + 1)
                    s = slice(t * TP, (t + 1) * TP)
                    pb = bank[t % 4][:, 0:KC * TP].rearrange("p (k n) -> p k n", k=KC)
                    nc.scalar.copy(xn[:, :, s], pb)
                    nc.scalar.copy(xh[:, :, s], pb).then_inc(high1, 1)

            @block.vector
            def _(dve):
                L = dve_chain.link
                for t in range(NT):
                    if t % 5 == 0:
                        dve.wait_ge(x_loaded[t // 5], 32)
                    L(dve, nc.vector.bn_stats(stat[:, t, :], nodes[:, t, :]))
                    last = nc.vector.bn_aggr(mv[:, t, :], stat[:, t, :])
                last.then_inc(stats_made, 1)
                dve.wait_ge(stats_made, 1)
                L(dve, nc.vector.tensor_scalar(tmp_t[:, :], mv[:, :, 1], EPS, None, ALU.add))
                dve.wait_ge(std_made, 1)
                newton_rsqrt(dve, rstd[:, :], tmp_t[:, :], tmp_s[:, :], stat[:, :, 0])
                for t in range(NT):
                    nc.vector.tensor_scalar(nodes[:, t, :], nodes[:, t, :], mv[:, t, 0:1], rstd[:, t:t + 1],
                                            ALU.subtract, ALU.mult).then_inc(centred, 1)
                dve.wait_ge(dst_loaded, 32)
                L(dve, nc.vector.tensor_copy(dstg[:, :], dstg_i[:, :]))
                nc.vector.tensor_copy(dst_f[:, :], dstc_i[:, :])
                nc.vector.tensor_reduce(mm[:, 0:1], dstg[:, :], AX_X, ALU.min)
                L(dve, nc.vector.tensor_reduce(mm[:, 1:2], dstg[:, :], AX_X, ALU.max))
                L(dve, nc.vector.tensor_scalar(win[:, :], mm[:, :], float(TP), None, ALU.is_ge))
                for w in range(2, NT):
                    L(dve, nc.vector.scalar_tensor_tensor(win[:, :], mm[:, :], float(TP * w), win[:, :],
                                                          ALU.is_ge, ALU.add))
                nc.vector.tensor_tensor(extra[:, :], win[:, 1:2], win[:, 0:1], ALU.subtract).then_inc(win_made, 1)
                dve.wait_ge(consts_made, 2)
                nc.vector.tensor_scalar(diag[:, :], ident[0:NG, 0:NG], win[:, 0:1], float(TP),
                                        ALU.mult, ALU.mult).then_inc(diag_made, 1)
                for t in range(NT):
                    dve.wait_ge(high1, t + 1)
                    pb = bank[t % 4][:, 0:KC * TP].rearrange("p (k n) -> p k n", k=KC)
                    s = slice(t * TP, (t + 1) * TP)
                    nc.vector.tensor_tensor(xl[:, :, s], pb, xh[:, :, s], ALU.subtract).then_inc(turned_used, 1)
                dve.wait_ge(rows_ready, 1)
                pr = bank[6][0:1, 0:3 * NG].rearrange("p (a g) -> p a g", a=3)
                L(dve, nc.vector.tensor_copy(rows[:, :, :], pr))
                lo, ex, x0 = rows[:, 0, :], rows[:, 1, :], rows[:, 2, :]
                L(dve, nc.vector.scalar_tensor_tensor(r1[:, :], x0, float(SCALE_X0 // 16), ex, ALU.mult, ALU.add))
                L(dve, nc.vector.scalar_tensor_tensor(word[:, :], r1[:, :], 16.0, lo, ALU.mult, ALU.add))
                ft = further[:, :].rearrange("p (g a) -> p g a", a=4)
                nc.vector.tensor_copy(ft[:, :, 0], x0)
                nc.vector.tensor_tensor(ft[:, :, 1], x0, ex, ALU.add)
                L(dve, nc.vector.scalar_tensor_tensor(r1[:, :], x0, -1.0, lo, ALU.mult, ALU.add))
                L(dve, nc.vector.tensor_scalar(ft[:, :, 2], r1[:, :], float(NG * NT), None, ALU.add))
                dve.wait_ge(spread_ready, 1)
                L(dve, nc.vector.tensor_tensor(
                    dst_rel[:, :].rearrange("p (g t) -> p g t", t=TG),
                    dst_f[:, :].rearrange("p (g t) -> p g t", t=TG),
                    bank[7][0:TP, 0:NG].unsqueeze(2).to_broadcast([TP, NG, TG]), ALU.subtract))
                L(dve, nc.vector.tensor_scalar(tmp_c[:, 0, :], COL["var"], EPS, None, ALU.add))
                dve.wait_ge(std_made, 2)
                newton_rsqrt(dve, gscale[:, :], tmp_c[:, 0, :], tmp_c[:, 1, :], tmp_c[:, 2, :])
                L(dve, nc.vector.tensor_tensor(gscale[:, :], gscale[:, :], COL["gamma"], ALU.mult))
                L(dve, nc.vector.tensor_tensor(gshift[:, :], gscale[:, :], COL["mean"], ALU.mult))
                L(dve, nc.vector.tensor_tensor(gshift[:, :], COL["beta"], gshift[:, :], ALU.subtract))
                L(dve, nc.vector.tensor_tensor(gshift[:, :], gshift[:, :], COL["bp"], ALU.add))
                nc.vector.tensor_tensor(brz[:, 0, :], COL["bir"], COL["bhr"], ALU.add)
                L(dve, nc.vector.tensor_tensor(brz[:, 1, :], COL["biz"], COL["bhz"], ALU.add))

            @block.tensor
            def _(pe):
                pe.wait_ge(consts_made, 2)
                for t in range(NT):
                    pe.wait_ge(centred, t + 1)
                    if t >= 4:
                        pe.wait_ge(turned_used, t - 3)
                    for k in range(KC):
                        last = nc.tensor.transpose(bank[t % 4][:, k * TP:(k + 1) * TP],
                                                   nodes[:, t, k * 128:(k + 1) * 128], ident[0:TP, 0:TP])
                    last.then_inc(turned, 1)
                pe.wait_ge(win_made, 1)
                nc.tensor.matmul(bank[6][0:1, 0:NG], win[:, 0:1], ident[0:NG, 0:NG], start=True, stop=True)
                nc.tensor.matmul(bank[6][0:1, NG:2 * NG], extra[:, :], ident[0:NG, 0:NG], start=True, stop=True)
                nc.tensor.matmul(bank[6][0:1, 2 * NG:3 * NG], extra[:, :], upper[:, :],
                                 start=True, stop=True).then_inc(rows_ready, 1)
                pe.wait_ge(diag_made, 1)
                nc.tensor.matmul(bank[7][0:TP, 0:NG], ones[0:NG, 0:TP], diag[:, :],
                                 start=True, stop=True).then_inc(spread_ready, 1)
        s1.close()

        s2 = ExitStack()
        kf = sb("kf", [TP, NT, D], F32, s2)
        qf = sb("qf", [128, KC, N], F32, s2)
        w_raw = [sb(f"w_raw{i}", [128, 2, D], F32, s2) for i in range(2)]
        w_hi = [sb(f"w_hi{i}", [128, KC, D], F32R, s2) for i in range(2)]
        w_lo = [sb(f"w_lo{i}", [128, KC, D], F32R, s2) for i in range(2)]
        bias_row = sb("bias_row", [TP, 3, D], F32, s2)
        row_out = [sb(f"row_out{i}", [TP, D], F32, s2) for i in range(2)]
        exp_t = [sb(f"exp_t{i}", [128, D], F32, s2) for i in range(2)]
        relu_t = [sb(f"relu_t{i}", [128, D], F32, s2) for i in range(2)]
        kv_sb = sb("kv_sb", [128, KC, 128], F32, s2)
        ksum8 = sb("ksum8", [128, KC, HEADS], F32, s2)
        rden = sb("rden", [TP, NT * HEADS], F32, s2)
        rden_t = kf[0:HEADS, :, :].rearrange("p t f -> p (t f)")[:, 0:N]
        head_rows = sb("head_rows", [HEADS, D], F32, s2)
        v_nodes = nodes
        UNITS = 5
        w_loaded = [sem(f"w_loaded{i}") for i in range(2)]
        w_high, w_low, out_ready = (sem(n) for n in (
            "w_high", "w_low", "out_ready"))
        proj_made, proj_stored, k_biased, k_parts, k_made, v_made, q_parts, q_made = (sem(n) for n in (
            "proj_made", "proj_stored", "k_biased", "k_parts", "k_made", "v_made", "q_parts", "q_made"))
        proj_stored = [proj_stored, sem("proj_stored1")]
        bias_loaded, kv_ready, kv_made, den_ready, rden_made, rdent_ready, rdent_made = (sem(n) for n in (
            "bias_loaded", "kv_ready", "kv_made", "den_ready", "rden_made", "rdent_ready", "rdent_made"))
        att_ready, rb_copied, att_made, att_high, att_low, base_made, s2_zeroed = (sem(n) for n in (
            "att_ready", "rb_copied", "att_made", "att_high", "att_low", "base_made", "s2_zeroed"))
        mix_ready, mix_added = sem("mix_ready"), sem("mix_added")
        att_f = exp_t
        rb_sb = relu_t

        def product3(out_ap, lhs, rhs, first, last):
            nc.tensor.matmul(out_ap, lhs[0], rhs[0], start=first, stop=False)
            nc.tensor.matmul(out_ap, lhs[0], rhs[1], start=False, stop=False)
            return nc.tensor.matmul(out_ap, lhs[1], rhs[0], start=False, stop=last)

        QJ = [(c, s) for c in range(KC) for s in range(len(SLICES))]

        with nc.Block() as block:
            @block.sync
            def _(sp):
                sp.dma_start(bias_row[:, 0, :], b1.unsqueeze(0).to_broadcast([TP, D])).then_inc(bias_loaded, 16)
                sp.dma_start(bias_row[:, 1, :], bk.unsqueeze(0).to_broadcast([TP, D])).then_inc(bias_loaded, 16)
                sp.dma_start(bias_row[:, 2, :], bv.unsqueeze(0).to_broadcast([TP, D])).then_inc(bias_loaded, 16)

                def load(h):
                    w = (w1a, wk, wv, wq, wp)[h // 2]
                    if h >= 2:
                        sp.wait_ge(w_low, h - 1)
                    sp.dma_start(w_raw[h % 2][:, :, :], w.rearrange("(k p) f -> p k f", p=128)[
                        :, 2 * (h % 2):2 * (h % 2) + 2, :]).then_inc(w_loaded[h % 2], 16)

                for h in range(4):
                    load(h)
                for t in range(NT):
                    sp.wait_ge(proj_made, t + 1)
                    rows_dma(sp, proj[t * TP:(t + 1) * TP, :], row_out[t % 2], proj_stored[t % 2])
                for h in range(4, 2 * UNITS):
                    load(h)
                sp.wait_ge(proj_stored[0], 32 * 5)
                sp.wait_ge(proj_stored[1], 32 * 5)

            @block.gpsimd
            def _(pool):
                nc.gpsimd.memset(kv_sb[:, :, :], 0.0)
                nc.gpsimd.memset(ksum8[:, :, :], 0.0)
                hr = head_rows[:, :]
                pool_chain.link(pool, nc.gpsimd.memset(hr, 1.0))
                pool_chain.link(pool, nc.gpsimd.affine_select(
                    out=hr, in_=hr, compare_op=ALU.is_ge, fill=0.0, base=0, pattern=[[1, D]], channel_multiplier=-DH))
                nc.gpsimd.affine_select(out=hr, in_=hr, compare_op=ALU.is_ge, fill=0.0, base=DH - 1,
                                        pattern=[[-1, D]], channel_multiplier=DH).then_inc(s2_zeroed, 1)
                pool.wait_ge(feat_loaded, 16)
                nc.gpsimd.tensor_tensor(base[:, :, :], base[:, :, :], xn[:, :, :], ALU.add).then_inc(base_made, 1)

            @block.scalar
            def _(act):
                def high(u):
                    if u >= 2:
                        act.wait_ge(out_ready, (u - 1) * NT)
                    for h in (2 * u, 2 * u + 1):
                        act.wait_ge(w_loaded[h % 2], 16 * (u + 1))
                        kk = slice(2 * (h % 2), 2 * (h % 2) + 2)
                        nc.scalar.copy(w_hi[u % 2][:, kk, :], w_raw[h % 2][:, :, :]).then_inc(w_high, 1)

                high(0)
                high(1)
                high(2)
                for t in range(NT):
                    act.wait_ge(k_biased, t + 1)
                    nc.scalar.activation(exp_t[t % 2][0:TP, :], row_out[t % 2][:, :], ACT.Exp)
                    nc.scalar.activation(relu_t[t % 2][0:TP, :], row_out[t % 2][:, :], ACT.Relu).then_inc(k_parts, 1)
                high(3)
                high(4)
                for j, (c, s) in enumerate(QJ):
                    a, n = SLICES[s]
                    act.wait_ge(out_ready, 3 * NT + j + 1)
                    if j < 2:
                        act.wait_ge(k_made, NT)
                    else:
                        act.wait_ge(q_made, j - 1)
                    pb = bank[(3 * NT + j) % 6][:, 0:n]
                    nc.scalar.activation(exp_t[j % 2][:, 0:n], pb, ACT.Exp, bias=COL["bq"][:, c:c + 1])
                    nc.scalar.activation(relu_t[j % 2][:, 0:n], pb, ACT.Relu,
                                         bias=COL["bq"][:, c:c + 1]).then_inc(q_parts, 1)
                for i in range(3):
                    act.wait_ge(rdent_ready, i + 1)
                    n = min(4, NT - 4 * i) * TP
                    nc.scalar.copy(rden_t[:, 4 * i * TP:4 * i * TP + n],
                                   bank[1 + i][0:HEADS, 0:n]).then_inc(rdent_made, 1)
                for j, (c, s) in enumerate(QJ):
                    a, n = SLICES[s]
                    act.wait_ge(att_ready, j + 1)
                    if j >= 2:
                        act.wait_ge(att_made, j - 1)
                    nc.scalar.copy(rb_sb[j % 2][:, 0:n], bank[6 + j % 2][:, 0:n]).then_inc(rb_copied, 1)
                    act.wait_ge(att_made, j + 1)
                    nc.scalar.copy(xh[:, c, a:a + n], att_f[j % 2][:, 0:n]).then_inc(att_high, 1)

            @block.vector
            def _(dve):
                def low(u):
                    for h in (2 * u, 2 * u + 1):
                        dve.wait_ge(w_high, h + 1)
                        kk = slice(2 * (h % 2), 2 * (h % 2) + 2)
                        nc.vector.tensor_tensor(w_lo[u % 2][:, kk, :], w_raw[h % 2][:, :, :],
                                                w_hi[u % 2][:, kk, :], ALU.subtract).then_inc(w_low, 1)

                low(0)
                low(1)
                dve.wait_ge(bias_loaded, 48)
                for t in range(NT):
                    dve.wait_ge(out_ready, t + 1)
                    if t >= 2:
                        dve.wait_ge(proj_stored[t % 2], 32 * (t // 2))
                    nc.vector.tensor_tensor(row_out[t % 2][:, :], bank[t % 6][0:TP, :], bias_row[:, 0, :],
                                            ALU.add).then_inc(proj_made, 1)
                low(2)

                def key(t):
                    dve.wait_ge(k_parts, t + 1)
                    nc.vector.scalar_tensor_tensor(kf[:, t, :], exp_t[t % 2][0:TP, :], 1.0, relu_t[t % 2][0:TP, :],
                                                   ALU.min, ALU.add).then_inc(k_made, 1)

                for t in range(NT):
                    dve.wait_ge(out_ready, NT + t + 1)
                    if t < 2:
                        dve.wait_ge(proj_stored[t % 2], 32 * 5)
                    else:
                        dve.wait_ge(k_parts, t - 1)
                    nc.vector.tensor_tensor(row_out[t % 2][:, :], bank[(NT + t) % 6][0:TP, :], bias_row[:, 1, :],
                                            ALU.add).then_inc(k_biased, 1)
                    if t:
                        key(t - 1)
                key(NT - 1)
                low(3)
                for t in range(NT):
                    dve.wait_ge(out_ready, 2 * NT + t + 1)
                    nc.vector.tensor_tensor(v_nodes[:, t, :], bank[(2 * NT + t) % 6][0:TP, :], bias_row[:, 2, :],
                                            ALU.add).then_inc(v_made, 1)
                low(4)
                for j, (c, s) in enumerate(QJ):
                    a, n = SLICES[s]
                    dve.wait_ge(q_parts, j + 1)
                    nc.vector.scalar_tensor_tensor(qf[:, c, a:a + n], exp_t[j % 2][:, 0:n], 1.0,
                                                   relu_t[j % 2][:, 0:n], ALU.min, ALU.add).then_inc(q_made, 1)
                dve.wait_ge(s2_zeroed, 1)
                dve.wait_ge(kv_ready, 1)
                kvp = bank[6][:, :].rearrange("p (c e) -> p c e", c=KC)
                k8 = ksum8[:, :, :].rearrange("p c h -> p (c h)")
                for h in range(2):
                    q = slice(64 * h, 64 * h + 64)
                    nc.vector.tensor_copy(kv_sb[q, :, q], kvp[q, :, q])
                    nc.vector.tensor_copy(k8[q, h:h + 31:10], bank[7][q, 0:KC]).then_inc(kv_made, 1)
                dve.wait_ge(den_ready, 1)
                nc.vector.reciprocal(rden[:, :], bank[0][0:TP, 0:NT * HEADS]).then_inc(rden_made, 1)
                for j, (c, s) in enumerate(QJ):
                    a, n = SLICES[s]
                    dve.wait_ge(rb_copied, j + 1)
                    if j >= 2:
                        dve.wait_ge(att_high, j - 1)
                    nc.vector.tensor_tensor(att_f[j % 2][:, 0:n], bank[4 + j % 2][:, 0:n], rb_sb[j % 2][:, 0:n],
                                            ALU.mult).then_inc(att_made, 1)
                    dve.wait_ge(att_high, j + 1)
                    nc.vector.tensor_tensor(xl[:, c, a:a + n], att_f[j % 2][:, 0:n], xh[:, c, a:a + n],
                                            ALU.subtract).then_inc(att_low, 1)
                dve.wait_ge(base_made, 1)
                for j, (c, s) in enumerate(QJ):
                    a, n = SLICES[s]
                    dve.wait_ge(mix_ready, j + 1)
                    nc.vector.scalar_tensor_tensor(base[:, c, a:a + n], bank[j % 4][:, 0:n], gshift[:, c:c + 1],
                                                   base[:, c, a:a + n], ALU.add, ALU.add).then_inc(mix_added, 1)

            @block.tensor
            def _(pe):
                def free(j):
                    j -= 6
                    if j < 0:
                        return
                    if j < NT:
                        pe.wait_ge(proj_made, j + 1)
                    elif j < 2 * NT:
                        pe.wait_ge(k_biased, j - NT + 1)
                    elif j < 3 * NT:
                        pe.wait_ge(v_made, j - 2 * NT + 1)
                    else:
                        pe.wait_ge(q_parts, j - 3 * NT + 1)

                for u in range(3):
                    pe.wait_ge(w_low, 2 * u + 2)
                    for t in range(NT):
                        free(u * NT + t)
                        s = slice(t * TP, (t + 1) * TP)
                        for k in range(KC):
                            last = product3(bank[(u * NT + t) % 6][0:TP, :], (xh[:, k, s], xl[:, k, s]),
                                            (w_hi[u % 2][:, k, :], w_lo[u % 2][:, k, :]), k == 0, k == KC - 1)
                        last.then_inc(out_ready, 1)
                pe.wait_ge(w_low, 8)
                for j, (c, s) in enumerate(QJ):
                    a, n = SLICES[s]
                    free(3 * NT + j)
                    cc = slice(c * 128, (c + 1) * 128)
                    for k in range(KC):
                        last = product3(bank[(3 * NT + j) % 6][:, 0:n], (w_hi[1][:, k, cc], w_lo[1][:, k, cc]),
                                        (xh[:, k, a:a + n], xl[:, k, a:a + n]), k == 0, k == KC - 1)
                    last.then_inc(out_ready, 1)
                pe.wait_ge(k_made, NT)
                pe.wait_ge(v_made, NT)
                for c in range(KC):
                    cc = slice(c * 128, (c + 1) * 128)
                    for t in range(NT):
                        nc.tensor.matmul(bank[6][:, cc], kf[:, t, cc], v_nodes[:, t, cc],
                                         start=(t == 0), stop=(t == NT - 1))
                        last = nc.tensor.matmul(bank[7][:, c:c + 1], kf[:, t, cc], ones[0:TP, 0:1],
                                                start=(t == 0), stop=(t == NT - 1))
                last.then_inc(kv_ready, 1)
                pe.wait_ge(kv_made, 2)
                pe.wait_ge(q_made, len(QJ))
                for t in range(NT):
                    for c in range(KC):
                        last = nc.tensor.matmul(bank[0][0:TP, t * HEADS:(t + 1) * HEADS],
                                                qf[:, c, t * TP:(t + 1) * TP], ksum8[:, c, :],
                                                start=(c == 0), stop=(c == KC - 1))
                last.then_inc(den_ready, 1)
                pe.wait_ge(rden_made, 1)
                for t in range(NT):
                    last = nc.tensor.transpose(bank[1 + t // 4][0:HEADS, (t % 4) * TP:(t % 4 + 1) * TP],
                                               rden[:, t * HEADS:(t + 1) * HEADS], ident[0:TP, 0:TP])
                    if t % 4 == 3 or t == NT - 1:
                        last.then_inc(rdent_ready, 1)
                pe.wait_ge(rdent_made, 3)
                for j, (c, s) in enumerate(QJ):
                    a, n = SLICES[s]
                    if j >= 2:
                        pe.wait_ge(att_made, j - 1)
                    nc.tensor.matmul(bank[4 + j % 2][:, 0:n], kv_sb[:, c, :], qf[:, c, a:a + n],
                                     start=True, stop=True)
                    nc.tensor.matmul(bank[6 + j % 2][:, 0:n], head_rows[:, c * 128:(c + 1) * 128],
                                     rden_t[:, a:a + n], start=True, stop=True).then_inc(att_ready, 1)
                pe.wait_ge(w_low, 10)
                pe.wait_ge(att_low, len(QJ))
                for j, (c, s) in enumerate(QJ):
                    a, n = SLICES[s]
                    if j >= 4:
                        pe.wait_ge(mix_added, j - 3)
                    cc = slice(c * 128, (c + 1) * 128)
                    for k in range(KC):
                        last = product3(bank[j % 4][:, 0:n], (w_hi[0][:, k, cc], w_lo[0][:, k, cc]),
                                        (xh[:, k, a:a + n], xl[:, k, a:a + n]), k == 0, k == KC - 1)
                    last.then_inc(mix_ready, 1)
        s2.close()
        split.close()

        s3 = ExitStack()
        wb_raw = sb("wb_raw", [ED, D], F32, s3)
        wb_hi = sb("wb_hi", [ED, D], F32R, s3)
        wb_lo = sb("wb_lo", [ED, D], F32R, s3)
        src_i = sb("src_i", [TP, NG * TG], I32, s3)
        iota_n = sb("iota_n", [TP, N], F32, s3)
        idx = [sb(f"idx{p}", [TP, TG], I32, s3) for p in range(2)]
        e_raw = [sb(f"e_raw{p}", [ED, EG], F32, s3) for p in range(2)]
        e_hi = [sb(f"e_hi{p}", [ED, EG], F32R, s3) for p in range(2)]
        e_lo = [sb(f"e_lo{p}", [ED, EG], F32R, s3) for p in range(2)]
        gath = [[sb(f"gath{p}{t}", [TP, D], F32, s3) for t in range(TG)] for p in range(2)]
        pre_sum = [sb(f"pre_sum{t}", [TP, D], F32, s3) for t in range(TG)]
        m_hi = [[sb(f"m_hi{p}{t}", [TP, D], F32R if t in TWO_PASS else F32, s3) for t in range(TG)] for p in range(2)]
        m_lo = [{t: sb(f"m_lo{p}{t}", [TP, D], F32R, s3) for t in TWO_PASS} for p in range(2)]
        hot = [sb(f"hot{p}", [TP, TG, TP + 1], F32R, s3) for p in range(2)]
        hot_x = sb("hot_x", [TP, TG, TP + 1], F32R, s3)
        ones2 = sb("ones2", [TP, 2], F32R, s3)
        NW = len(TWO_PASS)

        wb_loaded, src_loaded, wb_high, wb_low, iota_made = (sem(n) for n in (
            "wb_loaded", "src_loaded", "wb_high", "wb_low", "iota_made"))
        e_loaded = [sem(f"e_loaded{p}") for p in range(2)]
        gathered = [[sem(f"gathered{p}{t}") for t in range(TG)] for p in range(2)]
        e_high, e_low, idx_ready, pre_ready, added, relued, lowered, hot_made, summed, taken = (sem(n) for n in (
            "e_high", "e_low", "idx_ready", "pre_ready", "added", "relued", "lowered", "hot_made", "summed", "taken"))
        hot_x_made, summed_x, taken_x = sem("hot_x_made"), sem("summed_x"), sem("taken_x")
        PRE, SUM, DEG = bank[0:4], bank[4:6], bank[6:8]

        def in_pairs(eng, first, last, step):
            pairs = (last - first) // 2
            with eng.Fori(0, pairs) as j:
                for p in range(2):
                    step(j * 2 + (first + p), p)
            for g in range(first + 2 * pairs, last):
                step(g, g % 2)

        def a_window(value):
            return nc.s_assert_within(value, 0, NT - 1, skip_runtime_bounds_check_because="made on the chip from counts of exceeded window bounds")

        def word_at(g):
            return word[0:1, g:g + 1] if isinstance(g, int) else word[0:1, bass.ds(g, 1)]

        def if_further(eng, g, w, body):
            def span(a):
                return further[0:1, bass.ds(g * 4 + a, 1)] if not isinstance(g, int) else further[0:1, 4 * g + a:4 * g + a + 1]

            with eng.If((w & 255) >= 16):
                x0 = eng.value_load(span(0), min_val=0, max_val=NG * (NT - 1))
                x1 = eng.value_load(span(1), min_val=0, max_val=NG * (NT - 1))
                off = eng.value_load(span(2), min_val=0, max_val=2 * NG * NT)
                with eng.Fori(x0, x1) as x:
                    body(x, off)

        with nc.Block() as block:
            @block.sync
            def _(sp):
                sp.dma_start(wb_raw[:, :], w1b).then_inc(wb_loaded, 16)

                def step(g, p):
                    if not isinstance(g, int) or g >= 2:
                        sp.wait_ge(e_low, g - 1)
                    sp.dma_start(e_raw[p][:, :], edge_blocks[g] if isinstance(g, int) else
                                 edge_blocks[bass.ds(g, 1)].rearrange("a p e -> p (a e)")).then_inc(e_loaded[p], 16)

                step(0, 0)
                step(1, 1)
                in_pairs(sp, 2, NG, step)

            @block.gpsimd
            def _(pool):
                pool.dma_start(src_i[:, :], src_cols).then_inc(src_loaded, 16)
                nc.gpsimd.iota(iota_n[:, :], pattern=[[1, N]], base=0, channel_multiplier=0,
                               allow_small_or_imprecise_dtypes=True).then_inc(iota_made, 1)
                pool.wait_ge(src_loaded, 16)

                def step(g, p):
                    if not isinstance(g, int) or g >= 2:
                        pool.wait_ge(added, g * TG - TG)
                    cols_g = src_i[:, g * TG:(g + 1) * TG] if isinstance(g, int) else src_i[:, bass.ds(g * TG, TG)]
                    nc.gpsimd.tensor_copy(idx[p][:, :], cols_g).then_inc(idx_ready, 1)
                    pool.wait_ge(idx_ready, g * 2 + 1)
                    nc.gpsimd.tensor_tensor(pool_step[:, p:p + 1], epsc[0:1, :], epsc[0:1, :],
                                            ALU.add).then_inc(idx_ready, 1)
                    for t in range(TG):
                        pool.indirect_dma_start(
                            out=gath[p][t][:, :], out_offset=None, in_=proj,
                            in_offset=bass.IndirectOffsetOnAxis(ap=idx[p][:, t:t + 1], axis=0)
                        ).then_inc(gathered[p][t], 16)

                step(0, 0)
                step(1, 1)
                in_pairs(pool, 2, NG, step)

            @block.scalar
            def _(act):
                act.wait_ge(wb_loaded, 16)
                nc.scalar.copy(wb_hi[:, :], wb_raw[:, :]).then_inc(wb_high, 1)

                def edge_high(g, p):
                    act.wait_ge(e_loaded[p], (g - p) * 8 + 16)
                    if not isinstance(g, int) or g >= 2:
                        act.wait_ge(pre_ready, g * TG - TG)
                    nc.scalar.copy(e_hi[p][:, :], e_raw[p][:, :]).then_inc(e_high, 1)

                def relu(g, p):
                    for t in range(TG):
                        act.wait_ge(added, g * TG + (t + 1))
                        nc.scalar.activation(m_hi[p][t][:, :], pre_sum[t][:, :], ACT.Relu).then_inc(relued, 1)

                edge_high(0, 0)
                edge_high(1, 1)
                relu(0, 0)
                edge_high(2, 0)

                def step(g, p):
                    relu(g, p)
                    edge_high(g + 2, p)

                with act.Fori(0, (NG - 4) // 2) as j:
                    step(j * 2 + 1, 1)
                    step(j * 2 + 2, 0)
                step(NG - 3, 1)
                relu(NG - 2, 0)
                relu(NG - 1, 1)

            @block.vector
            def _(dve):
                nc.vector.memset(nodes[:, :, :], 0.0).then_inc(taken, 1)
                nc.vector.memset(deg[:, :, :], 0.0).then_inc(taken_x, 1)
                nc.vector.tensor_copy(ones2[:, :], ones[0:TP, 0:2])
                dve.wait_ge(wb_high, 1)
                nc.vector.tensor_tensor(wb_lo[:, :], wb_raw[:, :], wb_hi[:, :], ALU.subtract).then_inc(wb_low, 1)
                dve.wait_ge(iota_made, 1)

                def edge_low(g, p):
                    dve.wait_ge(e_high, g + 1)
                    nc.vector.tensor_tensor(e_lo[p][:, :], e_raw[p][:, :], e_hi[p][:, :], ALU.subtract).then_inc(e_low, 1)

                def one_hot(dst_hot, g, of, first_node, signal):
                    for t in range(TG):
                        d = (of[:, g * TG + t:g * TG + t + 1] if isinstance(g, int)
                             else of[:, bass.ds(g * TG + t, 1)])
                        last = nc.vector.tensor_scalar(dst_hot[:, t, 0:TP], first_node, d, None, ALU.is_equal)
                    last.then_inc(signal, 1)

                def add(g, p, t):
                    dve.wait_ge(pre_ready, g * TG + (t + 1))
                    dve.wait_ge(gathered[p][t], (g - p) * 8 + 16)
                    if not isinstance(g, int) or g >= 1:
                        dve.wait_ge(relued, g * TG + (t + 1 - TG))
                        if t in TWO_PASS:
                            dve.wait_ge(lowered, g * NW + (TWO_PASS.index(t) + 1 - NW))
                    nc.vector.tensor_tensor(pre_sum[t][:, :], PRE[t][0:TP, :], gath[p][t][:, :],
                                            ALU.add).then_inc(added, 1)

                def low_part(g, p, t):
                    if t in TWO_PASS:
                        dve.wait_ge(relued, g * TG + (t + 1))
                        nc.vector.scalar_tensor_tensor(m_lo[p][t][:, :], pre_sum[t][:, :], 0.0, m_hi[p][t][:, :],
                                                       ALU.max, ALU.subtract).then_inc(lowered, 1)

                def add_group(g, p):
                    add(g, p, 0)
                    for t in range(1, TG):
                        add(g, p, t)
                        low_part(g, p, t - 1)
                    low_part(g, p, TG - 1)
                    one_hot(hot[p], g, dst_rel, iota_n[:, 0:TP], hot_made)

                def accumulate(win_of, sums, degs, signal):
                    rows_w = nodes[:, :, :].rearrange("p t f -> p (t f)")[:, bass.ds(win_of * D, D)]
                    deg_w = deg[:, :, :].rearrange("p t a -> p (t a)")[:, bass.ds(win_of * 2, 2)]
                    nc.vector.tensor_tensor(rows_w, sums[0:TP, :], rows_w, ALU.add)
                    nc.vector.tensor_tensor(deg_w, degs, deg_w, ALU.add).then_inc(signal, 1)

                def take(g, p):
                    w = dve.value_load(word_at(g), min_val=0, max_val=SCALE_X0 * NG * NT)
                    dve.wait_ge(summed, g + 1)
                    dve.wait_ge(taken, g + 1)
                    dve.wait_ge(taken_x, 1)
                    accumulate(a_window(w & 15), SUM[p], DEG[p][0:TP, 0:2], taken)

                    def body(x, off):
                        window = a_window(x + off - (NG * NT - 1))
                        one_hot(hot_x, g, dst_f, iota_n[:, bass.ds(window * TP, TP)], hot_x_made)
                        dve.wait_ge(summed_x, x + 1)
                        dve.wait_ge(taken, g + 2)
                        accumulate(window, SUM[p], DEG[p][0:TP, 0:2], taken_x)
                        dve.wait_ge(taken_x, x + 2)

                    if_further(dve, g, w, body)

                edge_low(0, 0)
                edge_low(1, 1)
                add_group(0, 0)
                edge_low(2, 0)

                def step(g, p):
                    add_group(g, p)
                    edge_low(g + 2, p)
                    take(g - 1, 1 - p)

                with dve.Fori(0, (NG - 4) // 2) as j:
                    step(j * 2 + 1, 1)
                    step(j * 2 + 2, 0)
                step(NG - 3, 1)
                add_group(NG - 2, 0)
                take(NG - 3, 1)
                add_group(NG - 1, 1)
                take(NG - 2, 0)
                take(NG - 1, 1)

            @block.tensor
            def _(pe):
                pe.wait_ge(wb_low, 1)

                def pre(g, p):
                    pe.wait_ge(e_low, g + 1)
                    for t in range(TG):
                        if not isinstance(g, int) or g >= 1:
                            pe.wait_ge(added, g * TG + (t + 1 - TG))
                        c = slice(t * TP, (t + 1) * TP)
                        product3(PRE[t][0:TP, :], (e_hi[p][:, c], e_lo[p][:, c]), (wb_hi[:, :], wb_lo[:, :]),
                                 True, True).then_inc(pre_ready, 1)

                def window_sum(h, p, sums, degs, signal):
                    for t in range(TG):
                        if t in TWO_PASS:
                            nc.tensor.matmul(sums[0:TP, :], h[:, t, 0:TP], m_hi[p][t][:, :],
                                             start=(t == 0), stop=False)
                            nc.tensor.matmul(sums[0:TP, :], h[:, t, 0:TP], m_lo[p][t][:, :],
                                             start=False, stop=(t == TG - 1))
                        else:
                            nc.tensor.matmul(sums[0:TP, :], h[:, t, 0:TP].bitcast(F32), m_hi[p][t][:, :],
                                             start=(t == 0), stop=(t == TG - 1))
                    for t in range(TG):
                        last = nc.tensor.matmul(degs, h[:, t, 0:TP], ones2[:, :], start=(t == 0), stop=(t == TG - 1))
                    last.then_inc(signal, 1)

                def group_sum(g, p):
                    w = pe.value_load(word_at(g), min_val=0, max_val=SCALE_X0 * NG * NT)
                    pe.wait_ge(hot_made, g + 1)
                    pe.wait_ge(relued, g * TG + TG)
                    if NW:
                        pe.wait_ge(lowered, g * NW + NW)
                    if not isinstance(g, int) or g >= 2:
                        pe.wait_ge(taken, g)
                    window_sum(hot[p], p, SUM[p], DEG[p][0:TP, 0:2], summed)

                    def body(x, off):
                        pe.wait_ge(hot_x_made, x + 1)
                        pe.wait_ge(taken, g + 2)
                        pe.wait_ge(taken_x, x + 1)
                        window_sum(hot_x, p, SUM[p], DEG[p][0:TP, 0:2], summed_x)

                    if_further(pe, g, w, body)

                pre(0, 0)
                for g in range(2):
                    pre(g + 1, 1 - g)
                    group_sum(g, g)
                with pe.Fori(0, (NG - 4) // 2) as j:
                    for p in range(2):
                        pre(j * 2 + (p + 3), 1 - p)
                        group_sum(j * 2 + (p + 2), p)
                pre(NG - 1, 1)
                group_sum(NG - 2, 0)
                group_sum(NG - 1, 1)
        s3.close()

        s4 = ExitStack()
        tr_hi = sb("tr_hi", [128, KC, N], F32R, s4)
        tr_lo = sb("tr_lo", [128, KC, N], F32R, s4)
        ag_hi = sb("ag_hi", [128, KC, N], F32R, s4)
        ag_lo = sb("ag_lo", [128, KC, N], F32R, s4)
        s4a = ExitStack()
        w2_raw = sb("w2_raw", [128, KC, D], F32, s4a)
        w2_hi = sb("w2_hi", [128, KC, D], F32R, s4a)
        w2_lo = sb("w2_lo", [128, KC, D], F32R, s4a)
        b2_row = sb("b2_row", [1, D], F32, s4a)
        deg_row = sb("deg_row", [1, N], F32, s4a)
        w2_loaded, b2_loaded, w2_high, w2_low, sums_turned, sums_high, sums_low, deg_turned, deg_taken = (
            sem(n) for n in ("w2_loaded", "b2_loaded", "w2_high", "w2_low", "sums_turned", "sums_high", "sums_low",
                             "deg_turned", "deg_taken"))
        agg_ready, agg_high, agg_low = sem("agg_ready"), sem("agg_high"), sem("agg_low")

        with nc.Block() as block:
            @block.sync
            def _(sp):
                sp.dma_start(w2_raw[:, :, :], w2.rearrange("(k p) f -> p k f", p=128)).then_inc(w2_loaded, 16)
                sp.dma_start(b2_row[:, :], b2.unsqueeze(0)).then_inc(b2_loaded, 16)

            def bank_nodes(t):
                return bank[t % 4][:, 0:KC * TP].rearrange("p (k n) -> p k n", k=KC)

            @block.scalar
            def _(act):
                for t in range(NT):
                    act.wait_ge(sums_turned, t + 1)
                    nc.scalar.copy(tr_hi[:, :, t * TP:(t + 1) * TP], bank_nodes(t)).then_inc(sums_high, 1)
                    if t == 1:
                        act.wait_ge(w2_loaded, 16)
                        nc.scalar.copy(w2_hi[:, :, :], w2_raw[:, :, :]).then_inc(w2_high, 1)
                for j, (c, s) in enumerate(QJ):
                    a, n = SLICES[s]
                    act.wait_ge(agg_ready, j + 1)
                    nc.scalar.copy(ag_hi[:, c, a:a + n], bank[j % 4][:, 0:n]).then_inc(agg_high, 1)

            @block.vector
            def _(dve):
                for t in range(NT):
                    dve.wait_ge(sums_high, t + 1)
                    s = slice(t * TP, (t + 1) * TP)
                    nc.vector.tensor_tensor(tr_lo[:, :, s], bank_nodes(t), tr_hi[:, :, s],
                                            ALU.subtract).then_inc(sums_low, 1)
                    if t == 2:
                        dve.wait_ge(w2_high, 1)
                        nc.vector.tensor_tensor(w2_lo[:, :, :], w2_raw[:, :, :], w2_hi[:, :, :],
                                                ALU.subtract).then_inc(w2_low, 1)
                for i in range(3):
                    dve.wait_ge(deg_turned, i + 1)
                    n = min(4, NT - 4 * i) * TP
                    nc.vector.tensor_copy(deg_row[:, 4 * i * TP:4 * i * TP + n],
                                          bank[4 + i][0:1, 0:n]).then_inc(deg_taken, 1)
                for j, (c, s) in enumerate(QJ):
                    a, n = SLICES[s]
                    dve.wait_ge(agg_high, j + 1)
                    nc.vector.tensor_tensor(ag_lo[:, c, a:a + n], bank[j % 4][:, 0:n], ag_hi[:, c, a:a + n],
                                            ALU.subtract).then_inc(agg_low, 1)

            @block.tensor
            def _(pe):
                for t in range(NT):
                    if t >= 4:
                        pe.wait_ge(sums_low, t - 3)
                    for k in range(KC):
                        last = nc.tensor.transpose(bank[t % 4][:, k * TP:(k + 1) * TP],
                                                   nodes[:, t, k * 128:(k + 1) * 128], ident[0:TP, 0:TP])
                    last.then_inc(sums_turned, 1)
                for t in range(NT):
                    last = nc.tensor.transpose(bank[4 + t // 4][0:1, (t % 4) * TP:(t % 4 + 1) * TP],
                                               deg[:, t, 0:1], ident[0:TP, 0:TP])
                    if t % 4 == 3 or t == NT - 1:
                        last.then_inc(deg_turned, 1)
                pe.wait_ge(w2_low, 1)
                pe.wait_ge(sums_low, NT)
                pe.wait_ge(deg_taken, 3)
                pe.wait_ge(b2_loaded, 16)
                for j, (c, s) in enumerate(QJ):
                    a, n = SLICES[s]
                    if j >= 4:
                        pe.wait_ge(agg_low, j - 3)
                    cc = slice(c * 128, (c + 1) * 128)
                    nc.tensor.matmul(bank[j % 4][:, 0:n], b2_row[0:1, cc], deg_row[0:1, a:a + n],
                                     start=True, stop=False)
                    for k in range(KC):
                        last = product3(bank[j % 4][:, 0:n], (w2_hi[:, k, cc], w2_lo[:, k, cc]),
                                        (tr_hi[:, k, a:a + n], tr_lo[:, k, a:a + n]), False, k == KC - 1)
                    last.then_inc(agg_ready, 1)
        s4a.close()

        s4b = ExitStack()
        RING = 4
        g_raw = [sb(f"g_raw{i}", [128, KC, 128], F32, s4b) for i in range(RING)]
        g_hi = [sb(f"g_hi{i}", [128, KC, 128], F32R, s4b) for i in range(RING)]
        g_lo = [sb(f"g_lo{i}", [128, KC, 128], F32R, s4b) for i in range(RING)]
        gate_r = [sb(f"gate_r{i}", [128, N], F32, s4b) for i in range(2)]
        gate_z = [sb(f"gate_z{i}", [128, N], F32, s4b) for i in range(2)]
        wide = SLICES[0][1]
        cand = [sb(f"cand{i}", [128, wide], F32, s4b) for i in range(2)]
        new = [sb(f"new{i}", [128, wide], F32, s4b) for i in range(2)]
        mixd = [sb(f"mixd{i}", [128, wide], F32, s4b) for i in range(2)]
        NP = 6 * KC
        g_loaded = [sem(f"g_loaded{i}") for i in range(RING)]
        g_high, g_low, gate_done, gate_ready, gate_taken, xn_high, xn_low, cand_made, new_made, x1_made = (
            sem(n) for n in ("g_high", "g_low", "gate_done", "gate_ready", "gate_taken", "xn_high", "xn_low",
                             "cand_made", "new_made", "x1_made"))

        with nc.Block() as block:
            @block.sync
            def _(sp):
                for q in range(NP):
                    if q >= RING:
                        sp.wait_ge(g_low, q - RING + 1)
                    sp.dma_start(g_raw[q % RING][:, :, :], gate_blocks[q]).then_inc(g_loaded[q % RING], 16)

            @block.scalar
            def _(act):
                def high(*qs):
                    for q in qs:
                        if q >= NP:
                            return
                        act.wait_ge(g_loaded[q % RING], 16 * (q // RING + 1))
                        if q >= RING:
                            act.wait_ge(gate_done, (q - RING) // 2 + 1)
                        nc.scalar.copy(g_hi[q % RING][:, :, :], g_raw[q % RING][:, :, :]).then_inc(g_high, 1)

                high(0, 1)
                for c in range(KC):
                    nc.scalar.copy(tr_hi[:, c, :], xn[:, c, :]).then_inc(xn_high, 1)
                high(2, 3)
                for c in range(KC):
                    for gate, dst in ((0, gate_r[c % 2]), (1, gate_z[c % 2])):
                        for s, (a, n) in enumerate(SLICES):
                            job = 12 * c + 3 * gate + s
                            act.wait_ge(gate_ready, job + 1)
                            if c >= 2:
                                act.wait_ge(x1_made, 3 * (c - 1))
                            nc.scalar.activation(dst[:, a:a + n], bank[job % 8][:, 0:n], ACT.Sigmoid,
                                                 bias=brz[:, gate, c:c + 1]).then_inc(gate_taken, 1)
                        high(6 * c + 4 + 2 * gate, 6 * c + 5 + 2 * gate)
                    for s, (a, n) in enumerate(SLICES):
                        i = 3 * c + s
                        act.wait_ge(cand_made, i + 1)
                        if i >= 2:
                            act.wait_ge(x1_made, i - 1)
                        nc.scalar.activation(new[i % 2][:, 0:n], cand[i % 2][:, 0:n], ACT.Tanh).then_inc(new_made, 1)
                    high(6 * c + 8, 6 * c + 9)

            @block.vector
            def _(dve):
                L = dve_chain.link

                def low(*qs):
                    for q in qs:
                        if q < NP:
                            dve.wait_ge(g_high, q + 1)
                            nc.vector.tensor_tensor(g_lo[q % RING][:, :, :], g_raw[q % RING][:, :, :],
                                                    g_hi[q % RING][:, :, :], ALU.subtract).then_inc(g_low, 1)

                def candidate(c, s):
                    a, n = SLICES[s]
                    i, job = 3 * c + s, 12 * c + 6 + 2 * s
                    dve.wait_ge(gate_ready, job + 2)
                    dve.wait_ge(gate_taken, 6 * c + 6)
                    L(dve, nc.vector.scalar_tensor_tensor(
                        cand[i % 2][:, 0:n], bank[(job + 1) % 8][:, 0:n], COL["bhn"][:, c:c + 1],
                        gate_r[c % 2][:, a:a + n], ALU.add, ALU.mult))
                    nc.vector.scalar_tensor_tensor(
                        cand[i % 2][:, 0:n], bank[job % 8][:, 0:n], COL["bin"][:, c:c + 1],
                        cand[i % 2][:, 0:n], ALU.add, ALU.add).then_inc(cand_made, 1)

                def combine(c, s):
                    a, n = SLICES[s]
                    i = 3 * c + s
                    dve.wait_ge(new_made, i + 1)
                    m, nw = mixd[i % 2][:, 0:n], new[i % 2][:, 0:n]
                    L(dve, nc.vector.tensor_tensor(m, xn[:, c, a:a + n], nw, ALU.subtract))
                    L(dve, nc.vector.tensor_tensor(m, m, gate_z[c % 2][:, a:a + n], ALU.mult))
                    L(dve, nc.vector.tensor_tensor(m, m, nw, ALU.add))
                    nc.vector.scalar_tensor_tensor(base[:, c, a:a + n], m, gscale[:, c:c + 1], base[:, c, a:a + n],
                                                   ALU.mult, ALU.add).then_inc(x1_made, 1)

                low(0, 1)
                for c in range(KC):
                    dve.wait_ge(xn_high, c + 1)
                    nc.vector.tensor_tensor(tr_lo[:, c, :], xn[:, c, :], tr_hi[:, c, :], ALU.subtract).then_inc(xn_low, 1)
                low(2, 3)
                for c in range(KC):
                    low(6 * c + 4, 6 * c + 5)
                    low(6 * c + 6, 6 * c + 7)
                    candidate(c, 0)
                    candidate(c, 1)
                    combine(c, 0)
                    candidate(c, 2)
                    combine(c, 1)
                    combine(c, 2)
                    low(6 * c + 8, 6 * c + 9)

            @block.tensor
            def _(pe):
                def free(job):
                    job -= 8
                    if job >= 0:
                        c, i = divmod(job, 12)
                        if i < 6:
                            pe.wait_ge(gate_taken, 6 * c + i + 1)
                        else:
                            pe.wait_ge(cand_made, 3 * c + (i - 6) // 2 + 1)

                def operand(q, k):
                    return g_hi[q % RING][:, k, :], g_lo[q % RING][:, k, :]

                for c in range(KC):
                    for gate in range(2):
                        q = 6 * c + 2 * gate
                        pe.wait_ge(g_low, q + 2)
                        for s, (a, n) in enumerate(SLICES):
                            job = 12 * c + 3 * gate + s
                            free(job)
                            for k in range(KC):
                                product3(bank[job % 8][:, 0:n], operand(q, k),
                                         (ag_hi[:, k, a:a + n], ag_lo[:, k, a:a + n]), k == 0, False)
                            if job == 0:
                                pe.wait_ge(xn_low, KC)
                            for k in range(KC):
                                last = product3(bank[job % 8][:, 0:n], operand(q + 1, k),
                                                (tr_hi[:, k, a:a + n], tr_lo[:, k, a:a + n]), False, k == KC - 1)
                            last.then_inc(gate_ready, 1)
                            if s == len(SLICES) - 1:
                                pe.nop().then_inc(gate_done, 1)
                    q = 6 * c + 4
                    pe.wait_ge(g_low, q + 2)
                    for s, (a, n) in enumerate(SLICES):
                        for part, (hi, lo) in enumerate(((ag_hi, ag_lo), (tr_hi, tr_lo))):
                            job = 12 * c + 6 + 2 * s + part
                            free(job)
                            for k in range(KC):
                                last = product3(bank[job % 8][:, 0:n], operand(q + part, k),
                                                (hi[:, k, a:a + n], lo[:, k, a:a + n]), k == 0, k == KC - 1)
                            last.then_inc(gate_ready, 1)
                    pe.nop().then_inc(gate_done, 1)
        s4b.close()
        s4.close()

        s5 = ExitStack()
        wg_sb = sb("wg_sb", [128, KC, NX], F32, s5)
        bg_sb = sb("bg_sb", [TP, NX], F32, s5)
        y = sb("y", [TP, NT, D], F32, s5)
        before = sb("before", [128, 128], F32, s5)
        csum = sb("csum", [TP, NX], F32, s5)
        R3 = lambda n: sb(n, [TP, NT, NX], F32, s5)
        logit, prob, is_max, hot_e, place = R3("logit"), R3("prob"), R3("is_max"), R3("hot_e"), R3("place")
        e_less = sb("e_less", [TP, NX], F32, s5)
        best = sb("best", [TP, NT], F32, s5)
        score = sb("score", [TP, NT], F32, s5)
        slot_f = sb("slot_f", [TP, NT], F32, s5)
        slot = sb("slot", [TP, NT], I32, s5)
        held = sb("held", [TP, NX], F32, s5)
        count = sb("count", [TP, NX], F32, s5)
        tiles = sb("tiles", [TP, NX], F32, s5)
        cum = sb("cum", [TP, NX], F32, s5)
        tile_no = sb("tile_no", [1, NST], F32, s5)
        tile_ef = sb("tile_ef", [1, NST], F32, s5)
        tile_e = sb("tile_e", [1, NST], I32, s5)
        FR = 3
        w1e = [sb(f"w1e{i}", [128, KC, HX], F32, s5) for i in range(FR)]
        w2e = [sb(f"w2e{i}", [128, HX // 128, D], F32, s5) for i in range(FR)]
        b1e = [sb(f"b1e{i}", [128, HX // 128], F32, s5) for i in range(FR)]
        b2e = [sb(f"b2e{i}", [128, D], F32, s5) for i in range(FR)]
        yin = [sb(f"yin{i}", [128, D], F32, s5) for i in range(FR)]
        yt = [sb(f"yt{i}", [128, KC, TS], F32, s5) for i in range(2)]
        hid = [sb(f"hid{i}", [128, HX // 128, TS], F32, s5) for i in range(2)]
        fo = [sb(f"fo{i}", [128, D], F32, s5) for i in range(2)]
        fg = sb("fg", [TP, NT, D], F32, s5)
        wg_loaded, x1_turned, x1_taken, logits_ready, consts5, stats5, std5 = (sem(n) for n in (
            "wg_loaded", "x1_turned", "x1_taken", "logits_ready", "consts5", "stats5", "std5"))
        shifted, exp_made, held_made, counts_ready, y_made, slots_made, scattered = (sem(n) for n in (
            "shifted", "exp_made", "held_made", "counts_ready", "y_made", "slots_made", "scattered"))
        ew_loaded = [sem(f"ew_loaded{i}") for i in range(FR)]
        ew_loaded2 = [sem(f"yin_loaded{i}") for i in range(FR)]
        y_turned, yt_made, hid_ready, hid_made, f_ready, f_made = (sem(n) for n in (
            "y_turned", "yt_made", "hid_ready", "hid_made", "f_ready", "f_made"))
        f_stored = [sem(f"f_stored{i}") for i in range(2)]
        f_back = [sem(f"f_back{t}") for t in range(NT)]
        out_made, out_stored = sem("out_made"), sem("out_stored")

        with nc.Block() as block:
            @block.sync
            def _(sp):
                sp.dma_start(wg_sb[:, :, :], wg.rearrange("(k p) e -> p k e", p=128)).then_inc(wg_loaded, 16)
                sp.dma_start(bg_sb[:, :], bg.unsqueeze(0).to_broadcast([TP, NX])).then_inc(wg_loaded, 16)
                sp.wait_ge(slots_made, 1)
                for i in range(NST):
                    r = i % FR
                    e = sp.value_load(tile_e[0:1, i:i + 1], min_val=0, max_val=NX - 1)
                    if i >= FR:
                        sp.wait_ge(f_made, i - FR + 1)
                    sp.dma_start(w1e[r][:, :, :], we1[bass.ds(e, 1)].rearrange("a (k p) h -> p (a k) h", p=128)
                                 ).then_inc(ew_loaded[r], 16)
                    sp.dma_start(w2e[r][:, :, :], we2[bass.ds(e, 1)].rearrange("a (k p) h -> p (a k) h", p=128)
                                 ).then_inc(ew_loaded[r], 16)
                    sp.dma_start(b1e[r][:, :], be1[bass.ds(e, 1)].rearrange("a p k -> p (a k)")
                                 ).then_inc(ew_loaded[r], 16)
                    sp.dma_start(b2e[r][:, :], be2[bass.ds(e, 1)].to_broadcast([128, D])).then_inc(ew_loaded[r], 16)
                    if i == 0:
                        sp.wait_ge(scattered, 16 * NT)
                    sp.dma_start(yin[r][:, :], slot_in[i * TS:(i + 1) * TS, :]).then_inc(ew_loaded2[r], 16)
                for t in range(NT):
                    sp.wait_ge(out_made, t + 1)
                    rows_dma(sp, out[t * TP:(t + 1) * TP, :], fg[:, t, :], out_stored)
                sp.wait_ge(out_stored, 32 * NT)

            @block.gpsimd
            def _(pool):
                nc.gpsimd.iota(e_less[:, :], pattern=[[1, NX]], base=-NX, channel_multiplier=0,
                               allow_small_or_imprecise_dtypes=True)
                nc.gpsimd.iota(tile_no[:, :], pattern=[[1, NST]], base=0, channel_multiplier=0,
                               allow_small_or_imprecise_dtypes=True)
                nc.gpsimd.affine_select(out=before[:, :], in_=ones[:, :], compare_op=ALU.is_gt, fill=0.0,
                                        base=0, pattern=[[1, 128]], channel_multiplier=-1).then_inc(consts5, 1)
                pool.wait_ge(y_made, NT)
                pool.wait_ge(slots_made, 1)
                pool.wait_ge(table_zeroed, 16 * NST)
                for t in range(NT):
                    pool.indirect_dma_start(out=slot_in, out_offset=bass.IndirectOffsetOnAxis(ap=slot[:, t:t + 1], axis=0),
                                            in_=y[:, t, :], in_offset=None).then_inc(scattered, 16)
                pool.wait_ge(f_stored[0], 16 * ((NST + 1) // 2))
                pool.wait_ge(f_stored[1], 16 * (NST // 2))
                for t in range(NT):
                    pool.indirect_dma_start(out=fg[:, t, :], out_offset=None, in_=slot_out,
                                            in_offset=bass.IndirectOffsetOnAxis(ap=slot[:, t:t + 1], axis=0)
                                            ).then_inc(f_back[t], 16)

            @block.scalar
            def _(act):
                for t in range(NT):
                    act.wait_ge(x1_turned, t + 1)
                    nc.scalar.copy(nodes[:, t, :], bank[t % 3][0:TP, :]).then_inc(x1_taken, 1)
                act.wait_ge(stats5, 1)
                nc.scalar.activation(rstd[:, :], mv[:, :, 1], ACT.Sqrt, bias=epsc[0:TP, :]).then_inc(std5, 1)
                act.wait_ge(shifted, 1)
                nc.scalar.activation(prob[:, :, :], logit[:, :, :], ACT.Exp).then_inc(exp_made, 1)
                for i in range(NST):
                    act.wait_ge(y_turned, i + 1)
                    nc.scalar.copy(yt[i % 2][:, :, :].rearrange("p k n -> p (k n)"), bank[i % 2][:, :]).then_inc(yt_made, 1)
                    act.wait_ge(hid_ready, i + 1)
                    if i >= 2:
                        act.wait_ge(f_ready, i - 1)
                    for m in range(HX // 128):
                        last = nc.scalar.activation(hid[i % 2][:, m, :], bank[2 + i % 2][:, m * TS:(m + 1) * TS],
                                                    ACT.Relu, bias=b1e[i % FR][:, m:m + 1])
                    last.then_inc(hid_made, 1)
                    act.wait_ge(f_made, i + 1)
                    act.dma_start(slot_out[i * TS:(i + 1) * TS, :], fo[i % 2][:, :]).then_inc(f_stored[i % 2], 16)

            @block.vector
            def _(dve):
                L = dve_chain.link
                for t in range(NT):
                    dve.wait_ge(x1_taken, t + 1)
                    L(dve, nc.vector.bn_stats(stat[:, t, :], nodes[:, t, :]))
                    last = nc.vector.bn_aggr(mv[:, t, :], stat[:, t, :])
                last.then_inc(stats5, 1)
                dve.wait_ge(stats5, 1)
                L(dve, nc.vector.tensor_scalar(tmp_t[:, :], mv[:, :, 1], EPS, None, ALU.add))
                dve.wait_ge(logits_ready, 1)
                nc.vector.tensor_copy(csum[:, :], bank[5][0:TP, 0:NX])
                L(dve, nc.vector.tensor_copy(logit[:, :, :].rearrange("p t e -> p (t e)"), bank[4][0:TP, 0:NT * NX]))
                dve.wait_ge(std5, 1)
                newton_rsqrt(dve, rstd[:, :], tmp_t[:, :], tmp_s[:, :], stat[:, :, 0])

                def over_e(ap):
                    return ap.unsqueeze(2).to_broadcast([TP, NT, NX])

                def over_t(ap):
                    return ap.unsqueeze(1).to_broadcast([TP, NT, NX])

                TT = nc.vector.tensor_tensor
                L(dve, TT(place[:, :, :], over_e(mv[:, :, 0]), over_t(csum[:, :]), ALU.mult))
                L(dve, TT(logit[:, :, :], logit[:, :, :], place[:, :, :], ALU.subtract))
                L(dve, TT(logit[:, :, :], logit[:, :, :], over_e(rstd[:, :]), ALU.mult))
                dve.wait_ge(wg_loaded, 32)
                L(dve, TT(logit[:, :, :], logit[:, :, :], over_t(bg_sb[:, :]), ALU.add))
                L(dve, nc.vector.tensor_reduce(best[:, :], logit[:, :, :], AX_X, ALU.max))
                TT(logit[:, :, :], logit[:, :, :], over_e(best[:, :]), ALU.subtract).then_inc(shifted, 1)
                dve.wait_ge(shifted, 1)
                dve.wait_ge(consts5, 1)
                L(dve, nc.vector.tensor_scalar(is_max[:, :, :], logit[:, :, :], 0.0, None, ALU.is_equal))
                L(dve, TT(is_max[:, :, :], is_max[:, :, :], over_t(e_less[:, :]), ALU.mult))
                L(dve, nc.vector.tensor_reduce(best[:, :], is_max[:, :, :], AX_X, ALU.min))
                L(dve, TT(hot_e[:, :, :], over_t(e_less[:, :]), over_e(best[:, :]), ALU.is_equal))
                nc.vector.tensor_reduce(held[:, :], hot_e[:, :, :].rearrange("p t e -> p e t"), AX_X,
                                        ALU.add).then_inc(held_made, 1)
                dve.wait_ge(exp_made, 1)
                L(dve, nc.vector.tensor_reduce(score[:, :], prob[:, :, :], AX_X, ALU.add))
                L(dve, nc.vector.reciprocal(score[:, :], score[:, :]))
                dve.wait_ge(counts_ready, 1)
                nc.vector.tensor_copy(place[:, 0, :], bank[6][0:TP, NX:2 * NX])
                L(dve, nc.vector.tensor_copy(count[:, :], bank[6][0:TP, 0:NX]))
                L(dve, nc.vector.tensor_scalar(tiles[:, :], count[:, :], 0.0, None, ALU.is_gt))
                for k in range(1, -(-N // TS)):
                    L(dve, nc.vector.scalar_tensor_tensor(tiles[:, :], count[:, :], float(TS * k), tiles[:, :],
                                                          ALU.is_gt, ALU.add))
                L(dve, nc.vector.tensor_copy(cum[:, :], tiles[:, :]))
                for e in range(1, NX):
                    L(dve, TT(cum[:, e:e + 1], cum[:, e - 1:e], tiles[:, e:e + 1], ALU.add))
                L(dve, TT(count[:, :], cum[:, :], tiles[:, :], ALU.subtract))
                L(dve, nc.vector.scalar_tensor_tensor(place[:, 0, :], count[:, :], float(TS), place[:, 0, :],
                                                      ALU.mult, ALU.add))
                for t in range(1, NT):
                    L(dve, TT(place[:, t, :], place[:, t - 1, :], hot_e[:, t - 1, :], ALU.add))
                L(dve, TT(place[:, :, :], place[:, :, :], hot_e[:, :, :], ALU.mult))
                L(dve, nc.vector.tensor_reduce(slot_f[:, :], place[:, :, :], AX_X, ALU.add))
                nc.vector.tensor_copy(slot[:, :], slot_f[:, :])
                L(dve, nc.vector.tensor_scalar(tile_ef[:, :], tile_no[:, :], cum[0:1, 0:1], None, ALU.is_ge))
                for e in range(1, NX):
                    L(dve, nc.vector.scalar_tensor_tensor(tile_ef[:, :], tile_no[:, :], cum[0:1, e:e + 1],
                                                          tile_ef[:, :], ALU.is_ge, ALU.add))
                nc.vector.tensor_scalar(tile_e[:, :], tile_ef[:, :], float(NX - 1), None, ALU.min).then_inc(slots_made, 1)
                for t in range(NT):
                    nc.vector.tensor_scalar(y[:, t, :], nodes[:, t, :], mv[:, t, 0:1], rstd[:, t:t + 1],
                                            ALU.subtract, ALU.mult).then_inc(y_made, 1)
                for i in range(NST):
                    dve.wait_ge(f_ready, i + 1)
                    if i >= 2:
                        dve.wait_ge(f_stored[i % 2], 16 * (i // 2))
                    nc.vector.tensor_tensor(fo[i % 2][:, :], bank[4 + i % 2][:, :], b2e[i % FR][:, :],
                                            ALU.add).then_inc(f_made, 1)
                for t in range(NT):
                    dve.wait_ge(f_back[t], 16)
                    nc.vector.scalar_tensor_tensor(fg[:, t, :], fg[:, t, :], score[:, t:t + 1], nodes[:, t, :],
                                                   ALU.mult, ALU.add).then_inc(out_made, 1)

            @block.tensor
            def _(pe):
                for t in range(NT):
                    if t >= 3:
                        pe.wait_ge(x1_taken, t - 2)
                    for k in range(KC):
                        last = nc.tensor.transpose(bank[t % 3][0:TP, k * 128:(k + 1) * 128],
                                                   base[:, k, t * TP:(t + 1) * TP], ident[:, :])
                    last.then_inc(x1_turned, 1)
                pe.wait_ge(wg_loaded, 32)
                for t in range(NT):
                    for k in range(KC):
                        nc.tensor.matmul(bank[4][0:TP, t * NX:(t + 1) * NX], base[:, k, t * TP:(t + 1) * TP],
                                         wg_sb[:, k, :], start=(k == 0), stop=(k == KC - 1))
                for k in range(KC):
                    last = nc.tensor.matmul(bank[5][0:TP, 0:NX], ones[:, 0:TP], wg_sb[:, k, :],
                                            start=(k == 0), stop=(k == KC - 1))
                last.then_inc(logits_ready, 1)
                pe.wait_ge(held_made, 1)
                pe.wait_ge(consts5, 1)
                nc.tensor.matmul(bank[6][0:TP, 0:NX], ones[0:TP, 0:TP], held[:, :], start=True, stop=True)
                nc.tensor.matmul(bank[6][0:TP, NX:2 * NX], before[0:TP, 0:TP], held[:, :],
                                 start=True, stop=True).then_inc(counts_ready, 1)

                def turn(i):
                    pe.wait_ge(ew_loaded2[i % FR], 16 * (i // FR + 1))
                    if i >= 2:
                        pe.wait_ge(yt_made, i - 1)
                    for k in range(KC):
                        last = nc.tensor.transpose(bank[i % 2][:, k * TS:(k + 1) * TS],
                                                   yin[i % FR][:, k * 128:(k + 1) * 128], ident[:, :])
                    last.then_inc(y_turned, 1)

                turn(0)
                for i in range(NST):
                    r = i % FR
                    pe.wait_ge(ew_loaded[r], 64 * (i // FR + 1))
                    pe.wait_ge(yt_made, i + 1)
                    if i >= 2:
                        pe.wait_ge(hid_made, i - 1)
                    for m in range(HX // 128):
                        for k in range(KC):
                            last = nc.tensor.matmul(bank[2 + i % 2][:, m * TS:(m + 1) * TS],
                                                    w1e[r][:, k, m * 128:(m + 1) * 128], yt[i % 2][:, k, :],
                                                    start=(k == 0), stop=(k == KC - 1))
                    last.then_inc(hid_ready, 1)
                    if i + 1 < NST:
                        turn(i + 1)
                    pe.wait_ge(hid_made, i + 1)
                    if i >= 2:
                        pe.wait_ge(f_made, i - 1)
                    for m in range(HX // 128):
                        last = nc.tensor.matmul(bank[4 + i % 2][:, :], hid[i % 2][:, m, :], w2e[r][:, m, :],
                                                start=(m == 0), stop=(m == HX // 128 - 1))
                    last.then_inc(f_ready, 1)
        s5.close()


def layouts(np, a):
    blocks = lambda w: w.T.reshape(KC, 128, w.shape[0]).transpose(1, 0, 2)
    ih, hh = blocks(a["L0_gnn_W_ih"]), blocks(a["L0_gnn_W_hh"])
    column = lambda v: v.reshape(KC, 128).T
    bih, bhh = a["L0_gnn_b_ih"].reshape(3, D), a["L0_gnn_b_hh"].reshape(3, D)
    return {
        "x_nodes": a["x"],
        "x_feat": a["x"].T,
        "src_cols": a["src"].reshape(NG * TG, TP).T,
        "dst_cols": a["dst"].reshape(NG * TG, TP).T,
        "dst_groups": a["dst"].reshape(NG, EG),
        "edge_blocks": a["edge_attr_128"].reshape(NG, EG, ED).transpose(0, 2, 1),
        "w1a": a["L0_gnn_W1"][:, :D].T,
        "w1b": a["L0_gnn_W1"][:, D:].T,
        "wk": a["L0_mix_Wk"], "wv": a["L0_mix_Wv"], "wq": a["L0_mix_Wq"], "wp": a["L0_mix_Wp"],
        "w2": a["L0_gnn_W2"].T,
        "gate_blocks": np.stack([w[:, :, g * D + c * 128:g * D + (c + 1) * 128]
                                 for c in range(KC) for g in range(3) for w in (ih, hh)]),
        "wg": a["L0_ffn_Wg"], "we1": a["L0_ffn_W1"], "we2": a["L0_ffn_W2"],
        "b1": a["L0_gnn_b1"], "bk": a["L0_mix_bk"], "bv": a["L0_mix_bv"], "b2": a["L0_gnn_b2"],
        "cols": np.stack([column(v) for v in (
            a["L0_mix_bq"], a["L0_mix_bp"], bih[0], bih[1], bih[2], bhh[0], bhh[1], bhh[2], a["L0_gnn_gamma"],
            a["L0_gnn_beta"], a["L0_gnn_run_mean"], a["L0_gnn_run_var"])], axis=1),
        "bg": a["L0_ffn_bg"],
        "be1": a["L0_ffn_b1"].reshape(NX, HX // 128, 128).transpose(0, 2, 1),
        "be2": a["L0_ffn_b2"],
    }


def kernel(**inputs):
    import numpy as _np
    import concourse.bacc as _bacc
    from concourse.bass_utils import run_bass_kernel_spmd as _run

    nc = _bacc.Bacc("TRN2", target_bir_lowering=False, num_devices=1)
    arrays, aps = {}, {}
    for name, a in layouts(_np, {k: _np.asarray(v) for k, v in inputs.items()}).items():
        a = _np.ascontiguousarray(a)
        arrays[f"in_{name}"] = a
        aps[name] = nc.dram_tensor(f"in_{name}", a.shape, mybir.dt.from_np(a.dtype), kind="ExternalInput").ap()
    for name, rows_n in (("proj", N), ("slot_in", NSLOT), ("slot_out", NSLOT)):
        aps[name] = nc.dram_tensor(f"{name}_table", (rows_n, D), F32, kind="Internal").ap()
    aps["out"] = nc.dram_tensor("out_x", (N, D), F32, kind="ExternalOutput").ap()
    build(nc, **aps)
    r = _run(nc, [arrays], core_ids=[0])
    return r.results[0]["out_x"]
```

```python
from contextlib import ExitStack

import concourse.bass as bass
from concourse import mybir

F32 = mybir.dt.float32
F32R = mybir.dt.float32r
I32 = mybir.dt.int32
ALU = mybir.AluOpType
ACT = mybir.ActivationFunctionType
AX_X = mybir.AxisListType.X

N, D, E, ED = 1250, 512, 40000, 128
TP = 125
NT = N // TP
KC = D // 128
TG = 4
EG = TP * TG
NG = E // EG
HEADS, DH = 8, 64
NX, HX = 8, 256
TS = 128
NST = (N + NX * (TS - 1)) // TS
NSLOT = NST * TS
ROW = D + 4
EPS = 1e-5
SLICES = [(0, 418), (418, 416), (834, 416)]
TWO_PASS = (0, 2)
SCALE_X0 = 256


class Counter:

    def __init__(self, sem):
        self.sem, self.n = sem, 0

    def link(self, eng, ins):
        ins.then_inc(self.sem, 1)
        self.n += 1
        eng.wait_ge(self.sem, self.n)


def rows_dma(eng, dst, src, sem):
    eng.dma_start(dst[0:112], src[0:112]).then_inc(sem, 16)
    eng.dma_start(dst[112:TP], src[112:TP]).then_inc(sem, 16)


def build(nc, x_nodes, x_feat, src_blocks, dst_cols, dst_groups, edge_blocks, w1a, w1b, wk, wv, wq, wp, w2,
          gate_blocks, wg, we1, we2, b1, bk, bv, b2, cols, bg, be1, be2, proj, slot_in, out):
    with ExitStack() as ctx:
        def sb(name, shape, dt=F32, at=ctx):
            return at.enter_context(nc.sbuf_tensor(name, shape, dt))

        def sem(name):
            return ctx.enter_context(nc.semaphore(name))

        bank = [ctx.enter_context(nc.psum_tensor(f"bank{i}", [128, 512], F32)) for i in range(8)]

        base = sb("base", [128, KC, N])
        xn = sb("xn", [128, KC, N])
        rows = sb("rows", [TP, NT, ROW])
        nodes = rows[:, :, 0:D]
        ident = sb("ident", [128, 128])
        ones = sb("ones", [128, 128])
        bc = sb("bc", [128, 12, KC])
        COL = {n: bc[:, i, :] for i, n in enumerate(
            ["bq", "bp", "bir", "biz", "bin", "bhr", "bhz", "bhn", "gamma", "beta", "mean", "var"])}
        gscale = sb("gscale", [128, KC])
        gshift = sb("gshift", [128, KC])
        brz = sb("brz", [128, 2, KC])
        word = sb("word", [1, NG], I32)
        rel_neg = sb("rel_neg", [TP, NG * TG])
        dst_f = sb("dst_f", [TP, NG * TG])
        deg = sb("deg", [TP, NT, 2])
        stat = sb("stat", [TP, NT, KC, 6])
        mv = sb("mv", [TP, NT, 2])
        rstd = sb("rstd", [TP, NT])
        tmp_s = sb("tmp_s", [TP, NT])
        tmp_t = sb("tmp_t", [TP, NT])
        tmp_c = sb("tmp_c", [128, 3, KC])
        wg_sb = sb("wg_sb", [128, KC, NX])

        dve_chain, act_chain, pool_chain = (Counter(sem(n)) for n in ("dve_chain", "act_chain", "pool_chain"))
        epsc = sb("epsc", [128, 1])
        zeros = sb("zeros", [128, ROW // KC])

        def newton_rsqrt(dve, r, v, a, b):
            L = dve_chain.link
            L(dve, nc.vector.reciprocal(a, r))
            L(dve, nc.vector.tensor_tensor(b, a, a, ALU.mult))
            L(dve, nc.vector.tensor_tensor(b, b, v, ALU.mult))
            L(dve, nc.vector.tensor_scalar(b, b, -0.5, 1.5, ALU.mult, ALU.add))
            L(dve, nc.vector.tensor_tensor(r, a, b, ALU.mult))

        split = ExitStack()
        xh = sb("xh", [128, KC, N], F32R, split)
        xl = sb("xl", [128, KC, N], F32R, split)

        s1 = ExitStack()
        dstg_i = sb("dstg_i", [NG, EG], I32, s1)
        dstg = sb("dstg", [NG, EG], F32, s1)
        dstc_i = sb("dstc_i", [TP, NG * TG], I32, s1)
        mm = sb("mm", [NG, 2], F32, s1)
        win = sb("win", [NG, 2], F32, s1)
        extra = sb("extra", [NG, 1], F32, s1)
        upper = sb("upper", [NG, NG], F32, s1)
        diag = sb("diag", [NG, NG], F32, s1)
        lines = sb("lines", [1, 3, NG], F32, s1)
        r1 = sb("r1", [1, NG], F32, s1)
        x_loaded = [sem(f"x_loaded{h}") for h in range(2)]
        dst_loaded, cols_loaded, feat_loaded = (sem(n) for n in ("dst_loaded", "cols_loaded", "feat_loaded"))
        consts_made, stats_made, std_made, centred, turned, turned_used, high1 = (sem(n) for n in (
            "consts_made", "stats_made", "std_made", "centred", "turned", "turned_used", "high1"))
        win_made, rows_ready, diag_made, spread_ready, table_zeroed = (sem(n) for n in (
            "win_made", "rows_ready", "diag_made", "spread_ready", "table_zeroed"))
        zeros_made = sem("zeros_made")

        with nc.Block() as block:
            @block.sync
            def _(sp):
                for h in range(2):
                    rows_dma(sp, nodes[:, 5 * h:5 * h + 5, :],
                             x_nodes.rearrange("(t p) f -> p t f", p=TP)[:, 5 * h:5 * h + 5, :], x_loaded[h])
                sp.dma_start(dstg_i[:, :], dst_groups).then_inc(dst_loaded, 16)
                sp.dma_start(dstc_i[:, :], dst_cols).then_inc(dst_loaded, 16)
                sp.dma_start(bc[:, :, :], cols).then_inc(cols_loaded, 16)
                sp.dma_start(base[:, :, :], x_feat.rearrange("(k p) n -> p k n", p=128)).then_inc(feat_loaded, 16)
                sp.wait_ge(zeros_made, 1)
                for i in range(NST):
                    sp.dma_start(slot_in[i * TS:(i + 1) * TS, :].rearrange("p (a f) -> p a f", a=KC),
                                 zeros[0:TS, :].unsqueeze(1).to_broadcast([TS, KC, ROW // KC])).then_inc(table_zeroed, 16)

            @block.gpsimd
            def _(pool):
                nc.gpsimd.memset(zeros[:, :], 0.0).then_inc(zeros_made, 1)
                pool_chain.link(pool, nc.gpsimd.memset(ones[:, :], 1.0))
                pool_chain.link(pool, nc.gpsimd.memset(epsc[:, :], EPS))
                nc.gpsimd.affine_select(out=ident[:, :], in_=ones[:, :], compare_op=ALU.is_equal, fill=0.0,
                                        base=0, pattern=[[-1, 128]], channel_multiplier=1).then_inc(consts_made, 1)
                nc.gpsimd.affine_select(out=upper[:, :], in_=ones[0:NG, 0:NG], compare_op=ALU.is_gt, fill=0.0,
                                        base=0, pattern=[[1, NG]], channel_multiplier=-1).then_inc(consts_made, 1)

            @block.scalar
            def _(act):
                act.wait_ge(stats_made, 1)
                act.wait_ge(consts_made, 2)
                nc.scalar.activation(rstd[:, :], mv[:, :, 1], ACT.Sqrt, bias=epsc[0:TP, :]).then_inc(std_made, 1)
                act.wait_ge(cols_loaded, 16)
                nc.scalar.activation(gscale[:, :], COL["var"], ACT.Sqrt, bias=epsc[:, :]).then_inc(std_made, 1)
                for t in range(NT):
                    act.wait_ge(turned, t + 1)
                    s = slice(t * TP, (t + 1) * TP)
                    pb = bank[t % 4][:, 0:KC * TP].rearrange("p (k n) -> p k n", k=KC)
                    nc.scalar.copy(xn[:, :, s], pb)
                    nc.scalar.copy(xh[:, :, s], pb).then_inc(high1, 1)

            @block.vector
            def _(dve):
                L = dve_chain.link
                for t in range(NT):
                    if t % 5 == 0:
                        dve.wait_ge(x_loaded[t // 5], 32)
                    L(dve, nc.vector.bn_stats(stat[:, t, 0, :], nodes[:, t, :]))
                    last = nc.vector.bn_aggr(mv[:, t, :], stat[:, t, 0, :])
                last.then_inc(stats_made, 1)
                dve.wait_ge(stats_made, 1)
                L(dve, nc.vector.tensor_scalar(tmp_t[:, :], mv[:, :, 1], EPS, None, ALU.add))
                dve.wait_ge(std_made, 1)
                newton_rsqrt(dve, rstd[:, :], tmp_t[:, :], tmp_s[:, :], stat[:, :, 0, 0])
                for t in range(NT):
                    nc.vector.tensor_scalar(nodes[:, t, :], nodes[:, t, :], mv[:, t, 0:1], rstd[:, t:t + 1],
                                            ALU.subtract, ALU.mult).then_inc(centred, 1)
                dve.wait_ge(dst_loaded, 32)
                L(dve, nc.vector.tensor_copy(dstg[:, :], dstg_i[:, :]))
                nc.vector.tensor_copy(dst_f[:, :], dstc_i[:, :])
                nc.vector.tensor_reduce(mm[:, 0:1], dstg[:, :], AX_X, ALU.min)
                L(dve, nc.vector.tensor_reduce(mm[:, 1:2], dstg[:, :], AX_X, ALU.max))
                L(dve, nc.vector.tensor_scalar(win[:, :], mm[:, :], float(TP), None, ALU.is_ge))
                for w in range(2, NT):
                    L(dve, nc.vector.scalar_tensor_tensor(win[:, :], mm[:, :], float(TP * w), win[:, :],
                                                          ALU.is_ge, ALU.add))
                nc.vector.tensor_tensor(extra[:, :], win[:, 1:2], win[:, 0:1], ALU.subtract).then_inc(win_made, 1)
                dve.wait_ge(consts_made, 2)
                nc.vector.tensor_scalar(diag[:, :], ident[0:NG, 0:NG], win[:, 0:1], float(TP),
                                        ALU.mult, ALU.mult).then_inc(diag_made, 1)
                for t in range(NT):
                    dve.wait_ge(high1, t + 1)
                    pb = bank[t % 4][:, 0:KC * TP].rearrange("p (k n) -> p k n", k=KC)
                    s = slice(t * TP, (t + 1) * TP)
                    nc.vector.tensor_tensor(xl[:, :, s], pb, xh[:, :, s], ALU.subtract).then_inc(turned_used, 1)
                dve.wait_ge(rows_ready, 1)
                pr = bank[6][0:1, 0:3 * NG].rearrange("p (a g) -> p a g", a=3)
                L(dve, nc.vector.tensor_copy(lines[:, :, :], pr))
                lo, ex, x0 = lines[:, 0, :], lines[:, 1, :], lines[:, 2, :]
                L(dve, nc.vector.scalar_tensor_tensor(r1[:, :], x0, float(SCALE_X0 // 16), ex, ALU.mult, ALU.add))
                L(dve, nc.vector.scalar_tensor_tensor(word[:, :], r1[:, :], 16.0, lo, ALU.mult, ALU.add))
                dve.wait_ge(spread_ready, 1)
                L(dve, nc.vector.tensor_tensor(
                    rel_neg[:, :].rearrange("p (g t) -> p g t", t=TG),
                    bank[7][0:TP, 0:NG].unsqueeze(2).to_broadcast([TP, NG, TG]),
                    dst_f[:, :].rearrange("p (g t) -> p g t", t=TG), ALU.subtract))
                L(dve, nc.vector.tensor_scalar(tmp_c[:, 0, :], COL["var"], EPS, None, ALU.add))
                dve.wait_ge(std_made, 2)
                newton_rsqrt(dve, gscale[:, :], tmp_c[:, 0, :], tmp_c[:, 1, :], tmp_c[:, 2, :])
                L(dve, nc.vector.tensor_tensor(gscale[:, :], gscale[:, :], COL["gamma"], ALU.mult))
                L(dve, nc.vector.tensor_tensor(gshift[:, :], gscale[:, :], COL["mean"], ALU.mult))
                L(dve, nc.vector.tensor_tensor(gshift[:, :], COL["beta"], gshift[:, :], ALU.subtract))
                L(dve, nc.vector.tensor_tensor(gshift[:, :], gshift[:, :], COL["bp"], ALU.add))
                nc.vector.tensor_tensor(brz[:, 0, :], COL["bir"], COL["bhr"], ALU.add)
                L(dve, nc.vector.tensor_tensor(brz[:, 1, :], COL["biz"], COL["bhz"], ALU.add))

            @block.tensor
            def _(pe):
                pe.wait_ge(consts_made, 2)
                for t in range(NT):
                    pe.wait_ge(centred, t + 1)
                    if t >= 4:
                        pe.wait_ge(turned_used, t - 3)
                    for k in range(KC):
                        last = nc.tensor.transpose(bank[t % 4][:, k * TP:(k + 1) * TP],
                                                   nodes[:, t, k * 128:(k + 1) * 128], ident[0:TP, 0:TP])
                    last.then_inc(turned, 1)
                pe.wait_ge(win_made, 1)
                nc.tensor.matmul(bank[6][0:1, 0:NG], win[:, 0:1], ident[0:NG, 0:NG], start=True, stop=True)
                nc.tensor.matmul(bank[6][0:1, NG:2 * NG], extra[:, :], ident[0:NG, 0:NG], start=True, stop=True)
                nc.tensor.matmul(bank[6][0:1, 2 * NG:3 * NG], extra[:, :], upper[:, :],
                                 start=True, stop=True).then_inc(rows_ready, 1)
                pe.wait_ge(diag_made, 1)
                nc.tensor.matmul(bank[7][0:TP, 0:NG], ones[0:NG, 0:TP], diag[:, :],
                                 start=True, stop=True).then_inc(spread_ready, 1)
        s1.close()

        s2 = ExitStack()
        kf = sb("kf", [TP, NT, D], F32, s2)
        qf = sb("qf", [128, KC, N], F32, s2)
        w_raw = [sb(f"w_raw{i}", [128, 2, D], F32, s2) for i in range(2)]
        w_hi = [sb(f"w_hi{i}", [128, KC, D], F32R, s2) for i in range(2)]
        w_lo = [sb(f"w_lo{i}", [128, KC, D], F32R, s2) for i in range(2)]
        bias_row = sb("bias_row", [TP, 3, D], F32, s2)
        row_out = [sb(f"row_out{i}", [TP, D], F32, s2) for i in range(2)]
        exp_t = [sb(f"exp_t{i}", [128, D], F32, s2) for i in range(2)]
        relu_t = [sb(f"relu_t{i}", [128, D], F32, s2) for i in range(2)]
        kv_sb = sb("kv_sb", [128, KC, 128], F32, s2)
        ksum8 = sb("ksum8", [128, KC, HEADS], F32, s2)
        rden = sb("rden", [TP, NT * HEADS], F32, s2)
        rden_t = kf[0:HEADS, :, :].rearrange("p t f -> p (t f)")[:, 0:N]
        head_rows = sb("head_rows", [HEADS, D], F32, s2)
        v_nodes = nodes
        UNITS = 5
        w_loaded = [sem(f"w_loaded{i}") for i in range(2)]
        w_high, w_low, out_ready = (sem(n) for n in (
            "w_high", "w_low", "out_ready"))
        proj_made, proj_stored, k_biased, k_parts, k_made, v_made, q_parts, q_made = (sem(n) for n in (
            "proj_made", "proj_stored", "k_biased", "k_parts", "k_made", "v_made", "q_parts", "q_made"))
        proj_stored = [proj_stored, sem("proj_stored1")]
        bias_loaded, kv_ready, kv_made, den_ready, rden_made, rdent_ready, rdent_made = (sem(n) for n in (
            "bias_loaded", "kv_ready", "kv_made", "den_ready", "rden_made", "rdent_ready", "rdent_made"))
        att_ready, rb_copied, att_made, att_high, att_low, base_made, s2_zeroed = (sem(n) for n in (
            "att_ready", "rb_copied", "att_made", "att_high", "att_low", "base_made", "s2_zeroed"))
        mix_ready, mix_added = sem("mix_ready"), sem("mix_added")
        att_f = exp_t
        rb_sb = relu_t

        def product3(out_ap, lhs, rhs, first, last):
            nc.tensor.matmul(out_ap, lhs[0], rhs[0], start=first, stop=False)
            nc.tensor.matmul(out_ap, lhs[0], rhs[1], start=False, stop=False)
            return nc.tensor.matmul(out_ap, lhs[1], rhs[0], start=False, stop=last)

        QJ = [(c, s) for c in range(KC) for s in range(len(SLICES))]

        with nc.Block() as block:
            @block.sync
            def _(sp):
                sp.dma_start(bias_row[:, 0, :], b1.unsqueeze(0).to_broadcast([TP, D])).then_inc(bias_loaded, 16)
                sp.dma_start(bias_row[:, 1, :], bk.unsqueeze(0).to_broadcast([TP, D])).then_inc(bias_loaded, 16)
                sp.dma_start(bias_row[:, 2, :], bv.unsqueeze(0).to_broadcast([TP, D])).then_inc(bias_loaded, 16)

                def load(h):
                    w = (w1a, wk, wv, wq, wp)[h // 2]
                    if h >= 2:
                        sp.wait_ge(w_low, h - 1)
                    sp.dma_start(w_raw[h % 2][:, :, :], w.rearrange("(k p) f -> p k f", p=128)[
                        :, 2 * (h % 2):2 * (h % 2) + 2, :]).then_inc(w_loaded[h % 2], 16)

                for h in range(4):
                    load(h)
                for t in range(NT):
                    sp.wait_ge(proj_made, t + 1)
                    rows_dma(sp, proj[t * TP:(t + 1) * TP, :], row_out[t % 2], proj_stored[t % 2])
                for h in range(4, 2 * UNITS):
                    load(h)
                sp.wait_ge(proj_stored[0], 32 * 5)
                sp.wait_ge(proj_stored[1], 32 * 5)

            @block.gpsimd
            def _(pool):
                nc.gpsimd.memset(kv_sb[:, :, :], 0.0)
                nc.gpsimd.memset(ksum8[:, :, :], 0.0)
                hr = head_rows[:, :]
                pool_chain.link(pool, nc.gpsimd.memset(hr, 1.0))
                pool_chain.link(pool, nc.gpsimd.affine_select(
                    out=hr, in_=hr, compare_op=ALU.is_ge, fill=0.0, base=0, pattern=[[1, D]], channel_multiplier=-DH))
                nc.gpsimd.affine_select(out=hr, in_=hr, compare_op=ALU.is_ge, fill=0.0, base=DH - 1,
                                        pattern=[[-1, D]], channel_multiplier=DH).then_inc(s2_zeroed, 1)
                pool.wait_ge(feat_loaded, 16)
                nc.gpsimd.tensor_tensor(base[:, :, :], base[:, :, :], xn[:, :, :], ALU.add).then_inc(base_made, 1)

            @block.scalar
            def _(act):
                def high(u):
                    if u >= 2:
                        act.wait_ge(out_ready, (u - 1) * NT)
                    for h in (2 * u, 2 * u + 1):
                        act.wait_ge(w_loaded[h % 2], 16 * (u + 1))
                        kk = slice(2 * (h % 2), 2 * (h % 2) + 2)
                        nc.scalar.copy(w_hi[u % 2][:, kk, :], w_raw[h % 2][:, :, :]).then_inc(w_high, 1)

                high(0)
                high(1)
                high(2)
                for t in range(NT):
                    act.wait_ge(k_biased, t + 1)
                    nc.scalar.activation(exp_t[t % 2][0:TP, :], row_out[t % 2][:, :], ACT.Exp)
                    nc.scalar.activation(relu_t[t % 2][0:TP, :], row_out[t % 2][:, :], ACT.Relu).then_inc(k_parts, 1)
                high(3)
                high(4)
                for j, (c, s) in enumerate(QJ):
                    a, n = SLICES[s]
                    act.wait_ge(out_ready, 3 * NT + j + 1)
                    if j < 2:
                        act.wait_ge(k_made, NT)
                    else:
                        act.wait_ge(q_made, j - 1)
                    pb = bank[(3 * NT + j) % 6][:, 0:n]
                    nc.scalar.activation(exp_t[j % 2][:, 0:n], pb, ACT.Exp, bias=COL["bq"][:, c:c + 1])
                    nc.scalar.activation(relu_t[j % 2][:, 0:n], pb, ACT.Relu,
                                         bias=COL["bq"][:, c:c + 1]).then_inc(q_parts, 1)
                for i in range(3):
                    act.wait_ge(rdent_ready, i + 1)
                    n = min(4, NT - 4 * i) * TP
                    nc.scalar.copy(rden_t[:, 4 * i * TP:4 * i * TP + n],
                                   bank[1 + i][0:HEADS, 0:n]).then_inc(rdent_made, 1)
                for j, (c, s) in enumerate(QJ):
                    a, n = SLICES[s]
                    act.wait_ge(att_ready, j + 1)
                    if j >= 2:
                        act.wait_ge(att_made, j - 1)
                    nc.scalar.copy(rb_sb[j % 2][:, 0:n], bank[6 + j % 2][:, 0:n]).then_inc(rb_copied, 1)
                    act.wait_ge(att_made, j + 1)
                    nc.scalar.copy(xh[:, c, a:a + n], att_f[j % 2][:, 0:n]).then_inc(att_high, 1)

            @block.vector
            def _(dve):
                def low(u):
                    for h in (2 * u, 2 * u + 1):
                        dve.wait_ge(w_high, h + 1)
                        kk = slice(2 * (h % 2), 2 * (h % 2) + 2)
                        nc.vector.tensor_tensor(w_lo[u % 2][:, kk, :], w_raw[h % 2][:, :, :],
                                                w_hi[u % 2][:, kk, :], ALU.subtract).then_inc(w_low, 1)

                low(0)
                low(1)
                dve.wait_ge(bias_loaded, 48)
                for t in range(NT):
                    dve.wait_ge(out_ready, t + 1)
                    if t >= 2:
                        dve.wait_ge(proj_stored[t % 2], 32 * (t // 2))
                    nc.vector.tensor_tensor(row_out[t % 2][:, :], bank[t % 6][0:TP, :], bias_row[:, 0, :],
                                            ALU.add).then_inc(proj_made, 1)
                low(2)

                def key(t):
                    dve.wait_ge(k_parts, t + 1)
                    nc.vector.scalar_tensor_tensor(kf[:, t, :], exp_t[t % 2][0:TP, :], 1.0, relu_t[t % 2][0:TP, :],
                                                   ALU.min, ALU.add).then_inc(k_made, 1)

                for t in range(NT):
                    dve.wait_ge(out_ready, NT + t + 1)
                    if t < 2:
                        dve.wait_ge(proj_stored[t % 2], 32 * 5)
                    else:
                        dve.wait_ge(k_parts, t - 1)
                    nc.vector.tensor_tensor(row_out[t % 2][:, :], bank[(NT + t) % 6][0:TP, :], bias_row[:, 1, :],
                                            ALU.add).then_inc(k_biased, 1)
                    if t:
                        key(t - 1)
                key(NT - 1)
                low(3)
                for t in range(NT):
                    dve.wait_ge(out_ready, 2 * NT + t + 1)
                    nc.vector.tensor_tensor(v_nodes[:, t, :], bank[(2 * NT + t) % 6][0:TP, :], bias_row[:, 2, :],
                                            ALU.add).then_inc(v_made, 1)
                low(4)
                for j, (c, s) in enumerate(QJ):
                    a, n = SLICES[s]
                    dve.wait_ge(q_parts, j + 1)
                    nc.vector.scalar_tensor_tensor(qf[:, c, a:a + n], exp_t[j % 2][:, 0:n], 1.0,
                                                   relu_t[j % 2][:, 0:n], ALU.min, ALU.add).then_inc(q_made, 1)
                dve.wait_ge(s2_zeroed, 1)
                dve.wait_ge(kv_ready, 1)
                kvp = bank[6][:, :].rearrange("p (c e) -> p c e", c=KC)
                k8 = ksum8[:, :, :].rearrange("p c h -> p (c h)")
                for h in range(2):
                    q = slice(64 * h, 64 * h + 64)
                    nc.vector.tensor_copy(kv_sb[q, :, q], kvp[q, :, q])
                    nc.vector.tensor_copy(k8[q, h:h + 31:10], bank[7][q, 0:KC]).then_inc(kv_made, 1)
                dve.wait_ge(den_ready, 1)
                nc.vector.reciprocal(rden[:, :], bank[0][0:TP, 0:NT * HEADS]).then_inc(rden_made, 1)
                for j, (c, s) in enumerate(QJ):
                    a, n = SLICES[s]
                    dve.wait_ge(rb_copied, j + 1)
                    if j >= 2:
                        dve.wait_ge(att_high, j - 1)
                    nc.vector.tensor_tensor(att_f[j % 2][:, 0:n], bank[4 + j % 2][:, 0:n], rb_sb[j % 2][:, 0:n],
                                            ALU.mult).then_inc(att_made, 1)
                    dve.wait_ge(att_high, j + 1)
                    nc.vector.tensor_tensor(xl[:, c, a:a + n], att_f[j % 2][:, 0:n], xh[:, c, a:a + n],
                                            ALU.subtract).then_inc(att_low, 1)
                dve.wait_ge(base_made, 1)
                for j, (c, s) in enumerate(QJ):
                    a, n = SLICES[s]
                    dve.wait_ge(mix_ready, j + 1)
                    nc.vector.scalar_tensor_tensor(base[:, c, a:a + n], bank[j % 4][:, 0:n], gshift[:, c:c + 1],
                                                   base[:, c, a:a + n], ALU.add, ALU.add).then_inc(mix_added, 1)

            @block.tensor
            def _(pe):
                def free(j):
                    j -= 6
                    if j < 0:
                        return
                    if j < NT:
                        pe.wait_ge(proj_made, j + 1)
                    elif j < 2 * NT:
                        pe.wait_ge(k_biased, j - NT + 1)
                    elif j < 3 * NT:
                        pe.wait_ge(v_made, j - 2 * NT + 1)
                    else:
                        pe.wait_ge(q_parts, j - 3 * NT + 1)

                for u in range(3):
                    pe.wait_ge(w_low, 2 * u + 2)
                    for t in range(NT):
                        free(u * NT + t)
                        s = slice(t * TP, (t + 1) * TP)
                        for k in range(KC):
                            last = product3(bank[(u * NT + t) % 6][0:TP, :], (xh[:, k, s], xl[:, k, s]),
                                            (w_hi[u % 2][:, k, :], w_lo[u % 2][:, k, :]), k == 0, k == KC - 1)
                        last.then_inc(out_ready, 1)
                pe.wait_ge(w_low, 8)
                for j, (c, s) in enumerate(QJ):
                    a, n = SLICES[s]
                    free(3 * NT + j)
                    cc = slice(c * 128, (c + 1) * 128)
                    for k in range(KC):
                        last = product3(bank[(3 * NT + j) % 6][:, 0:n], (w_hi[1][:, k, cc], w_lo[1][:, k, cc]),
                                        (xh[:, k, a:a + n], xl[:, k, a:a + n]), k == 0, k == KC - 1)
                    last.then_inc(out_ready, 1)
                pe.wait_ge(k_made, NT)
                pe.wait_ge(v_made, NT)
                for c in range(KC):
                    cc = slice(c * 128, (c + 1) * 128)
                    for t in range(NT):
                        nc.tensor.matmul(bank[6][:, cc], kf[:, t, cc], v_nodes[:, t, cc],
                                         start=(t == 0), stop=(t == NT - 1))
                        last = nc.tensor.matmul(bank[7][:, c:c + 1], kf[:, t, cc], ones[0:TP, 0:1],
                                                start=(t == 0), stop=(t == NT - 1))
                last.then_inc(kv_ready, 1)
                pe.wait_ge(kv_made, 2)
                pe.wait_ge(q_made, len(QJ))
                for t in range(NT):
                    for c in range(KC):
                        last = nc.tensor.matmul(bank[0][0:TP, t * HEADS:(t + 1) * HEADS],
                                                qf[:, c, t * TP:(t + 1) * TP], ksum8[:, c, :],
                                                start=(c == 0), stop=(c == KC - 1))
                last.then_inc(den_ready, 1)
                pe.wait_ge(rden_made, 1)
                for t in range(NT):
                    last = nc.tensor.transpose(bank[1 + t // 4][0:HEADS, (t % 4) * TP:(t % 4 + 1) * TP],
                                               rden[:, t * HEADS:(t + 1) * HEADS], ident[0:TP, 0:TP])
                    if t % 4 == 3 or t == NT - 1:
                        last.then_inc(rdent_ready, 1)
                pe.wait_ge(rdent_made, 3)
                for j, (c, s) in enumerate(QJ):
                    a, n = SLICES[s]
                    if j >= 2:
                        pe.wait_ge(att_made, j - 1)
                    nc.tensor.matmul(bank[4 + j % 2][:, 0:n], kv_sb[:, c, :], qf[:, c, a:a + n],
                                     start=True, stop=True)
                    nc.tensor.matmul(bank[6 + j % 2][:, 0:n], head_rows[:, c * 128:(c + 1) * 128],
                                     rden_t[:, a:a + n], start=True, stop=True).then_inc(att_ready, 1)
                pe.wait_ge(w_low, 10)
                pe.wait_ge(att_low, len(QJ))
                for j, (c, s) in enumerate(QJ):
                    a, n = SLICES[s]
                    if j >= 4:
                        pe.wait_ge(mix_added, j - 3)
                    cc = slice(c * 128, (c + 1) * 128)
                    for k in range(KC):
                        last = product3(bank[j % 4][:, 0:n], (w_hi[0][:, k, cc], w_lo[0][:, k, cc]),
                                        (xh[:, k, a:a + n], xl[:, k, a:a + n]), k == 0, k == KC - 1)
                    last.then_inc(mix_ready, 1)
        s2.close()
        split.close()

        s3 = ExitStack()
        wb_raw = sb("wb_raw", [ED, D], F32, s3)
        wb_hi = sb("wb_hi", [ED, D], F32R, s3)
        wb_lo = sb("wb_lo", [ED, D], F32R, s3)
        iota_n = sb("iota_n", [TP, N + 2], F32, s3)
        idx = [sb(f"idx{p}", [TP, TG], I32, s3) for p in range(2)]
        e_raw = [sb(f"e_raw{p}", [ED, EG], F32, s3) for p in range(2)]
        e_hi = [sb(f"e_hi{p}", [ED, EG], F32R, s3) for p in range(2)]
        e_lo = [sb(f"e_lo{p}", [ED, EG], F32R, s3) for p in range(2)]
        gath = [[sb(f"gath{p}{t}", [TP, D], F32, s3) for t in range(TG)] for p in range(2)]
        pre_sum = [sb(f"pre_sum{t}", [TP, D], F32, s3) for t in range(TG)]
        m_hi = [[sb(f"m_hi{p}{t}", [TP, D], F32R if t in TWO_PASS else F32, s3) for t in range(TG)] for p in range(2)]
        m_lo = [{t: sb(f"m_lo{p}{t}", [TP, D], F32R, s3) for t in TWO_PASS} for p in range(2)]
        hot = [sb(f"hot{p}", [TP, TG, TP + 1], F32R, s3) for p in range(2)]
        hot_x = sb("hot_x", [TP, TG, TP + 1], F32R, s3)
        offset_sq = sb("offset_sq", [TP, TG, TP + 1], F32, s3)
        ones2 = sb("ones2", [TP, 2], F32R, s3)
        NW = len(TWO_PASS)

        wb_loaded, wb_high, wb_low, iota_made = (sem(n) for n in (
            "wb_loaded", "wb_high", "wb_low", "iota_made"))
        e_loaded = [sem(f"e_loaded{p}") for p in range(2)]
        idx_loaded = [sem(f"idx_loaded{p}") for p in range(2)]
        gathered = [[sem(f"gathered{p}{t}") for t in range(TG)] for p in range(2)]
        e_high, e_low, pre_ready, added, relued, lowered, hot_made, summed, taken = (sem(n) for n in (
            "e_high", "e_low", "pre_ready", "added", "relued", "lowered", "hot_made", "summed", "taken"))
        squared = sem("squared")
        hot_x_made, summed_x, taken_x = sem("hot_x_made"), sem("summed_x"), sem("taken_x")
        e_low_first = sem("e_low_first")
        EH = EG // 2
        PRE, SUM, DEG = bank[0:4], bank[4:6], bank[6:8]

        def rel_neg_at(i):
            return rel_neg[:, i:i + 1] if isinstance(i, int) else rel_neg[:, bass.ds(i, 1)]

        def in_pairs(eng, first, last, step):
            pairs = (last - first) // 2
            with eng.Fori(0, pairs) as j:
                for p in range(2):
                    step(j * 2 + (first + p), p)
            for g in range(first + 2 * pairs, last):
                step(g, g % 2)

        def a_window(value):
            return nc.s_assert_within(value, 0, NT - 1, skip_runtime_bounds_check_because="made on the chip from counts of exceeded window bounds")

        def word_at(g):
            return word[0:1, g:g + 1] if isinstance(g, int) else word[0:1, bass.ds(g, 1)]

        def has_further(w):
            return (w & 255) >= 16

        def further_start(w):
            return nc.s_assert_within(w >> 8, 0, NG * (NT - 1) - 1, skip_runtime_bounds_check_because="made on the chip from counts of exceeded window bounds")

        def rest(eng, w, body):
            x0, more = further_start(w), (w >> 4) & 15
            with eng.If((w & 255) >= 32):
                with eng.Fori(x0 + 1, x0 + more) as x:
                    body(x, a_window(x - x0 + ((w & 15) + 1)))

        with nc.Block() as block:
            @block.sync
            def _(sp):
                sp.dma_start(wb_raw[:, :], w1b).then_inc(wb_loaded, 16)

                def step(g, p):
                    if not isinstance(g, int) or g >= 2:
                        sp.wait_ge(e_low, g - 1)
                        sp.wait_ge(e_low_first, g - 1)
                    sp.dma_start(e_raw[p][:, :], edge_blocks[g] if isinstance(g, int) else
                                 edge_blocks[bass.ds(g, 1)].rearrange("a p e -> p (a e)")).then_inc(e_loaded[p], 16)
                    if not isinstance(g, int) or g >= 2:
                        sp.wait_ge(added, g * TG - TG)
                    sp.dma_start(idx[p][:, :], src_blocks[g] if isinstance(g, int) else
                                 src_blocks[bass.ds(g, 1)].rearrange("a p t -> p (a t)")).then_inc(idx_loaded[p], 16)

                step(0, 0)
                step(1, 1)
                in_pairs(sp, 2, NG, step)

            @block.gpsimd
            def _(pool):
                nc.gpsimd.iota(iota_n[:, :], pattern=[[1, N + 2]], base=0, channel_multiplier=0,
                               allow_small_or_imprecise_dtypes=True).then_inc(iota_made, 1)

                def step(g, p):
                    pool.wait_ge(e_high, g + 1)
                    pool.wait_ge(idx_loaded[p], (g - p) * 8 + 16)
                    if not isinstance(g, int) or g >= 2:
                        pool.wait_ge(added, g * TG - TG)
                    nc.gpsimd.tensor_tensor(e_lo[p][:, EH:], e_raw[p][:, EH:], e_hi[p][:, EH:],
                                            ALU.subtract).then_inc(e_low, 1)
                    for t in range(TG):
                        pool.indirect_dma_start(
                            out=gath[p][t][:, :], out_offset=None, in_=proj,
                            in_offset=bass.IndirectOffsetOnAxis(ap=idx[p][:, t:t + 1], axis=0)
                        ).then_inc(gathered[p][t], 16)

                step(0, 0)
                step(1, 1)
                in_pairs(pool, 2, NG, step)

            @block.scalar
            def _(act):
                act.wait_ge(wb_loaded, 16)
                nc.scalar.copy(wb_hi[:, :], wb_raw[:, :]).then_inc(wb_high, 1)

                def edge_high(g, p):
                    act.wait_ge(e_loaded[p], (g - p) * 8 + 16)
                    if not isinstance(g, int) or g >= 2:
                        act.wait_ge(pre_ready, g * TG - TG)
                    nc.scalar.copy(e_hi[p][:, :], e_raw[p][:, :]).then_inc(e_high, 1)

                def one_hot_squares(g):
                    if not isinstance(g, int) or g >= 1:
                        act.wait_ge(hot_made, g)
                    for t in range(TG):
                        last = nc.scalar.activation(offset_sq[:, t, :], iota_n[:, 0:TP + 1], ACT.Square,
                                                    bias=rel_neg_at(g * TG + t))
                    last.then_inc(squared, 1)

                def one_hot_of(g, p):
                    act.wait_ge(squared, g + 1)
                    if not isinstance(g, int) or g >= 2:
                        act.wait_ge(summed, g - 1)
                    nc.scalar.activation(hot[p][:, :, :], offset_sq[:, :, :], ACT.Relu, scale=-2.0,
                                         bias=ones[0:TP, 0:1]).then_inc(hot_made, 1)

                def relu(g, p):
                    one_hot_squares(g)
                    for t in range(TG):
                        if t == 1:
                            one_hot_of(g, p)
                        act.wait_ge(added, g * TG + (t + 1))
                        nc.scalar.activation(m_hi[p][t][:, :], pre_sum[t][:, :], ACT.Relu).then_inc(relued, 1)

                edge_high(0, 0)
                edge_high(1, 1)
                act.wait_ge(iota_made, 1)
                relu(0, 0)
                edge_high(2, 0)

                def step(g, p):
                    relu(g, p)
                    edge_high(g + 2, p)

                with act.Fori(0, (NG - 4) // 2) as j:
                    step(j * 2 + 1, 1)
                    step(j * 2 + 2, 0)
                step(NG - 3, 1)
                relu(NG - 2, 0)
                relu(NG - 1, 1)

            @block.vector
            def _(dve):
                nc.vector.memset(nodes[:, :, :], 0.0).then_inc(taken, 1)
                nc.vector.memset(deg[:, :, :], 0.0).then_inc(taken_x, 1)
                nc.vector.tensor_copy(ones2[:, :], ones[0:TP, 0:2])
                dve.wait_ge(wb_high, 1)
                nc.vector.tensor_tensor(wb_lo[:, :], wb_raw[:, :], wb_hi[:, :], ALU.subtract).then_inc(wb_low, 1)
                dve.wait_ge(iota_made, 1)

                def one_hot(dst_hot, g, of, first_node, signal):
                    for t in range(TG):
                        d = (of[:, g * TG + t:g * TG + t + 1] if isinstance(g, int)
                             else of[:, bass.ds(g * TG + t, 1)])
                        last = nc.vector.tensor_scalar(dst_hot[:, t, :], first_node, d, None, ALU.is_equal)
                    last.then_inc(signal, 1)

                def edge_low(g, p):
                    dve.wait_ge(e_high, g + 1)
                    if not isinstance(g, int) or g >= 2:
                        dve.wait_ge(pre_ready, g * TG - TG)
                    nc.vector.tensor_tensor(e_lo[p][:, 0:EH], e_raw[p][:, 0:EH], e_hi[p][:, 0:EH],
                                            ALU.subtract).then_inc(e_low_first, 1)

                def add(g, p, t):
                    dve.wait_ge(pre_ready, g * TG + (t + 1))
                    dve.wait_ge(gathered[p][t], (g - p) * 8 + 16)
                    if not isinstance(g, int) or g >= 1:
                        dve.wait_ge(relued, g * TG + (t + 1 - TG))
                        if t in TWO_PASS:
                            dve.wait_ge(lowered, g * NW + (TWO_PASS.index(t) + 1 - NW))
                    nc.vector.tensor_tensor(pre_sum[t][:, :], PRE[t][0:TP, :], gath[p][t][:, :],
                                            ALU.add).then_inc(added, 1)

                def low_part(g, p, t):
                    if t in TWO_PASS:
                        dve.wait_ge(relued, g * TG + (t + 1))
                        nc.vector.scalar_tensor_tensor(m_lo[p][t][:, :], pre_sum[t][:, :], 0.0, m_hi[p][t][:, :],
                                                       ALU.max, ALU.subtract).then_inc(lowered, 1)

                def add_group(g, p):
                    for t in range(TG):
                        add(g, p, t)
                        if t == 1 and not (isinstance(g, int) and g + 1 >= NG):
                            edge_low(g + 1, 1 - p)
                        if t >= 2:
                            low_part(g, p, t - 2)
                    low_part(g, p, TG - 2)
                    low_part(g, p, TG - 1)

                def accumulate(win_of, sums, degs, signal):
                    rows_w = rows[:, :, :].rearrange("p t f -> p (t f)")[:, bass.ds(win_of * ROW, D)]
                    deg_w = deg[:, :, :].rearrange("p t a -> p (t a)")[:, bass.ds(win_of * 2, 2)]
                    nc.vector.tensor_tensor(deg_w, degs, deg_w, ALU.add)
                    nc.vector.tensor_tensor(rows_w, sums[0:TP, :], rows_w, ALU.add).then_inc(signal, 1)

                def take_first(g, p, w):
                    dve.wait_ge(summed, g + 1)
                    dve.wait_ge(taken, g + 1)
                    dve.wait_ge(taken_x, further_start(w) + 1)
                    accumulate(a_window(w & 15), SUM[p], DEG[p][0:TP, 0:2], taken)

                def hot_further(g, x, window):
                    dve.wait_ge(taken_x, x + 1)
                    one_hot(hot_x, g, dst_f, iota_n[:, bass.ds(window * TP, TP + 1)], hot_x_made)

                def take_further(g, p, x, window):
                    dve.wait_ge(taken, g + 2)
                    dve.wait_ge(summed_x, x + 1)
                    accumulate(window, SUM[1 - p], DEG[1 - p][0:TP, 0:2], taken_x)

                def take(g, p):
                    w = dve.value_load(word_at(g), min_val=0, max_val=SCALE_X0 * NG * NT)
                    with dve.If(has_further(w)):
                        hot_further(g, further_start(w), a_window((w & 15) + 1))
                        take_first(g, p, w)
                        take_further(g, p, further_start(w), a_window((w & 15) + 1))
                        rest(dve, w, lambda x, window: (hot_further(g, x, window), take_further(g, p, x, window)))
                    with dve.Else():
                        take_first(g, p, w)

                def step(g, p):
                    add_group(g, p)
                    take(g - 1, 1 - p)

                edge_low(0, 0)
                add_group(0, 0)
                with dve.Fori(0, (NG - 2) // 2) as j:
                    step(j * 2 + 1, 1)
                    step(j * 2 + 2, 0)
                step(NG - 1, 1)
                take(NG - 1, 1)

            @block.tensor
            def _(pe):
                pe.wait_ge(wb_low, 1)

                def pre(g, p):
                    pe.wait_ge(e_low, g + 1)
                    pe.wait_ge(e_low_first, g + 1)
                    for t in range(TG):
                        if not isinstance(g, int) or g >= 1:
                            pe.wait_ge(added, g * TG + (t + 1 - TG))
                        c = slice(t * TP, (t + 1) * TP)
                        product3(PRE[t][0:TP, :], (e_hi[p][:, c], e_lo[p][:, c]), (wb_hi[:, :], wb_lo[:, :]),
                                 True, True).then_inc(pre_ready, 1)

                def window_sum(h, p, sums, degs, signal):
                    for t in range(TG):
                        if t in TWO_PASS:
                            nc.tensor.matmul(sums[0:TP, :], h[:, t, 0:TP], m_hi[p][t][:, :],
                                             start=(t == 0), stop=False)
                            nc.tensor.matmul(sums[0:TP, :], h[:, t, 0:TP], m_lo[p][t][:, :],
                                             start=False, stop=(t == TG - 1))
                        else:
                            nc.tensor.matmul(sums[0:TP, :], h[:, t, 0:TP].bitcast(F32), m_hi[p][t][:, :],
                                             start=(t == 0), stop=(t == TG - 1))
                    for t in range(TG):
                        last = nc.tensor.matmul(degs, h[:, t, 0:TP], ones2[:, :], start=(t == 0), stop=(t == TG - 1))
                    last.then_inc(signal, 1)

                def group_sum(g, p):
                    w = pe.value_load(word_at(g), min_val=0, max_val=SCALE_X0 * NG * NT)
                    pe.wait_ge(hot_made, g + 1)
                    pe.wait_ge(relued, g * TG + TG)
                    if NW:
                        pe.wait_ge(lowered, g * NW + NW)
                    if not isinstance(g, int) or g >= 2:
                        pe.wait_ge(taken, g)
                    if not isinstance(g, int) or g >= 1:
                        pe.wait_ge(taken_x, further_start(w) + 1)
                    window_sum(hot[p], p, SUM[p], DEG[p][0:TP, 0:2], summed)

                    def further_sum(x):
                        pe.wait_ge(taken, g + 1)
                        pe.wait_ge(taken_x, x + 1)
                        pe.wait_ge(hot_x_made, x + 1)
                        window_sum(hot_x, p, SUM[1 - p], DEG[1 - p][0:TP, 0:2], summed_x)

                    with pe.If(has_further(w)):
                        further_sum(further_start(w))
                        rest(pe, w, lambda x, window: further_sum(x))

                pre(0, 0)
                for g in range(2):
                    pre(g + 1, 1 - g)
                    group_sum(g, g)
                with pe.Fori(0, (NG - 4) // 2) as j:
                    for p in range(2):
                        pre(j * 2 + (p + 3), 1 - p)
                        group_sum(j * 2 + (p + 2), p)
                pre(NG - 1, 1)
                group_sum(NG - 2, 0)
                group_sum(NG - 1, 1)
        s3.close()

        s4 = ExitStack()
        tr_hi = sb("tr_hi", [128, KC, N], F32R, s4)
        tr_lo = sb("tr_lo", [128, KC, N], F32R, s4)
        ag_hi = sb("ag_hi", [128, KC, N], F32R, s4)
        ag_lo = sb("ag_lo", [128, KC, N], F32R, s4)
        s4a = ExitStack()
        w2_raw = sb("w2_raw", [128, KC, D], F32, s4a)
        w2_hi = sb("w2_hi", [128, KC, D], F32R, s4a)
        w2_lo = sb("w2_lo", [128, KC, D], F32R, s4a)
        b2_row = sb("b2_row", [1, D], F32, s4a)
        deg_row = sb("deg_row", [1, N], F32, s4a)
        w2_loaded, b2_loaded, w2_high, w2_low, sums_turned, sums_high, sums_low, deg_turned, deg_taken = (
            sem(n) for n in ("w2_loaded", "b2_loaded", "w2_high", "w2_low", "sums_turned", "sums_high", "sums_low",
                             "deg_turned", "deg_taken"))
        agg_ready, agg_high, agg_low = sem("agg_ready"), sem("agg_high"), sem("agg_low")

        with nc.Block() as block:
            @block.sync
            def _(sp):
                sp.dma_start(w2_raw[:, :, :], w2.rearrange("(k p) f -> p k f", p=128)).then_inc(w2_loaded, 16)
                sp.dma_start(b2_row[:, :], b2.unsqueeze(0)).then_inc(b2_loaded, 16)

            def bank_nodes(t):
                return bank[t % 4][:, 0:KC * TP].rearrange("p (k n) -> p k n", k=KC)

            @block.scalar
            def _(act):
                for t in range(NT):
                    act.wait_ge(sums_turned, t + 1)
                    nc.scalar.copy(tr_hi[:, :, t * TP:(t + 1) * TP], bank_nodes(t)).then_inc(sums_high, 1)
                    if t == 1:
                        act.wait_ge(w2_loaded, 16)
                        nc.scalar.copy(w2_hi[:, :, :], w2_raw[:, :, :]).then_inc(w2_high, 1)
                for j, (c, s) in enumerate(QJ):
                    a, n = SLICES[s]
                    act.wait_ge(agg_ready, j + 1)
                    nc.scalar.copy(ag_hi[:, c, a:a + n], bank[j % 4][:, 0:n]).then_inc(agg_high, 1)

            @block.vector
            def _(dve):
                for t in range(NT):
                    dve.wait_ge(sums_high, t + 1)
                    s = slice(t * TP, (t + 1) * TP)
                    nc.vector.tensor_tensor(tr_lo[:, :, s], bank_nodes(t), tr_hi[:, :, s],
                                            ALU.subtract).then_inc(sums_low, 1)
                    if t == 2:
                        dve.wait_ge(w2_high, 1)
                        nc.vector.tensor_tensor(w2_lo[:, :, :], w2_raw[:, :, :], w2_hi[:, :, :],
                                                ALU.subtract).then_inc(w2_low, 1)
                for i in range(3):
                    dve.wait_ge(deg_turned, i + 1)
                    n = min(4, NT - 4 * i) * TP
                    nc.vector.tensor_copy(deg_row[:, 4 * i * TP:4 * i * TP + n],
                                          bank[4 + i][0:1, 0:n]).then_inc(deg_taken, 1)
                for j, (c, s) in enumerate(QJ):
                    a, n = SLICES[s]
                    dve.wait_ge(agg_high, j + 1)
                    nc.vector.tensor_tensor(ag_lo[:, c, a:a + n], bank[j % 4][:, 0:n], ag_hi[:, c, a:a + n],
                                            ALU.subtract).then_inc(agg_low, 1)

            @block.tensor
            def _(pe):
                for t in range(NT):
                    if t >= 4:
                        pe.wait_ge(sums_low, t - 3)
                    for k in range(KC):
                        last = nc.tensor.transpose(bank[t % 4][:, k * TP:(k + 1) * TP],
                                                   nodes[:, t, k * 128:(k + 1) * 128], ident[0:TP, 0:TP])
                    last.then_inc(sums_turned, 1)
                for t in range(NT):
                    last = nc.tensor.transpose(bank[4 + t // 4][0:1, (t % 4) * TP:(t % 4 + 1) * TP],
                                               deg[:, t, 0:1], ident[0:TP, 0:TP])
                    if t % 4 == 3 or t == NT - 1:
                        last.then_inc(deg_turned, 1)
                pe.wait_ge(w2_low, 1)
                pe.wait_ge(sums_low, NT)
                pe.wait_ge(deg_taken, 3)
                pe.wait_ge(b2_loaded, 16)
                for j, (c, s) in enumerate(QJ):
                    a, n = SLICES[s]
                    if j >= 4:
                        pe.wait_ge(agg_low, j - 3)
                    cc = slice(c * 128, (c + 1) * 128)
                    nc.tensor.matmul(bank[j % 4][:, 0:n], b2_row[0:1, cc], deg_row[0:1, a:a + n],
                                     start=True, stop=False)
                    for k in range(KC):
                        last = product3(bank[j % 4][:, 0:n], (w2_hi[:, k, cc], w2_lo[:, k, cc]),
                                        (tr_hi[:, k, a:a + n], tr_lo[:, k, a:a + n]), False, k == KC - 1)
                    last.then_inc(agg_ready, 1)
        s4a.close()

        s4b = ExitStack()
        RING = 4
        g_raw = [sb(f"g_raw{i}", [128, KC, 128], F32, s4b) for i in range(RING)]
        g_hi = [sb(f"g_hi{i}", [128, KC, 128], F32R, s4b) for i in range(RING)]
        g_lo = [sb(f"g_lo{i}", [128, KC, 128], F32R, s4b) for i in range(RING)]
        gate_r = [sb(f"gate_r{i}", [128, N], F32, s4b) for i in range(2)]
        gate_z = [sb(f"gate_z{i}", [128, N], F32, s4b) for i in range(2)]
        wide = SLICES[0][1]
        cand = [sb(f"cand{i}", [128, wide], F32, s4b) for i in range(2)]
        new = [sb(f"new{i}", [128, wide], F32, s4b) for i in range(2)]
        mixd = [sb(f"mixd{i}", [128, wide], F32, s4b) for i in range(2)]
        NP = 6 * KC
        JB = 6
        FILLS = [(0, 4), (4, 4), (8, 2)]
        LOGITS = bank[7]
        wg_loaded, rows_turned, rows_copied, logits_ready, stats5, std5 = (sem(n) for n in (
            "wg_loaded", "rows_turned", "rows_copied", "logits_ready", "stats5", "std5"))
        fill_bank = lambda c, i: bank[6] if c < KC - 1 or i == 0 else bank[i - 1]
        g_loaded = [sem(f"g_loaded{i}") for i in range(RING)]
        g_high, g_low, gate_done, gate_ready, gate_taken, xn_high, xn_low, cand_made, new_made, x1_made = (
            sem(n) for n in ("g_high", "g_low", "gate_done", "gate_ready", "gate_taken", "xn_high", "xn_low",
                             "cand_made", "new_made", "x1_made"))

        with nc.Block() as block:
            @block.sync
            def _(sp):
                sp.dma_start(wg_sb[:, :, :], wg.rearrange("(k p) e -> p k e", p=128)).then_inc(wg_loaded, 16)
                for q in range(NP):
                    if q >= RING:
                        sp.wait_ge(g_low, q - RING + 1)
                    sp.dma_start(g_raw[q % RING][:, :, :], gate_blocks[q]).then_inc(g_loaded[q % RING], 16)

            @block.scalar
            def _(act):
                def high(*qs):
                    for q in qs:
                        if q >= NP:
                            return
                        act.wait_ge(g_loaded[q % RING], 16 * (q // RING + 1))
                        if q >= RING:
                            act.wait_ge(gate_done, (q - RING) // 2 + 1)
                        nc.scalar.copy(g_hi[q % RING][:, :, :], g_raw[q % RING][:, :, :]).then_inc(g_high, 1)

                def copy_rows(c, i):
                    t0, n = FILLS[i]
                    act.wait_ge(rows_turned, 3 * c + i + 1)
                    nc.scalar.copy(nodes[:, t0:t0 + n, c * 128:(c + 1) * 128],
                                   fill_bank(c, i)[0:TP, 0:n * 128].rearrange("p (t f) -> p t f", f=128)
                                   ).then_inc(rows_copied, 1)

                high(0, 1)
                for c in range(KC):
                    nc.scalar.copy(tr_hi[:, c, :], xn[:, c, :]).then_inc(xn_high, 1)
                high(2, 3)
                for c in range(KC):
                    for gate, dst in ((0, gate_r[c % 2]), (1, gate_z[c % 2])):
                        for s, (a, n) in enumerate(SLICES):
                            job = 12 * c + 3 * gate + s
                            act.wait_ge(gate_ready, job + 1)
                            if c >= 2:
                                act.wait_ge(x1_made, 3 * (c - 1))
                            nc.scalar.activation(dst[:, a:a + n], bank[job % JB][:, 0:n], ACT.Sigmoid,
                                                 bias=brz[:, gate, c:c + 1]).then_inc(gate_taken, 1)
                            if gate == 1 and c:
                                copy_rows(c - 1, s)
                        high(6 * c + 4 + 2 * gate, 6 * c + 5 + 2 * gate)
                    for s, (a, n) in enumerate(SLICES):
                        i = 3 * c + s
                        act.wait_ge(cand_made, i + 1)
                        if i >= 2:
                            act.wait_ge(x1_made, i - 1)
                        nc.scalar.activation(new[i % 2][:, 0:n], cand[i % 2][:, 0:n], ACT.Tanh).then_inc(new_made, 1)
                    high(6 * c + 8, 6 * c + 9)
                for i in range(3):
                    copy_rows(KC - 1, i)
                act.wait_ge(stats5, 1)
                nc.scalar.activation(rstd[:, :], mv[:, :, 1], ACT.Sqrt, bias=epsc[0:TP, :]).then_inc(std5, 1)

            @block.vector
            def _(dve):
                L = dve_chain.link

                def low(*qs):
                    for q in qs:
                        if q < NP:
                            dve.wait_ge(g_high, q + 1)
                            nc.vector.tensor_tensor(g_lo[q % RING][:, :, :], g_raw[q % RING][:, :, :],
                                                    g_hi[q % RING][:, :, :], ALU.subtract).then_inc(g_low, 1)

                def candidate(c, s):
                    a, n = SLICES[s]
                    i, job = 3 * c + s, 12 * c + 6 + 2 * s
                    dve.wait_ge(gate_ready, job + 2)
                    dve.wait_ge(gate_taken, 6 * c + 6)
                    L(dve, nc.vector.scalar_tensor_tensor(
                        cand[i % 2][:, 0:n], bank[(job + 1) % JB][:, 0:n], COL["bhn"][:, c:c + 1],
                        gate_r[c % 2][:, a:a + n], ALU.add, ALU.mult))
                    nc.vector.scalar_tensor_tensor(
                        cand[i % 2][:, 0:n], bank[job % JB][:, 0:n], COL["bin"][:, c:c + 1],
                        cand[i % 2][:, 0:n], ALU.add, ALU.add).then_inc(cand_made, 1)

                def combine(c, s):
                    a, n = SLICES[s]
                    i = 3 * c + s
                    dve.wait_ge(new_made, i + 1)
                    m, nw = mixd[i % 2][:, 0:n], new[i % 2][:, 0:n]
                    L(dve, nc.vector.tensor_tensor(m, xn[:, c, a:a + n], nw, ALU.subtract))
                    L(dve, nc.vector.tensor_tensor(m, m, gate_z[c % 2][:, a:a + n], ALU.mult))
                    L(dve, nc.vector.tensor_tensor(m, m, nw, ALU.add))
                    nc.vector.scalar_tensor_tensor(base[:, c, a:a + n], m, gscale[:, c:c + 1], base[:, c, a:a + n],
                                                   ALU.mult, ALU.add).then_inc(x1_made, 1)

                def chunk_stats(c, i):
                    dve.wait_ge(rows_copied, 3 * c + i + 1)
                    for t in range(FILLS[i][0], sum(FILLS[i])):
                        ins = nc.vector.bn_stats(stat[:, t, c, :], nodes[:, t, c * 128:(c + 1) * 128])
                    dve_chain.link(dve, ins)

                low(0, 1)
                for c in range(KC):
                    dve.wait_ge(xn_high, c + 1)
                    nc.vector.tensor_tensor(tr_lo[:, c, :], xn[:, c, :], tr_hi[:, c, :], ALU.subtract).then_inc(xn_low, 1)
                low(2, 3)
                for c in range(KC):
                    low(6 * c + 4, 6 * c + 5)
                    low(6 * c + 6, 6 * c + 7)
                    if c:
                        for i in range(3):
                            chunk_stats(c - 1, i)
                    candidate(c, 0)
                    candidate(c, 1)
                    combine(c, 0)
                    candidate(c, 2)
                    combine(c, 1)
                    combine(c, 2)
                    low(6 * c + 8, 6 * c + 9)
                for i in range(3):
                    chunk_stats(KC - 1, i)
                for t in range(NT):
                    ins = nc.vector.bn_aggr(mv[:, t, :], stat[:, t, :, :])
                ins.then_inc(stats5, 1)
                dve.wait_ge(stats5, 1)
                L(dve, nc.vector.tensor_scalar(tmp_t[:, :], mv[:, :, 1], EPS, None, ALU.add))
                dve.wait_ge(std5, 1)
                newton_rsqrt(dve, rstd[:, :], tmp_t[:, :], tmp_s[:, :], stat[:, :, 0, 0])
                nc.vector.tensor_copy(rows[:, :, D], rstd[:, :])
                nc.vector.scalar_tensor_tensor(rows[:, :, D + 1], mv[:, :, 0], -1.0, rstd[:, :], ALU.mult, ALU.mult)

            @block.tensor
            def _(pe):
                pe.wait_ge(wg_loaded, 16)
                for k in range(KC):
                    nc.tensor.matmul(LOGITS[0:TP, NT * NX:(NT + 1) * NX], ones[:, 0:TP], wg_sb[:, k, :],
                                     start=(k == 0), stop=False)

                def free(job):
                    job -= JB
                    if job >= 0:
                        c, i = divmod(job, 12)
                        if i < 6:
                            pe.wait_ge(gate_taken, 6 * c + i + 1)
                        else:
                            pe.wait_ge(cand_made, 3 * c + (i - 6) // 2 + 1)

                def operand(q, k):
                    return g_hi[q % RING][:, k, :], g_lo[q % RING][:, k, :]

                def turn_rows(c, i):
                    t0, n = FILLS[i]
                    pe.wait_ge(x1_made, 3 * c + (2 if i == 0 else 3))
                    if i or c:
                        pe.wait_ge(rows_copied, 3 * c + i if c < KC - 1 or i == 0 else 3 * c)
                    for t in range(t0, t0 + n):
                        last = nc.tensor.transpose(fill_bank(c, i)[0:TP, (t - t0) * 128:(t - t0 + 1) * 128],
                                                   base[:, c, t * TP:(t + 1) * TP], ident[:, :])
                    last.then_inc(rows_turned, 1)
                    for t in range(t0, t0 + n):
                        last = nc.tensor.matmul(LOGITS[0:TP, t * NX:(t + 1) * NX], base[:, c, t * TP:(t + 1) * TP],
                                                wg_sb[:, c, :], start=False, stop=(c == KC - 1 and t == NT - 1))
                    if c == KC - 1 and i == 2:
                        last.then_inc(logits_ready, 1)

                for c in range(KC):
                    for gate in range(2):
                        q = 6 * c + 2 * gate
                        pe.wait_ge(g_low, q + 2)
                        for s, (a, n) in enumerate(SLICES):
                            job = 12 * c + 3 * gate + s
                            free(job)
                            for k in range(KC):
                                product3(bank[job % JB][:, 0:n], operand(q, k),
                                         (ag_hi[:, k, a:a + n], ag_lo[:, k, a:a + n]), k == 0, False)
                            if job == 0:
                                pe.wait_ge(xn_low, KC)
                            for k in range(KC):
                                last = product3(bank[job % JB][:, 0:n], operand(q + 1, k),
                                                (tr_hi[:, k, a:a + n], tr_lo[:, k, a:a + n]), False, k == KC - 1)
                            last.then_inc(gate_ready, 1)
                            if gate == 1 and c:
                                turn_rows(c - 1, s)
                            if s == len(SLICES) - 1:
                                pe.nop().then_inc(gate_done, 1)
                    q = 6 * c + 4
                    pe.wait_ge(g_low, q + 2)
                    for s, (a, n) in enumerate(SLICES):
                        for part, (hi, lo) in enumerate(((ag_hi, ag_lo), (tr_hi, tr_lo))):
                            job = 12 * c + 6 + 2 * s + part
                            free(job)
                            for k in range(KC):
                                last = product3(bank[job % JB][:, 0:n], operand(q + part, k),
                                                (hi[:, k, a:a + n], lo[:, k, a:a + n]), k == 0, k == KC - 1)
                            last.then_inc(gate_ready, 1)
                    pe.nop().then_inc(gate_done, 1)
                for i in range(3):
                    turn_rows(KC - 1, i)
        s4b.close()
        s4.close()

        s5 = ExitStack()
        w1_all = sb("w1_all", [128, NX, KC, HX], F32, s5)
        w2_all = sb("w2_all", [128, NX, HX // 128, D], F32, s5)
        bias_all = sb("bias_all", [TS, NX * (HX + D)], F32, s5)
        b1_all, b2_all = bias_all[:, 0:NX * HX], bias_all[:, NX * HX:]
        bg_sb = sb("bg_sb", [TP, NX], F32, s5)
        before = sb("before", [128, 128], F32, s5)
        R3 = lambda n: sb(n, [TP, NT, NX], F32, s5)
        logit, prob, is_max, hot_e, place = R3("logit"), R3("prob"), R3("is_max"), R3("hot_e"), R3("place")
        e_less = sb("e_less", [TP, NX], F32, s5)
        best = sb("best", [TP, NT], F32, s5)
        score = sb("score", [TP, NT], F32, s5)
        slot_f = sb("slot_f", [TP, NT], F32, s5)
        slot = sb("slot", [TP, NT], I32, s5)
        held = sb("held", [TP, NX], F32, s5)
        MT = -(-N // TS)
        steps = sb("steps", [TP, NX, MT], F32, s5)
        over = sb("over", [TP, NX, MT], F32, s5)
        upto = sb("upto", [TP, NX, NX], F32, s5)
        parts = sb("parts", [TP, NX, NX], F32, s5)
        tiles = sb("tiles", [TP, NX], F32, s5)
        cum = sb("cum", [TP, NX], F32, s5)
        first = sb("first", [TP, NX], F32, s5)
        tile_no = sb("tile_no", [1, NST, NX], F32, s5)
        past = sb("past", [1, NST, NX], F32, s5)
        tile_ef = sb("tile_ef", [1, NST], F32, s5)
        tile_e = sb("tile_e", [1, NST], I32, s5)
        FR = 5
        row_in = [sb(f"row_in{i}", [TS, ROW], F32, s5) for i in range(FR)]
        node_i = [sb(f"node_i{i}", [TS, 1], I32, s5) for i in range(FR)]
        spare = sb("spare", [TS, NST], F32, s5)
        is_spare = [sb(f"is_spare{i}", [TS, 1], F32, s5) for i in range(2)]
        y = [sb(f"y{i}", [TS, D], F32, s5) for i in range(2)]
        yt = [sb(f"yt{i}", [128, KC, TS], F32, s5) for i in range(2)]
        pre_hid = [sb(f"pre_hid{i}", [TS, HX], F32, s5) for i in range(2)]
        hid = [sb(f"hid{i}", [128, HX // 128, TS], F32, s5) for i in range(2)]
        fo = [sb(f"fo{i}", [TS, D], F32, s5) for i in range(2)]
        bg_loaded, experts_loaded, consts5, shifted, exp_made, held_made, counts_ready, slots_made, scattered = (
            sem(n) for n in ("bg_loaded", "experts_loaded", "consts5", "shifted", "exp_made", "held_made",
                             "counts_ready", "slots_made", "scattered"))
        row_loaded = [sem(f"row_loaded{i}") for i in range(FR)]
        y_made, y_turned, yt_made, pre_ready5, pre_made, hid_turned, hid_made, f_ready, f_made = (sem(n) for n in (
            "y_made", "y_turned", "yt_made", "pre_ready5", "pre_made", "hid_turned", "hid_made", "f_ready", "f_made"))
        tiles_made, bias_in, bias_spread, bias_made = (sem(n) for n in (
            "tiles_made", "bias_in", "bias_spread", "bias_made"))
        NB = NX * (HX + D) // 512
        out_stored = [sem(f"out_stored{i}") for i in range(2)]

        def an_expert(eng, i):
            return eng.value_load(tile_e[0:1, i:i + 1], min_val=0, max_val=NX - 1)

        with nc.Block() as block:
            @block.sync
            def _(sp):
                sp.dma_start(bg_sb[:, :], bg.unsqueeze(0).to_broadcast([TP, NX])).then_inc(bg_loaded, 16)
                sp.dma_start(b1_all[0:1, :], be1.rearrange("e h -> (e h)").unsqueeze(0)).then_inc(bias_in, 16)
                sp.dma_start(b2_all[0:1, :], be2.rearrange("e h -> (e h)").unsqueeze(0)).then_inc(bias_in, 16)
                for e in range(NX):
                    sp.dma_start(w1_all[:, e, :, :], we1[e].rearrange("(k p) h -> p k h", p=128)).then_inc(experts_loaded, 16)
                    sp.dma_start(w2_all[:, e, :, :], we2[e].rearrange("(k p) h -> p k h", p=128)).then_inc(experts_loaded, 16)
                sp.wait_ge(scattered, 16 * NT)
                for i in range(NST):
                    if i >= FR:
                        sp.wait_ge(f_made, i - FR + 1)
                    sp.dma_start(row_in[i % FR][:, :], slot_in[i * TS:(i + 1) * TS, :]).then_inc(row_loaded[i % FR], 16)
                sp.wait_ge(out_stored[0], 16 * ((NST + 1) // 2))
                sp.wait_ge(out_stored[1], 16 * (NST // 2))

            @block.gpsimd
            def _(pool):
                exact = dict(allow_small_or_imprecise_dtypes=True)
                nc.gpsimd.iota(e_less[:, :], pattern=[[1, NX]], base=-NX, channel_multiplier=0, **exact)
                nc.gpsimd.iota(tile_no[:, :, :], pattern=[[1, NST], [0, NX]], base=0, channel_multiplier=0, **exact)
                nc.gpsimd.iota(steps[:, :, :], pattern=[[0, NX], [TS, MT]], base=0, channel_multiplier=0, **exact)
                nc.gpsimd.iota(score[:, :], pattern=[[TP, NT]], base=1, channel_multiplier=1, **exact)
                nc.gpsimd.iota(spare[:, :], pattern=[[TS, NST]], base=N + 1, channel_multiplier=1, **exact)
                pool_chain.link(pool, nc.gpsimd.memset(place[:, 0, :], 0.0))
                nc.gpsimd.tensor_copy(rows[:, :, D + 3], score[:, :])
                nc.gpsimd.affine_select(out=upto[:, :, :], in_=ones[0:TP, 0:NX * NX].rearrange("p (a b) -> p a b", a=NX),
                                        compare_op=ALU.is_ge, fill=0.0, base=0, pattern=[[1, NX], [-1, NX]],
                                        channel_multiplier=0)
                nc.gpsimd.affine_select(out=before[:, :], in_=ones[:, :], compare_op=ALU.is_gt, fill=0.0,
                                        base=0, pattern=[[1, 128]], channel_multiplier=-1).then_inc(consts5, 1)
                pool.wait_ge(slots_made, 1)
                pool.wait_ge(table_zeroed, 16 * NST)
                for t in range(NT):
                    pool.indirect_dma_start(out=slot_in, out_offset=bass.IndirectOffsetOnAxis(ap=slot[:, t:t + 1], axis=0),
                                            in_=rows[:, t, :], in_offset=None).then_inc(scattered, 16)
                for i in range(NST):
                    pool.wait_ge(f_made, i + 1)
                    pool.indirect_dma_start(out=out, out_offset=bass.IndirectOffsetOnAxis(ap=node_i[i % FR][:, 0:1], axis=0),
                                            in_=fo[i % 2][:, :], in_offset=None).then_inc(out_stored[i % 2], 16)

            @block.scalar
            def _(act):
                act.wait_ge(shifted, 1)
                nc.scalar.activation(prob[:, :, :], logit[:, :, :], ACT.Exp).then_inc(exp_made, 1)

                for i in range(NB):
                    act.wait_ge(bias_spread, i + 1)
                    nc.scalar.copy(bias_all[:, i * 512:(i + 1) * 512], bank[i % 2][0:TS, :]).then_inc(bias_made, 1)

                def norm(i):
                    act.wait_ge(row_loaded[i % FR], 16 * (i // FR + 1))
                    if i >= 2:
                        act.wait_ge(y_turned, i - 1)
                    r = row_in[i % FR]
                    nc.scalar.activation(y[i % 2][:, :], r[:, 0:D], ACT.Identity, scale=r[:, D:D + 1],
                                         bias=r[:, D + 1:D + 2]).then_inc(y_made, 1)

                def turned(i):
                    act.wait_ge(y_turned, i + 1)
                    if i >= 2:
                        act.wait_ge(pre_ready5, i - 1)
                    nc.scalar.copy(yt[i % 2][:, :, :].rearrange("p k n -> p (k n)"), bank[i % 2][:, :]).then_inc(yt_made, 1)

                norm(0)
                norm(1)
                turned(0)
                for i in range(NST):
                    if i + 1 < NST:
                        turned(i + 1)
                    if i + 2 < NST:
                        norm(i + 2)
                    act.wait_ge(hid_turned, i + 1)
                    if i >= 2:
                        act.wait_ge(f_ready, i - 1)
                    nc.scalar.activation(hid[i % 2][:, :, :].rearrange("p k n -> p (k n)"), bank[6 + i % 2][:, 0:HX],
                                         ACT.Relu).then_inc(hid_made, 1)

            @block.vector
            def _(dve):
                L = dve_chain.link

                def over_e(ap):
                    return ap.unsqueeze(2).to_broadcast([TP, NT, NX])

                def over_t(ap):
                    return ap.unsqueeze(1).to_broadcast([TP, NT, NX])

                TT = nc.vector.tensor_tensor
                L(dve, TT(logit[:, :, :], over_e(mv[:, :, 0]), over_t(LOGITS[0:TP, NT * NX:(NT + 1) * NX]), ALU.mult))
                L(dve, TT(logit[:, :, :], LOGITS[0:TP, 0:NT * NX].rearrange("p (t e) -> p t e", e=NX), logit[:, :, :],
                          ALU.subtract))
                L(dve, TT(logit[:, :, :], logit[:, :, :], over_e(rstd[:, :]), ALU.mult))
                dve.wait_ge(bg_loaded, 16)
                L(dve, TT(logit[:, :, :], logit[:, :, :], over_t(bg_sb[:, :]), ALU.add))
                L(dve, nc.vector.tensor_reduce(best[:, :], logit[:, :, :], AX_X, ALU.max))
                TT(logit[:, :, :], logit[:, :, :], over_e(best[:, :]), ALU.subtract).then_inc(shifted, 1)
                dve.wait_ge(shifted, 1)
                dve.wait_ge(consts5, 1)
                L(dve, nc.vector.scalar_tensor_tensor(is_max[:, :, :], logit[:, :, :], 0.0, over_t(e_less[:, :]),
                                                      ALU.is_equal, ALU.mult))
                L(dve, nc.vector.tensor_reduce(best[:, :], is_max[:, :, :], AX_X, ALU.min))
                L(dve, TT(hot_e[:, :, :], over_t(e_less[:, :]), over_e(best[:, :]), ALU.is_equal))
                nc.vector.tensor_reduce(held[:, :], hot_e[:, :, :].rearrange("p t e -> p e t"), AX_X,
                                        ALU.add).then_inc(held_made, 1)
                for t in range(1, NT):
                    L(dve, TT(place[:, t, :], place[:, t - 1, :], hot_e[:, t - 1, :], ALU.add))
                dve.wait_ge(counts_ready, 1)
                L(dve, TT(over[:, :, :], bank[6][0:TP, 0:NX].unsqueeze(2).to_broadcast([TP, NX, MT]), steps[:, :, :],
                          ALU.is_gt))
                L(dve, nc.vector.tensor_reduce(tiles[:, :], over[:, :, :], AX_X, ALU.add))
                L(dve, TT(parts[:, :, :], tiles[:, :].unsqueeze(1).to_broadcast([TP, NX, NX]), upto[:, :, :], ALU.mult))
                L(dve, nc.vector.tensor_reduce(cum[:, :], parts[:, :, :], AX_X, ALU.add))
                L(dve, TT(first[:, :], cum[:, :], tiles[:, :], ALU.subtract))
                L(dve, nc.vector.scalar_tensor_tensor(first[:, :], first[:, :], float(TS), bank[6][0:TP, NX:2 * NX],
                                                      ALU.mult, ALU.add))
                L(dve, TT(place[:, :, :], place[:, :, :], over_t(first[:, :]), ALU.add))
                L(dve, TT(place[:, :, :], place[:, :, :], hot_e[:, :, :], ALU.mult))
                L(dve, nc.vector.tensor_reduce(slot_f[:, :], place[:, :, :], AX_X, ALU.add))
                dve.wait_ge(exp_made, 1)
                L(dve, nc.vector.tensor_reduce(score[:, :], prob[:, :, :], AX_X, ALU.add))
                nc.vector.reciprocal(rows[:, :, D + 2], score[:, :])
                nc.vector.tensor_copy(slot[:, :], slot_f[:, :]).then_inc(slots_made, 1)
                L(dve, TT(past[:, :, :], tile_no[:, :, :], cum[0:1, :].unsqueeze(1).to_broadcast([1, NST, NX]), ALU.is_ge))
                L(dve, nc.vector.tensor_reduce(tile_ef[:, :], past[:, :, :], AX_X, ALU.add))
                nc.vector.tensor_scalar(tile_e[:, :], tile_ef[:, :], float(NX - 1), None, ALU.min).then_inc(tiles_made, 1)
                dve.wait_ge(tiles_made, 1)
                dve.wait_ge(bias_made, NB)

                def result(i, e):
                    r = row_in[i % FR]
                    dve.wait_ge(f_ready, i + 1)
                    if i >= 2:
                        dve.wait_ge(out_stored[i % 2], 16 * (i // 2))
                    L(dve, TT(fo[i % 2][:, :], bank[4 + i % 2][0:TS, :], b2_all[:, bass.ds(e * D, D)], ALU.add))
                    nc.vector.scalar_tensor_tensor(fo[i % 2][:, :], fo[i % 2][:, :], r[:, D + 2:D + 3], r[:, 0:D],
                                                   ALU.mult, ALU.add).then_inc(f_made, 1)

                e_last = None
                for i in range(NST):
                    e = an_expert(dve, i)
                    dve.wait_ge(row_loaded[i % FR], 16 * (i // FR + 1))
                    if i >= FR:
                        dve.wait_ge(out_stored[(i - FR) % 2], 16 * ((i - FR) // 2 + 1))
                    node1 = row_in[i % FR][:, D + 3:D + 4]
                    L(dve, nc.vector.scalar_tensor_tensor(is_spare[i % 2][:, :], node1, 0.0, spare[:, i:i + 1],
                                                          ALU.is_equal, ALU.mult))
                    nc.vector.scalar_tensor_tensor(node_i[i % FR][:, :], node1, -1.0, is_spare[i % 2][:, :],
                                                   ALU.add, ALU.add)
                    dve.wait_ge(pre_ready5, i + 1)
                    if i >= 2:
                        dve.wait_ge(hid_turned, i - 1)
                    TT(pre_hid[i % 2][:, :], bank[2 + i % 2][0:TS, 0:HX], b1_all[:, bass.ds(e * HX, HX)],
                       ALU.add).then_inc(pre_made, 1)
                    if i:
                        result(i - 1, e_last)
                    e_last = e
                result(NST - 1, e_last)

            @block.tensor
            def _(pe):
                pe.wait_ge(held_made, 1)
                pe.wait_ge(consts5, 1)
                nc.tensor.matmul(bank[6][0:TP, 0:NX], ones[0:TP, 0:TP], held[:, :], start=True, stop=True)
                nc.tensor.matmul(bank[6][0:TP, NX:2 * NX], before[0:TP, 0:TP], held[:, :],
                                 start=True, stop=True).then_inc(counts_ready, 1)

                def turn_y(i):
                    pe.wait_ge(y_made, i + 1)
                    if i >= 2:
                        pe.wait_ge(yt_made, i - 1)
                    for k in range(KC):
                        last = nc.tensor.transpose(bank[i % 2][:, k * TS:(k + 1) * TS],
                                                   y[i % 2][:, k * 128:(k + 1) * 128], ident[0:TS, 0:TS])
                    last.then_inc(y_turned, 1)

                def first_layer(i, e):
                    pe.wait_ge(yt_made, i + 1)
                    if i >= 2:
                        pe.wait_ge(pre_made, i - 1)
                    for k in range(KC):
                        last = nc.tensor.matmul(bank[2 + i % 2][0:TS, 0:HX], yt[i % 2][:, k, :], w1_of(e, k),
                                                start=(k == 0), stop=(k == KC - 1))
                    last.then_inc(pre_ready5, 1)

                def w1_of(e, k):
                    return w1_all[:, :, :, :].rearrange("p e k h -> p (e k h)")[:, bass.ds(e * (KC * HX) + k * HX, HX)]

                def turn_hid(i):
                    pe.wait_ge(pre_made, i + 1)
                    if i >= 2:
                        pe.wait_ge(hid_made, i - 1)
                    for m in range(HX // 128):
                        last = nc.tensor.transpose(bank[6 + i % 2][:, m * TS:(m + 1) * TS],
                                                   pre_hid[i % 2][:, m * 128:(m + 1) * 128], ident[0:TS, 0:TS])
                    last.then_inc(hid_turned, 1)

                def second_layer(i, e):
                    pe.wait_ge(hid_made, i + 1)
                    if i >= 2:
                        pe.wait_ge(f_made, i - 1)
                    w2_of = w2_all[:, :, :, :].rearrange("p e k h -> p (e k h)")
                    for m in range(HX // 128):
                        last = nc.tensor.matmul(bank[4 + i % 2][0:TS, :], hid[i % 2][:, m, :],
                                                w2_of[:, bass.ds(e * (HX // 128 * D) + m * D, D)],
                                                start=(m == 0), stop=(m == HX // 128 - 1))
                    last.then_inc(f_ready, 1)

                pe.wait_ge(bias_in, 32)
                for i in range(NB):
                    if i >= 2:
                        pe.wait_ge(bias_made, i - 1)
                    nc.tensor.matmul(bank[i % 2][0:TS, :], ones[0:1, 0:TS], bias_all[0:1, i * 512:(i + 1) * 512],
                                     start=True, stop=True).then_inc(bias_spread, 1)
                pe.wait_ge(tiles_made, 1)
                pe.wait_ge(experts_loaded, 16 * 2 * NX)
                pe.wait_ge(bias_made, NB)
                turn_y(0)
                e_last = None
                for i in range(NST):
                    e = an_expert(pe, i)
                    first_layer(i, e)
                    if i + 1 < NST:
                        turn_y(i + 1)
                    if i:
                        second_layer(i - 1, e_last)
                    turn_hid(i)
                    e_last = e
                second_layer(NST - 1, e_last)
        s5.close()


def layouts(np, a):
    blocks = lambda w: w.T.reshape(KC, 128, w.shape[0]).transpose(1, 0, 2)
    ih, hh = blocks(a["L0_gnn_W_ih"]), blocks(a["L0_gnn_W_hh"])
    column = lambda v: v.reshape(KC, 128).T
    bih, bhh = a["L0_gnn_b_ih"].reshape(3, D), a["L0_gnn_b_hh"].reshape(3, D)
    return {
        "x_nodes": a["x"],
        "x_feat": a["x"].T,
        "src_blocks": a["src"].reshape(NG, TG, TP).transpose(0, 2, 1),
        "dst_cols": a["dst"].reshape(NG * TG, TP).T,
        "dst_groups": a["dst"].reshape(NG, EG),
        "edge_blocks": a["edge_attr_128"].reshape(NG, EG, ED).transpose(0, 2, 1),
        "w1a": a["L0_gnn_W1"][:, :D].T,
        "w1b": a["L0_gnn_W1"][:, D:].T,
        "wk": a["L0_mix_Wk"], "wv": a["L0_mix_Wv"], "wq": a["L0_mix_Wq"], "wp": a["L0_mix_Wp"],
        "w2": a["L0_gnn_W2"].T,
        "gate_blocks": np.stack([w[:, :, g * D + c * 128:g * D + (c + 1) * 128]
                                 for c in range(KC) for g in range(3) for w in (ih, hh)]),
        "wg": a["L0_ffn_Wg"], "we1": a["L0_ffn_W1"], "we2": a["L0_ffn_W2"],
        "b1": a["L0_gnn_b1"], "bk": a["L0_mix_bk"], "bv": a["L0_mix_bv"], "b2": a["L0_gnn_b2"],
        "cols": np.stack([column(v) for v in (
            a["L0_mix_bq"], a["L0_mix_bp"], bih[0], bih[1], bih[2], bhh[0], bhh[1], bhh[2], a["L0_gnn_gamma"],
            a["L0_gnn_beta"], a["L0_gnn_run_mean"], a["L0_gnn_run_var"])], axis=1),
        "bg": a["L0_ffn_bg"],
        "be1": a["L0_ffn_b1"], "be2": a["L0_ffn_b2"],
    }


def kernel(**inputs):
    import numpy as _np
    import concourse.bacc as _bacc
    from concourse.bass_utils import run_bass_kernel_spmd as _run

    nc = _bacc.Bacc("TRN2", target_bir_lowering=False, num_devices=1)
    arrays, aps = {}, {}
    for name, a in layouts(_np, {k: _np.asarray(v) for k, v in inputs.items()}).items():
        a = _np.ascontiguousarray(a)
        arrays[f"in_{name}"] = a
        aps[name] = nc.dram_tensor(f"in_{name}", a.shape, mybir.dt.from_np(a.dtype), kind="ExternalInput").ap()
    aps["proj"] = nc.dram_tensor("proj_table", (N, D), F32, kind="Internal").ap()
    aps["slot_in"] = nc.dram_tensor("slot_table", (NSLOT, ROW), F32, kind="Internal").ap()
    aps["out"] = nc.dram_tensor("out_x", (N + NSLOT, D), F32, kind="ExternalOutput").ap()
    build(nc, **aps)
    r = _run(nc, [arrays], core_ids=[0])
    return r.results[0]["out_x"][:N]
```

```python
from contextlib import ExitStack

import concourse.bass as bass
from concourse import mybir

F32 = mybir.dt.float32
F32R = mybir.dt.float32r
I32 = mybir.dt.int32
ALU = mybir.AluOpType
ACT = mybir.ActivationFunctionType
AX_X = mybir.AxisListType.X

N, D, E, ED = 1250, 512, 40000, 128
TP = 125
NT = N // TP
KC = D // 128
TG = 4
EG = TP * TG
HW = 128
NG = E // EG
HEADS, DH = 8, 64
NX, HX = 8, 256
TS = 128
NST = (N + NX * (TS - 1)) // TS
NSLOT = NST * TS
ROW = D + 4
EPS = 1e-5
SLICES = [(0, 418), (418, 416), (834, 416)]
TWO_PASS = (0, 1, 2)
SCALE_X0, STARTS, ENDS = 256, 1 << 18, 1 << 19
WORD_MAX = 2 * ENDS - 1


class Counter:

    def __init__(self, sem):
        self.sem, self.n = sem, 0

    def link(self, eng, ins):
        ins.then_inc(self.sem, 1)
        self.n += 1
        eng.wait_ge(self.sem, self.n)


def rows_dma(eng, dst, src, sem):
    eng.dma_start(dst[0:112], src[0:112]).then_inc(sem, 16)
    eng.dma_start(dst[112:TP], src[112:TP]).then_inc(sem, 16)


def build(nc, x_nodes, x_feat, src_blocks, dst_cols, dst_groups, edge_blocks, w1a, w1b, wk, wv, wq, wp, w2,
          gate_blocks, wg, we1, we2, b1, bk, bv, b2, cols, bg, be1, be2, proj, slot_in, out):
    with ExitStack() as ctx:
        def sb(name, shape, dt=F32, at=ctx, side=None):
            return at.enter_context(nc.sbuf_tensor(name, shape, dt, side=side))

        def sem(name):
            return ctx.enter_context(nc.semaphore(name))

        bank = [ctx.enter_context(nc.psum_tensor(f"bank{i}", [128, 512], F32)) for i in range(8)]

        base = sb("base", [128, KC, N])
        rows = sb("rows", [TP, NT, ROW])
        nodes = rows[:, :, 0:D]
        ident = sb("ident", [128, 128])
        ones = sb("ones", [128, 128])
        bc = sb("bc", [128, 12, KC])
        COL = {n: bc[:, i, :] for i, n in enumerate(
            ["bq", "bp", "bir", "biz", "bin", "bhr", "bhz", "bhn", "gamma", "beta", "mean", "var"])}
        gscale = sb("gscale", [128, KC])
        gshift = sb("gshift", [128, KC])
        brz = sb("brz", [128, 2, KC])
        word = sb("word", [1, NG], I32)
        stat = sb("stat", [TP, NT, KC, 6])
        mv = sb("mv", [TP, NT, 2])
        rstd = sb("rstd", [TP, NT])
        tmp_s = sb("tmp_s", [TP, NT])
        tmp_t = sb("tmp_t", [TP, NT])
        tmp_c = sb("tmp_c", [128, 3, KC])
        wg_sb = sb("wg_sb", [128, KC, NX])

        dve_chain, act_chain, pool_chain = (Counter(sem(n)) for n in ("dve_chain", "act_chain", "pool_chain"))
        epsc = sb("epsc", [128, 1])

        def newton_rsqrt(dve, r, v, a, b):
            L = dve_chain.link
            L(dve, nc.vector.reciprocal(a, r))
            L(dve, nc.vector.tensor_tensor(b, a, a, ALU.mult))
            L(dve, nc.vector.tensor_tensor(b, b, v, ALU.mult))
            L(dve, nc.vector.tensor_scalar(b, b, -0.5, 1.5, ALU.mult, ALU.add))
            L(dve, nc.vector.tensor_tensor(r, a, b, ALU.mult))

        held_x = ExitStack()
        xn = sb("xn", [128, KC, N], F32, held_x, "right")
        dst_f = sb("dst_f", [TP, NG * TG], F32, held_x, "right")
        rel_neg = sb("rel_neg", [TP, NG * TG], F32, held_x, "right")
        node_no = sb("node_no", [TP, HW], F32, held_x, "right")

        held_w = ExitStack()
        w_raw = [sb(f"w_raw{i}", [128, 2, D], F32, held_w, "right") for i in range(2)]
        w_hi = [sb(f"w_hi{i}", [128, KC, D], F32R, held_w, "right") for i in range(2)]
        w_lo = [sb(f"w_lo{i}", [128, KC, D], F32R, held_w, "right") for i in range(2)]
        w_loaded = [sem(f"w_loaded{i}") for i in range(2)]
        w_high, w_low = sem("w_high"), sem("w_low")

        held_kq = ExitStack()
        kf = sb("kf", [TP, NT, D], F32, held_kq, "right")
        qf = sb("qf", [128, KC, N], F32, held_kq, "right")
        idx = [sb(f"idx{p}", [TP, TG], I32, held_kq, "right") for p in range(2)]
        gath = [[kf[:, TG * p + t, :] for t in range(TG)] for p in range(2)]

        split = ExitStack()
        xh = sb("xh", [128, KC, N], F32R, split)
        xl = sb("xl", [128, KC, N], F32R, split)

        s2 = ExitStack()
        bias_row = sb("bias_row", [TP, 3, D], F32, s2)
        row_out = [sb(f"row_out{i}", [TP, D], F32, s2) for i in range(2)]
        exp_t = [sb(f"exp_t{i}", [128, D], F32, s2) for i in range(2)]
        relu_t = [sb(f"relu_t{i}", [128, D], F32, s2) for i in range(2)]
        kv_sb = sb("kv_sb", [128, KC, 130], F32, s2)
        zeros = sb("zeros", [128, ROW // KC], F32, s2)
        rden = sb("rden", [TP, NT, KC, 2], F32, s2)
        mm = sb("mm", [NG, 2], F32, s2)
        win = sb("win", [NG, 2], F32, s2)
        extra = sb("extra", [NG, 1], F32, s2)
        upper = sb("upper", [NG, NG], F32, s2)
        diag = sb("diag", [NG, NG], F32, s2)
        qf_flat = qf[:, :, :].rearrange("p k n -> p (k n)")
        dstg_i = qf_flat[0:NG, 0:EG].bitcast(I32)
        dstg = qf_flat[0:NG, EG:2 * EG]
        dstc_i = qf_flat[0:TP, 2 * EG:2 * EG + NG * TG].bitcast(I32)
        lines = qf_flat[0:1, 2 * EG + NG * TG:2 * EG + NG * TG + 3 * NG].rearrange("p (a g) -> p a g", a=3)
        r1, starts, ends = (qf_flat[0:1, 2 * EG + NG * TG + i * NG:2 * EG + NG * TG + (i + 1) * NG] for i in (3, 4, 5))
        e_raw = [qf_flat[:, p * EG:(p + 1) * EG] for p in range(2)]
        e_hi, e_lo = ([w[1][:, 1 + p, 0:EG] for p in range(2)] for w in (w_hi, w_lo))
        v_nodes = nodes
        k_part = bias_row[:, 0, :]
        X_PIECES = [(0, 2), (2, 3), (5, 5)]
        HALVES = [(0, 5), (5, 5)]

        x_loaded = [sem(f"x_loaded{h}") for h in range(3)]
        dst_loaded, cols_loaded, feat_loaded = (sem(n) for n in ("dst_loaded", "cols_loaded", "feat_loaded"))
        consts_made, stats_made, std_made, scale_std, centred, turned, turned_used, high1 = (sem(n) for n in (
            "consts_made", "stats_made", "std_made", "scale_std", "centred", "turned", "turned_used", "high1"))
        win_made, rows_ready, diag_made, spread_ready, table_zeroed, banks_read = (sem(n) for n in (
            "win_made", "rows_ready", "diag_made", "spread_ready", "table_zeroed", "banks_read"))
        zeros_made = sem("zeros_made")
        out_ready, proj_made, k_biased, k_parts, k_made, v_made, q_parts, q_made = (sem(n) for n in (
            "out_ready", "proj_made", "k_biased", "k_parts", "k_made", "v_made", "q_parts", "q_made"))
        proj_stored = [sem(f"proj_stored{i}") for i in range(2)]
        bias_loaded, kv_ready, kv_made = (sem(n) for n in ("bias_loaded", "kv_ready", "kv_made"))
        k_summed, att_ready, att_made, att_turned, att_high, att_low, base_made, s2_zeroed = (sem(n) for n in (
            "k_summed", "att_ready", "att_made", "att_turned", "att_high", "att_low", "base_made", "s2_zeroed"))
        mix_ready, mix_added = sem("mix_ready"), sem("mix_added")
        taken, taken_x = sem("taken"), sem("taken_x")
        att = row_out

        def product3(out_ap, lhs, rhs, first, last):
            nc.tensor.matmul(out_ap, lhs[0], rhs[0], start=first, stop=False)
            nc.tensor.matmul(out_ap, lhs[0], rhs[1], start=False, stop=False)
            return nc.tensor.matmul(out_ap, lhs[1], rhs[0], start=False, stop=last)

        def turned_att(t):
            return bank[4 + t % 2][:, 0:KC * TP].rearrange("p (k n) -> p k n", k=KC)

        QJ = [(c, s) for c in range(KC) for s in range(len(SLICES))]
        MJ = [(c, s) for s in range(len(SLICES)) for c in range(KC)]
        PROJ, K, V, Q, MIX, EDGE, SUMS = range(7)
        W_HALVES = [(w, u % 2, slice(2 * h, 2 * h + 2))
                    for u, w in enumerate((w1a, wk, wv, wq, wp)) for h in range(2)]
        W_HALVES.append((w1b, 1, slice(0, 1)))
        W_HALVES += [(w2, 0, slice(2 * h, 2 * h + 2)) for h in range(2)]
        LAST_HALF = [1, 3, 5, 7, 9, 10, 12]

        def load_weights(sp, i):
            w, _, kk = W_HALVES[i]
            if i >= 2:
                sp.wait_ge(w_low, i - 1)
            sp.dma_start(w_raw[i % 2][:, 0:kk.stop - kk.start, :],
                         w.rearrange("(k p) f -> p k f", p=128)[:, kk, :]).then_inc(w_loaded[i % 2], 16)

        def weights_high(act, i):
            _, slot, kk = W_HALVES[i]
            act.wait_ge(w_loaded[i % 2], 16 * (i // 2 + 1))
            nc.scalar.copy(w_hi[slot][:, kk, :], w_raw[i % 2][:, 0:kk.stop - kk.start, :]).then_inc(w_high, 1)

        def weights_low(dve, i):
            _, slot, kk = W_HALVES[i]
            dve.wait_ge(w_high, i + 1)
            nc.vector.tensor_tensor(w_lo[slot][:, kk, :], w_raw[i % 2][:, 0:kk.stop - kk.start, :],
                                    w_hi[slot][:, kk, :], ALU.subtract).then_inc(w_low, 1)

        e_loaded = [sem(f"e_loaded{p}") for p in range(2)]
        idx_loaded = [sem(f"idx_loaded{p}") for p in range(2)]
        gathered = [[sem(f"gathered{p}{t}") for t in range(TG)] for p in range(2)]
        e_high, e_low, e_low_first, added = (sem(n) for n in ("e_high", "e_low", "e_low_first", "added"))
        EH = EG // 2

        def load_edges(sp, g, p):
            sp.dma_start(e_raw[p], edge_blocks[g] if isinstance(g, int) else
                         edge_blocks[bass.ds(g, 1)].rearrange("a p e -> p (a e)")).then_inc(e_loaded[p], 16)

        def load_idx(sp, g, p):
            sp.dma_start(idx[p][:, :], src_blocks[g] if isinstance(g, int) else
                         src_blocks[bass.ds(g, 1)].rearrange("a p t -> p (a t)")).then_inc(idx_loaded[p], 16)

        def gather(pool, p):
            for t in range(TG):
                pool.indirect_dma_start(
                    out=gath[p][t], out_offset=None, in_=proj,
                    in_offset=bass.IndirectOffsetOnAxis(ap=idx[p][:, t:t + 1], axis=0)
                ).then_inc(gathered[p][t], 16)

        def edge_low_last(p):
            nc.gpsimd.tensor_tensor(e_lo[p][:, EH:], e_raw[p][:, EH:], e_hi[p][:, EH:], ALU.subtract).then_inc(e_low, 1)

        def edge_low_first(p):
            nc.vector.tensor_tensor(e_lo[p][:, 0:EH], e_raw[p][:, 0:EH], e_hi[p][:, 0:EH],
                                    ALU.subtract).then_inc(e_low_first, 1)

        with nc.Block() as block:
            @block.sync
            def _(sp):
                def load_x(h):
                    t0, n = X_PIECES[h]
                    rows_dma(sp, nodes[:, t0:t0 + n, :],
                             x_nodes.rearrange("(t p) f -> p t f", p=TP)[:, t0:t0 + n, :], x_loaded[h])

                load_x(0)
                load_x(1)
                load_weights(sp, 0)
                load_weights(sp, 1)
                load_x(2)
                sp.dma_start(bias_row[:, 0, :], b1.unsqueeze(0).to_broadcast([TP, D])).then_inc(bias_loaded, 16)
                sp.dma_start(bias_row[:, 1, :], bk.unsqueeze(0).to_broadcast([TP, D])).then_inc(bias_loaded, 16)
                sp.dma_start(bias_row[:, 2, :], bv.unsqueeze(0).to_broadcast([TP, D])).then_inc(bias_loaded, 16)
                load_weights(sp, 2)
                load_weights(sp, 3)
                sp.dma_start(dstg_i, dst_groups).then_inc(dst_loaded, 16)
                sp.dma_start(dstc_i, dst_cols).then_inc(dst_loaded, 16)
                sp.dma_start(bc[:, :, :], cols).then_inc(cols_loaded, 16)
                sp.dma_start(base[:, :, :], x_feat.rearrange("(k p) n -> p k n", p=128)).then_inc(feat_loaded, 16)
                for t in range(NT):
                    sp.wait_ge(proj_made, t + 1)
                    rows_dma(sp, proj[t * TP:(t + 1) * TP, :], row_out[t % 2], proj_stored[t % 2])
                for p in range(2):
                    load_idx(sp, p, p)
                for i in range(4, LAST_HALF[EDGE] + 1):
                    load_weights(sp, i)
                sp.wait_ge(att_ready, NT)
                for p in range(2):
                    load_edges(sp, p, p)
                sp.wait_ge(proj_stored[0], 32 * 5)
                sp.wait_ge(proj_stored[1], 32 * 5)

            @block.gpsimd
            def _(pool):
                pool_chain.link(pool, nc.gpsimd.memset(ones[:, :], 1.0))
                pool_chain.link(pool, nc.gpsimd.memset(epsc[:, :], EPS))
                nc.gpsimd.affine_select(out=ident[:, :], in_=ones[:, :], compare_op=ALU.is_equal, fill=0.0,
                                        base=0, pattern=[[-1, 128]], channel_multiplier=1).then_inc(consts_made, 1)
                nc.gpsimd.affine_select(out=upper[:, :], in_=ones[0:NG, 0:NG], compare_op=ALU.is_gt, fill=0.0,
                                        base=0, pattern=[[1, NG]], channel_multiplier=-1).then_inc(consts_made, 1)
                nc.gpsimd.memset(zeros[:, :], 0.0).then_inc(zeros_made, 1)
                nc.gpsimd.iota(node_no[:, :], pattern=[[1, HW]], base=0, channel_multiplier=0,
                               allow_small_or_imprecise_dtypes=True)
                nc.gpsimd.memset(kv_sb[:, :, :], 0.0).then_inc(s2_zeroed, 1)
                pool.wait_ge(feat_loaded, 16)
                pool.wait_ge(high1, 2 * NT)
                nc.gpsimd.tensor_tensor(base[:, :, :], base[:, :, :], xn[:, :, :], ALU.add).then_inc(base_made, 1)
                pool.wait_ge(zeros_made, 1)
                for i in range(NST):
                    pool.dma_start(slot_in[i * TS:(i + 1) * TS, :].rearrange("p (a f) -> p a f", a=KC),
                                   zeros[0:TS, :].unsqueeze(1).to_broadcast([TS, KC, ROW // KC])).then_inc(table_zeroed, 16)
                pool.wait_ge(proj_made, NT)
                pool.wait_ge(k_made, 2)
                ins = nc.gpsimd.tensor_tensor(k_part, kf[:, 0, :], kf[:, 1, :], ALU.add)
                for t in range(2, NT):
                    pool_chain.link(pool, ins)
                    pool.wait_ge(k_made, t + 1)
                    ins = nc.gpsimd.tensor_tensor(k_part, k_part, kf[:, t, :], ALU.add)
                ins.then_inc(k_summed, 1)
                pool.wait_ge(kv_ready, 1)
                nc.gpsimd.memset(nodes, 0.0).then_inc(taken, 1)
                pool.wait_ge(table_zeroed, 16 * NST)
                for p in range(2):
                    pool.wait_ge(proj_stored[p], 32 * 5)
                for p in range(2):
                    pool.wait_ge(idx_loaded[p], 16)
                    gather(pool, p)
                for p in range(2):
                    pool.wait_ge(e_high, p + 1)
                    edge_low_last(p)

            @block.scalar
            def _(act):
                def std(h):
                    t0, n = HALVES[h]
                    act.wait_ge(stats_made, h + 1)
                    nc.scalar.activation(rstd[:, t0:t0 + n], mv[:, t0:t0 + n, 1], ACT.Sqrt,
                                         bias=epsc[0:TP, :]).then_inc(std_made, 1)

                def parts(t):
                    act.wait_ge(turned, t + 1)
                    s = slice(t * TP, (t + 1) * TP)
                    pb = bank[6 + t % 2][:, 0:KC * TP].rearrange("p (k n) -> p k n", k=KC)
                    nc.scalar.copy(xh[:, :, s], pb).then_inc(high1, 1)
                    nc.scalar.copy(xn[:, :, s], pb).then_inc(high1, 1)

                weights_high(act, 0)
                act.wait_ge(consts_made, 2)
                std(0)
                weights_high(act, 1)
                for t in range(5):
                    parts(t)
                std(1)
                for t in range(5, NT):
                    parts(t)
                act.wait_ge(cols_loaded, 16)
                nc.scalar.activation(gscale[:, :], COL["var"], ACT.Sqrt, bias=epsc[:, :]).then_inc(scale_std, 1)

                def high(u):
                    if u >= 2:
                        act.wait_ge(out_ready, (u - 1) * NT)
                    for i in (2 * u, 2 * u + 1):
                        weights_high(act, i)

                high(K)
                high(V)
                for t in range(NT):
                    act.wait_ge(k_biased, t + 1)
                    nc.scalar.activation(exp_t[t % 2][0:TP, :], row_out[t % 2][:, :], ACT.Exp)
                    nc.scalar.activation(relu_t[t % 2][0:TP, :], row_out[t % 2][:, :], ACT.Relu).then_inc(k_parts, 1)
                high(Q)
                high(MIX)
                for j, (c, s) in enumerate(QJ):
                    a, n = SLICES[s]
                    act.wait_ge(out_ready, 3 * NT + j + 1)
                    if j < 2:
                        act.wait_ge(k_made, NT)
                    else:
                        act.wait_ge(q_made, j - 1)
                    pb = bank[(3 * NT + j) % 6][:, 0:n]
                    nc.scalar.activation(exp_t[j % 2][:, 0:n], pb, ACT.Exp, bias=COL["bq"][:, c:c + 1])
                    nc.scalar.activation(relu_t[j % 2][:, 0:n], pb, ACT.Relu,
                                         bias=COL["bq"][:, c:c + 1]).then_inc(q_parts, 1)
                weights_high(act, LAST_HALF[EDGE])
                for t in range(NT):
                    act.wait_ge(att_turned, t + 1)
                    nc.scalar.copy(xh[:, :, t * TP:(t + 1) * TP], turned_att(t)).then_inc(att_high, 1)
                for p in range(2):
                    act.wait_ge(e_loaded[p], 16)
                    nc.scalar.copy(e_hi[p], e_raw[p]).then_inc(e_high, 1)

            @block.vector
            def _(dve):
                L = dve_chain.link

                def centre(h):
                    t0, n = HALVES[h]
                    ts = slice(t0, t0 + n)
                    for t in range(t0, t0 + n):
                        for piece, (p0, _) in enumerate(X_PIECES):
                            if t == p0:
                                dve.wait_ge(x_loaded[piece], 32)
                        L(dve, nc.vector.bn_stats(stat[:, t, 0, :], nodes[:, t, :]))
                        last = nc.vector.bn_aggr(mv[:, t, :], stat[:, t, 0, :])
                    last.then_inc(stats_made, 1)
                    dve.wait_ge(stats_made, h + 1)
                    L(dve, nc.vector.tensor_scalar(tmp_t[:, ts], mv[:, ts, 1], EPS, None, ALU.add))
                    dve.wait_ge(std_made, h + 1)
                    newton_rsqrt(dve, rstd[:, ts], tmp_t[:, ts], tmp_s[:, ts], stat[:, ts, 0, 0])
                    for t in range(t0, t0 + n):
                        nc.vector.tensor_scalar(nodes[:, t, :], nodes[:, t, :], mv[:, t, 0:1], rstd[:, t:t + 1],
                                                ALU.subtract, ALU.mult).then_inc(centred, 1)

                def x_low(t):
                    dve.wait_ge(high1, 2 * t + 2)
                    pb = bank[6 + t % 2][:, 0:KC * TP].rearrange("p (k n) -> p k n", k=KC)
                    s = slice(t * TP, (t + 1) * TP)
                    nc.vector.tensor_tensor(xl[:, :, s], pb, xh[:, :, s], ALU.subtract).then_inc(turned_used, 1)

                def proj_add(t):
                    dve.wait_ge(out_ready, t + 1)
                    if t >= 2:
                        dve.wait_ge(proj_stored[t % 2], 32 * (t // 2))
                    nc.vector.tensor_tensor(row_out[t % 2][:, :], bank[t % 6][0:TP, :], bias_row[:, 0, :],
                                            ALU.add).then_inc(proj_made, 1)

                def low(u):
                    for i in (2 * u, 2 * u + 1):
                        weights_low(dve, i)

                centre(0)
                low(PROJ)
                for t in range(5):
                    x_low(t)
                centre(1)
                dve.wait_ge(bias_loaded, 48)
                proj_add(0)
                for t in range(5, NT):
                    x_low(t)
                proj_add(1)
                low(K)
                proj_add(2)
                proj_add(3)
                dve.wait_ge(dst_loaded, 32)
                L(dve, nc.vector.tensor_copy(dstg, dstg_i))
                nc.vector.tensor_copy(dst_f[:, :], dstc_i)
                nc.vector.tensor_reduce(mm[:, 0:1], dstg, AX_X, ALU.min)
                L(dve, nc.vector.tensor_reduce(mm[:, 1:2], dstg, AX_X, ALU.max))
                L(dve, nc.vector.tensor_scalar(win[:, :], mm[:, :], float(TP), None, ALU.is_ge))
                for w in range(2, NT):
                    L(dve, nc.vector.scalar_tensor_tensor(win[:, :], mm[:, :], float(TP * w), win[:, :],
                                                          ALU.is_ge, ALU.add))
                nc.vector.tensor_tensor(extra[:, :], win[:, 1:2], win[:, 0:1], ALU.subtract).then_inc(win_made, 1)
                dve.wait_ge(consts_made, 2)
                nc.vector.tensor_scalar(diag[:, :], ident[0:NG, 0:NG], win[:, 0:1], float(TP),
                                        ALU.mult, ALU.mult).then_inc(diag_made, 1)
                for t in range(4, NT):
                    proj_add(t)
                dve.wait_ge(rows_ready, 1)
                pr = bank[6][0:1, 0:3 * NG].rearrange("p (a g) -> p a g", a=3)
                L(dve, nc.vector.tensor_copy(lines, pr))
                lo, ex, x0 = lines[:, 0, :], lines[:, 1, :], lines[:, 2, :]
                L(dve, nc.vector.scalar_tensor_tensor(r1, x0, float(SCALE_X0 // 16), ex, ALU.mult, ALU.add))
                L(dve, nc.vector.scalar_tensor_tensor(r1, r1, 16.0, lo, ALU.mult, ALU.add))
                L(dve, nc.vector.memset(ends, 1.0))
                L(dve, nc.vector.tensor_tensor(ends[:, 0:NG - 1], lo[:, 1:], lo[:, 0:NG - 1], ALU.is_gt))
                L(dve, nc.vector.tensor_tensor(starts[:, 1:], lo[:, 1:], lo[:, 0:NG - 1], ALU.is_lt))
                L(dve, nc.vector.tensor_tensor(ends[:, 0:NG - 1], ends[:, 0:NG - 1], starts[:, 1:], ALU.add))
                L(dve, nc.vector.tensor_tensor(ends[:, 0:NG - 1], ends[:, 0:NG - 1], ex[:, 0:NG - 1], ALU.add))
                L(dve, nc.vector.tensor_scalar(ends, ends, 1.0, None, ALU.min))
                L(dve, nc.vector.memset(starts[:, 0:1], 1.0))
                L(dve, nc.vector.tensor_copy(starts[:, 1:], ends[:, 0:NG - 1]))
                L(dve, nc.vector.scalar_tensor_tensor(r1, starts, float(STARTS), r1, ALU.mult, ALU.add))
                L(dve, nc.vector.scalar_tensor_tensor(word[:, :], ends, float(ENDS), r1, ALU.mult, ALU.add))
                dve.wait_ge(spread_ready, 1)
                nc.vector.tensor_tensor(
                    rel_neg[:, :].rearrange("p (g t) -> p g t", t=TG),
                    bank[7][0:TP, 0:NG].unsqueeze(2).to_broadcast([TP, NG, TG]),
                    dst_f[:, :].rearrange("p (g t) -> p g t", t=TG), ALU.subtract).then_inc(banks_read, 1)
                dve.wait_ge(cols_loaded, 16)
                L(dve, nc.vector.tensor_scalar(tmp_c[:, 0, :], COL["var"], EPS, None, ALU.add))
                dve.wait_ge(scale_std, 1)
                newton_rsqrt(dve, gscale[:, :], tmp_c[:, 0, :], tmp_c[:, 1, :], tmp_c[:, 2, :])
                L(dve, nc.vector.tensor_tensor(gscale[:, :], gscale[:, :], COL["gamma"], ALU.mult))
                L(dve, nc.vector.tensor_tensor(gshift[:, :], gscale[:, :], COL["mean"], ALU.mult))
                L(dve, nc.vector.tensor_tensor(gshift[:, :], COL["beta"], gshift[:, :], ALU.subtract))
                L(dve, nc.vector.tensor_tensor(gshift[:, :], gshift[:, :], COL["bp"], ALU.add))
                nc.vector.tensor_tensor(brz[:, 0, :], COL["bir"], COL["bhr"], ALU.add)
                L(dve, nc.vector.tensor_tensor(brz[:, 1, :], COL["biz"], COL["bhz"], ALU.add))
                low(V)

                def key(t):
                    dve.wait_ge(k_parts, t + 1)
                    nc.vector.scalar_tensor_tensor(kf[:, t, :], exp_t[t % 2][0:TP, :], 1.0, relu_t[t % 2][0:TP, :],
                                                   ALU.min, ALU.add).then_inc(k_made, 1)

                for t in range(NT):
                    dve.wait_ge(out_ready, NT + t + 1)
                    if t < 2:
                        dve.wait_ge(proj_stored[t % 2], 32 * 5)
                    else:
                        dve.wait_ge(k_parts, t - 1)
                    nc.vector.tensor_tensor(row_out[t % 2][:, :], bank[(NT + t) % 6][0:TP, :], bias_row[:, 1, :],
                                            ALU.add).then_inc(k_biased, 1)
                    if t:
                        key(t - 1)
                key(NT - 1)
                low(Q)
                for t in range(NT):
                    dve.wait_ge(out_ready, 2 * NT + t + 1)
                    nc.vector.tensor_tensor(v_nodes[:, t, :], bank[(2 * NT + t) % 6][0:TP, :], bias_row[:, 2, :],
                                            ALU.add).then_inc(v_made, 1)
                low(MIX)
                for j, (c, s) in enumerate(QJ):
                    a, n = SLICES[s]
                    dve.wait_ge(q_parts, j + 1)
                    nc.vector.scalar_tensor_tensor(qf[:, c, a:a + n], exp_t[j % 2][:, 0:n], 1.0,
                                                   relu_t[j % 2][:, 0:n], ALU.min, ALU.add).then_inc(q_made, 1)
                weights_low(dve, LAST_HALF[EDGE])
                dve.wait_ge(s2_zeroed, 1)
                dve.wait_ge(kv_ready, 1)
                kvp = bank[6][:, :].rearrange("p (c e) -> p c e", c=KC)
                for h in range(2):
                    q = slice(64 * h, 64 * h + 64)
                    nc.vector.tensor_copy(kv_sb[q, :, 128 + h], bank[7][q, 0:KC])
                    nc.vector.tensor_copy(kv_sb[q, :, q], kvp[q, :, q]).then_inc(kv_made, 1)

                def normalise(t):
                    dve.wait_ge(att_ready, t + 1)
                    pairs = [bank[2 * (t % 2) + b][0:TP, 0:260].rearrange("p (c e) -> p c e", c=2) for b in range(2)]
                    for b in range(2):
                        last = nc.vector.reciprocal(rden[:, t, 2 * b:2 * b + 2, :], pairs[b][:, :, 128:130])
                    L(dve, last)
                    if t >= 2:
                        dve.wait_ge(att_turned, t - 1)
                    for b in range(2):
                        last = nc.vector.tensor_tensor(
                            att[t % 2][:, 256 * b:256 * b + 256].rearrange("p (c h e) -> p c h e", c=2, h=2),
                            pairs[b][:, :, 0:128].rearrange("p c (h e) -> p c h e", h=2),
                            rden[:, t, 2 * b:2 * b + 2, :].unsqueeze(3).to_broadcast([TP, 2, 2, DH]), ALU.mult)
                    last.then_inc(att_made, 1)

                def att_low_part(t):
                    dve.wait_ge(att_high, t + 1)
                    at = slice(t * TP, (t + 1) * TP)
                    nc.vector.tensor_tensor(xl[:, :, at], turned_att(t), xh[:, :, at], ALU.subtract).then_inc(att_low, 1)

                for t in range(NT):
                    normalise(t)
                    if t:
                        att_low_part(t - 1)
                att_low_part(NT - 1)
                dve.wait_ge(base_made, 1)
                for j, (c, s) in enumerate(MJ):
                    a, n = SLICES[s]
                    dve.wait_ge(mix_ready, j + 1)
                    nc.vector.scalar_tensor_tensor(base[:, c, a:a + n], bank[(6, 7, 0, 1)[j % 4]][:, 0:n], gshift[:, c:c + 1],
                                                   base[:, c, a:a + n], ALU.add, ALU.add).then_inc(mix_added, 1)
                dve.wait_ge(e_high, 1)
                edge_low_first(0)

            @block.tensor
            def _(pe):
                def turn(t):
                    pe.wait_ge(centred, t + 1)
                    if t >= 2:
                        pe.wait_ge(turned_used, t - 1)
                    for k in range(KC):
                        last = nc.tensor.transpose(bank[6 + t % 2][:, k * TP:(k + 1) * TP],
                                                   nodes[:, t, k * 128:(k + 1) * 128], ident[0:TP, 0:TP])
                    last.then_inc(turned, 1)

                def free(j):
                    j -= 6
                    if j < 0:
                        return
                    if j < NT:
                        pe.wait_ge(proj_made, j + 1)
                    elif j < 2 * NT:
                        pe.wait_ge(k_biased, j - NT + 1)
                    elif j < 3 * NT:
                        pe.wait_ge(v_made, j - 2 * NT + 1)
                    else:
                        pe.wait_ge(q_parts, j - 3 * NT + 1)

                def row_product(u, t):
                    free(u * NT + t)
                    s = slice(t * TP, (t + 1) * TP)
                    for k in range(KC):
                        last = product3(bank[(u * NT + t) % 6][0:TP, :], (xh[:, k, s], xl[:, k, s]),
                                        (w_hi[u % 2][:, k, :], w_lo[u % 2][:, k, :]), k == 0, k == KC - 1)
                    last.then_inc(out_ready, 1)

                pe.wait_ge(consts_made, 2)
                for t in range(5):
                    turn(t)
                pe.wait_ge(w_low, LAST_HALF[PROJ] + 1)
                for t in range(NT):
                    pe.wait_ge(turned_used, t + 1)
                    row_product(PROJ, t)
                    for later in {3: (5, 6), 4: (7, 8), 5: (9,)}.get(t, ()):
                        turn(later)
                pe.wait_ge(w_low, LAST_HALF[K] + 1)
                for t in range(3):
                    row_product(K, t)
                pe.wait_ge(win_made, 1)
                nc.tensor.matmul(bank[6][0:1, 0:NG], win[:, 0:1], ident[0:NG, 0:NG], start=True, stop=True)
                nc.tensor.matmul(bank[6][0:1, NG:2 * NG], extra[:, :], ident[0:NG, 0:NG], start=True, stop=True)
                nc.tensor.matmul(bank[6][0:1, 2 * NG:3 * NG], extra[:, :], upper[:, :],
                                 start=True, stop=True).then_inc(rows_ready, 1)
                pe.wait_ge(diag_made, 1)
                nc.tensor.matmul(bank[7][0:TP, 0:NG], ones[0:NG, 0:TP], diag[:, :],
                                 start=True, stop=True).then_inc(spread_ready, 1)
                for t in range(3, NT):
                    row_product(K, t)
                pe.wait_ge(w_low, LAST_HALF[V] + 1)
                for t in range(NT):
                    row_product(V, t)
                pe.wait_ge(w_low, LAST_HALF[Q] + 1)
                for j, (c, s) in enumerate(QJ):
                    a, n = SLICES[s]
                    free(3 * NT + j)
                    cc = slice(c * 128, (c + 1) * 128)
                    for k in range(KC):
                        last = product3(bank[(3 * NT + j) % 6][:, 0:n], (w_hi[1][:, k, cc], w_lo[1][:, k, cc]),
                                        (xh[:, k, a:a + n], xl[:, k, a:a + n]), k == 0, k == KC - 1)
                    last.then_inc(out_ready, 1)
                pe.wait_ge(k_made, NT)
                pe.wait_ge(v_made, NT)
                pe.wait_ge(banks_read, 1)
                for c in range(KC):
                    cc = slice(c * 128, (c + 1) * 128)
                    for t in range(NT):
                        nc.tensor.matmul(bank[6][:, cc], kf[:, t, cc], v_nodes[:, t, cc],
                                         start=(t == 0), stop=(t == NT - 1))
                pe.wait_ge(k_summed, 1)
                for c in range(KC):
                    last = nc.tensor.matmul(bank[7][:, c:c + 1], k_part[:, c * 128:(c + 1) * 128], ones[0:TP, 0:1],
                                            start=True, stop=True)
                last.then_inc(kv_ready, 1)
                pe.wait_ge(kv_made, 2)
                pe.wait_ge(q_made, len(QJ))

                def turn_att(t):
                    pe.wait_ge(att_made, t + 1)
                    if t >= 2:
                        pe.wait_ge(att_low, t - 1)
                    for k in range(KC):
                        last = nc.tensor.transpose(turned_att(t)[:, k, :], att[t % 2][:, k * 128:(k + 1) * 128],
                                                   ident[0:TP, 0:TP])
                    last.then_inc(att_turned, 1)

                for t in range(NT):
                    if t >= 2:
                        pe.wait_ge(att_made, t - 1)
                    for c in range(KC):
                        last = nc.tensor.matmul(bank[2 * (t % 2) + c // 2][0:TP, 130 * (c % 2):130 * (c % 2) + 130],
                                                qf[:, c, t * TP:(t + 1) * TP], kv_sb[:, c, :], start=True, stop=True)
                    last.then_inc(att_ready, 1)
                    if t:
                        turn_att(t - 1)
                turn_att(NT - 1)
                pe.wait_ge(w_low, LAST_HALF[MIX] + 1)
                for j, (c, s) in enumerate(MJ):
                    a, n = SLICES[s]
                    pe.wait_ge(att_low, -(-(a + n) // TP))
                    if j >= 4:
                        pe.wait_ge(mix_added, j - 3)
                    cc = slice(c * 128, (c + 1) * 128)
                    for k in range(KC):
                        last = product3(bank[(6, 7, 0, 1)[j % 4]][:, 0:n], (w_hi[0][:, k, cc], w_lo[0][:, k, cc]),
                                        (xh[:, k, a:a + n], xl[:, k, a:a + n]), k == 0, k == KC - 1)
                    last.then_inc(mix_ready, 1)
        s2.close()
        split.close()

        s3 = ExitStack()
        wb_hi, wb_lo = w_hi[1][:, 0, :], w_lo[1][:, 0, :]
        iota_n = sb("iota_n", [TP, N - TP + HW], F32, s3)
        pre_sum = [sb(f"pre_sum{t}", [TP, D], F32, s3) for t in range(TG)]
        m_hi = [[sb(f"m_hi{p}{t}", [TP, D], F32R if t in TWO_PASS else F32, s3) for t in range(TG)] for p in range(2)]
        m_lo = [{t: sb(f"m_lo{p}{t}", [TP, D], F32R, s3) for t in TWO_PASS} for p in range(2)]
        hot = [sb(f"hot{p}", [TP, TG, HW], F32R, s3) for p in range(2)]
        hot_x = sb("hot_x", [TP, TG, HW], F32R, s3)
        offset_sq = sb("offset_sq", [TP, TG, HW], F32, s3)
        ones2 = sb("ones2", [TP, 2], F32R, s3)
        zeros3 = sb("zeros3", [TP, D], F32R, s3)
        NW = len(TWO_PASS)

        iota_made = sem("iota_made")
        pre_ready, relued, lowered, hot_made, summed = (sem(n) for n in (
            "pre_ready", "relued", "lowered", "hot_made", "summed"))
        squared = sem("squared")
        spare_w = [w[:, :, :].rearrange("p k f -> p (k f)")[0:1, :] for w in w_raw]
        cut, n_last = SLICES[-1]
        deg_rows = [spare_w[0][:, 0:cut], spare_w[1][:, 0:n_last]]
        b2_row = spare_w[1][:, n_last:n_last + D]

        def deg_slice(a, n):
            return deg_rows[0][:, a:a + n] if a < cut else deg_rows[1][:, a - cut:a - cut + n]
        hot_x_made, summed_x, main_taken = sem("hot_x_made"), sem("summed_x"), sem("main_taken")
        PRE, SUM, SUM_X, DEG, DEG_X = bank[0:4], bank[4], bank[5], bank[6], bank[7]
        tick = sb("tick", [1, 1], F32, s3)
        deg = sb("deg", [1, 2, N], F32, s3)

        def rel_neg_at(i):
            return rel_neg[:, i:i + 1] if isinstance(i, int) else rel_neg[:, bass.ds(i, 1)]

        def in_pairs(eng, first, last, step):
            pairs = (last - first) // 2
            with eng.Fori(0, pairs) as j:
                for p in range(2):
                    step(j * 2 + (first + p), p)
            for g in range(first + 2 * pairs, last):
                step(g, g % 2)

        def a_window(value):
            return nc.s_assert_within(value, 0, NT - 1, skip_runtime_bounds_check_because="made on the chip from counts of exceeded window bounds")

        def word_at(g):
            return word[0:1, g:g + 1] if isinstance(g, int) else word[0:1, bass.ds(g, 1)]

        def has_further(w):
            return (w & 255) >= 16

        def starts_sums(w):
            return (w & STARTS) >= STARTS

        def ends_sums(w):
            return w >= ENDS

        def further_start(w):
            return nc.s_assert_within((w >> 8) & 1023, 0, NG * (NT - 1) - 1, skip_runtime_bounds_check_because="made on the chip from counts of exceeded window bounds")

        def rest(eng, w, body):
            x0, more = further_start(w), (w >> 4) & 15
            with eng.If((w & 255) >= 32):
                with eng.Fori(x0 + 1, x0 + more) as x:
                    body(x, a_window(x - x0 + ((w & 15) + 1)))

        with nc.Block() as block:
            @block.sync
            def _(sp):
                def step(g, p):
                    sp.wait_ge(e_low, g - 1)
                    sp.wait_ge(e_low_first, g - 1)
                    load_edges(sp, g, p)
                    sp.wait_ge(added, g * TG - TG)
                    load_idx(sp, g, p)

                for i in range(LAST_HALF[EDGE] + 1, LAST_HALF[SUMS] + 1):
                    load_weights(sp, i)
                in_pairs(sp, 2, NG, step)

            @block.gpsimd
            def _(pool):
                def step(g, p):
                    pool.wait_ge(e_high, g + 1)
                    pool.wait_ge(idx_loaded[p], (g - p) * 8 + 16)
                    pool.wait_ge(added, g * TG - TG)
                    edge_low_last(p)
                    gather(pool, p)

                nc.gpsimd.memset(deg[:, :, :], 0.0).then_inc(taken_x, 1)
                nc.gpsimd.iota(iota_n[:, :], pattern=[[1, N - TP + HW]], base=0, channel_multiplier=0,
                               allow_small_or_imprecise_dtypes=True).then_inc(iota_made, 1)
                in_pairs(pool, 2, NG, step)

            @block.scalar
            def _(act):
                def edge_high(g, p):
                    act.wait_ge(e_loaded[p], (g - p) * 8 + 16)
                    if not isinstance(g, int) or g >= 2:
                        act.wait_ge(pre_ready, g * TG - TG)
                    nc.scalar.copy(e_hi[p], e_raw[p]).then_inc(e_high, 1)

                def one_hot_squares(g):
                    if not isinstance(g, int) or g >= 1:
                        act.wait_ge(hot_made, g)
                    for t in range(TG):
                        last = nc.scalar.activation(offset_sq[:, t, :], node_no[:, :], ACT.Square,
                                                    bias=rel_neg_at(g * TG + t))
                    last.then_inc(squared, 1)

                def one_hot_of(g, p):
                    act.wait_ge(squared, g + 1)
                    nc.scalar.activation(hot[p][:, :, :], offset_sq[:, :, :], ACT.Relu, scale=-2.0,
                                         bias=ones[0:TP, 0:1]).then_inc(hot_made, 1)

                def relu(g, p):
                    one_hot_squares(g)
                    for t in range(TG):
                        if t == 1:
                            one_hot_of(g, p)
                        act.wait_ge(added, g * TG + (t + 1))
                        nc.scalar.activation(m_hi[p][t][:, :], pre_sum[t][:, :], ACT.Relu).then_inc(relued, 1)

                relu(0, 0)
                edge_high(2, 0)

                def step(g, p):
                    relu(g, p)
                    edge_high(g + 2, p)

                with act.Fori(0, (NG - 4) // 2) as j:
                    step(j * 2 + 1, 1)
                    step(j * 2 + 2, 0)
                step(NG - 3, 1)
                relu(NG - 2, 0)
                relu(NG - 1, 1)
                for i in range(LAST_HALF[EDGE] + 1, LAST_HALF[SUMS] + 1):
                    weights_high(act, i)

            @block.vector
            def _(dve):
                nc.vector.tensor_copy(ones2[:, :], ones[0:TP, 0:2])
                nc.vector.tensor_scalar(zeros3[:, :].rearrange("p (a n) -> p a n", n=128),
                                        ones[0:TP, :].unsqueeze(1).to_broadcast([TP, D // 128, 128]), 0.0, None, ALU.mult)

                L = dve_chain.link

                def one_hot(dst_hot, g, of, first_node, signal):
                    for t in range(TG):
                        d = (of[:, g * TG + t:g * TG + t + 1] if isinstance(g, int)
                             else of[:, bass.ds(g * TG + t, 1)])
                        last = nc.vector.tensor_scalar(dst_hot[:, t, :], first_node, d, None, ALU.is_equal)
                    last.then_inc(signal, 1)

                def edge_low(g, p):
                    dve.wait_ge(e_high, g + 1)
                    if not isinstance(g, int) or g >= 2:
                        dve.wait_ge(pre_ready, g * TG - TG)
                    edge_low_first(p)

                def add(g, p, t):
                    dve.wait_ge(pre_ready, g * TG + (t + 1))
                    dve.wait_ge(gathered[p][t], (g - p) * 8 + 16)
                    if not isinstance(g, int) or g >= 1:
                        dve.wait_ge(relued, g * TG + (t + 1 - TG))
                        if t in TWO_PASS:
                            dve.wait_ge(lowered, g * NW + (TWO_PASS.index(t) + 1 - NW))
                    nc.vector.tensor_tensor(pre_sum[t][:, :], PRE[t][0:TP, :], gath[p][t],
                                            ALU.add).then_inc(added, 1)

                def low_part(g, p, t):
                    if t in TWO_PASS:
                        dve.wait_ge(relued, g * TG + (t + 1))
                        nc.vector.scalar_tensor_tensor(m_lo[p][t][:, :], pre_sum[t][:, :], 0.0, m_hi[p][t][:, :],
                                                       ALU.max, ALU.subtract).then_inc(lowered, 1)

                def add_group(g, p):
                    for t in range(TG):
                        add(g, p, t)
                        if t == 1 and not (isinstance(g, int) and g + 1 >= NG):
                            edge_low(g + 1, 1 - p)
                        if t >= 2:
                            low_part(g, p, t - 2)
                    low_part(g, p, TG - 2)
                    low_part(g, p, TG - 1)

                def accumulate(win_of, sums, degs, signal):
                    rows_w = rows[:, :, :].rearrange("p t f -> p (t f)")[:, bass.ds(win_of * ROW, D)]
                    deg_w = deg[:, :, bass.ds(win_of * TP, TP)]
                    nc.vector.tensor_tensor(rows_w, sums[0:TP, :], rows_w, ALU.add)
                    nc.vector.tensor_tensor(deg_w, degs[0:1, 0:2 * HW].rearrange("p (t n) -> p t n", t=2)[:, :, 0:TP],
                                            deg_w, ALU.add).then_inc(signal, 1)

                def hot_further(g, x, window):
                    dve.wait_ge(taken_x, x + 1)
                    one_hot(hot_x, g, dst_f, iota_n[:, bass.ds(window * TP, HW)], hot_x_made)

                def take_further(g, p, x, window):
                    dve.wait_ge(taken_x, x + 1)
                    dve.wait_ge(summed_x, x + 1)
                    accumulate(window, SUM_X, DEG_X, taken_x)

                def take(g, p):
                    w = dve.value_load(word_at(g), min_val=0, max_val=WORD_MAX)
                    with dve.If(ends_sums(w)):
                        with dve.If(has_further(w)):
                            hot_further(g, further_start(w), a_window((w & 15) + 1))
                        dve.wait_ge(summed, g + 1)
                        dve.wait_ge(taken, g + 1)
                        dve.wait_ge(taken_x, further_start(w) + 1)
                        accumulate(a_window(w & 15), SUM, DEG, main_taken)
                        with dve.If(has_further(w)):
                            take_further(g, p, further_start(w), a_window((w & 15) + 1))
                            rest(dve, w, lambda x, window: (hot_further(g, x, window), take_further(g, p, x, window)))
                    dve.wait_ge(taken, g + 1)
                    nc.vector.memset(tick[:, :], 0.0).then_inc(taken, 1)

                def step(g, p):
                    add_group(g, p)
                    take(g - 1, 1 - p)

                add_group(0, 0)
                dve.wait_ge(iota_made, 1)
                with dve.Fori(0, (NG - 2) // 2) as j:
                    step(j * 2 + 1, 1)
                    step(j * 2 + 2, 0)
                step(NG - 1, 1)
                for i in range(LAST_HALF[EDGE] + 1, LAST_HALF[SUMS] + 1):
                    weights_low(dve, i)
                take(NG - 1, 1)
                dve.wait_ge(taken, NG + 1)
                dve.wait_ge(w_low, LAST_HALF[SUMS] + 1)
                for lo, n in ((0, cut), (cut, n_last)):
                    nc.vector.tensor_tensor(deg_slice(lo, n), deg[:, 0, lo:lo + n], deg[:, 1, lo:lo + n], ALU.add)

            @block.tensor
            def _(pe):
                def pre(g, p):
                    pe.wait_ge(e_low, g + 1)
                    pe.wait_ge(e_low_first, g + 1)
                    for t in range(TG):
                        if not isinstance(g, int) or g >= 1:
                            pe.wait_ge(added, g * TG + (t + 1 - TG))
                        c = slice(t * TP, (t + 1) * TP)
                        product3(PRE[t][0:TP, :], (e_hi[p][:, c], e_lo[p][:, c]), (wb_hi, wb_lo),
                                 True, True).then_inc(pre_ready, 1)

                def window_sum(h, p, sums, degs, start):
                    todo = [(h[:, t, 0:TP], part[t][:, :]) if t in TWO_PASS else (h[:, t, 0:TP].bitcast(F32), part[t][:, :])
                            for t in range(TG) for part in ((m_hi[p], m_lo[p]) if t in TWO_PASS else (m_hi[p],))]
                    for i, (lhs, rhs) in enumerate(todo[:-1]):
                        nc.tensor.matmul(sums[0:TP, :], lhs, rhs, start=(start and i == 0), stop=False)

                    def end(signal, stop):
                        nc.tensor.matmul(sums[0:TP, :], *todo[-1], start=False, stop=stop)
                        for t in range(0, TG, 2):
                            last = nc.tensor.matmul(degs[0:2, 0:2 * HW], ones2[:, :],
                                                    h[:, t:t + 2, :].rearrange("p t n -> p (t n)"),
                                                    start=(start and t == 0), stop=(stop and t == TG - 2))
                        last.then_inc(signal, 1)
                    return end

                def group_sum(g, p):
                    w = pe.value_load(word_at(g), min_val=0, max_val=WORD_MAX)
                    pe.wait_ge(hot_made, g + 1)
                    pe.wait_ge(relued, g * TG + TG)
                    pe.wait_ge(lowered, g * NW + NW)
                    with pe.If(starts_sums(w)):
                        pe.wait_ge(taken, g + 1)
                        nc.tensor.matmul(SUM[0:TP, :], hot[p][:, 0, 0:TP], zeros3[:, :], start=True, stop=False)
                        nc.tensor.matmul(DEG[0:2, 0:2 * HW], ones2[:, :], zeros3[:, 0:2 * HW],
                                         start=True, stop=False)
                    end = window_sum(hot[p], p, SUM, DEG, False)

                    def further_sum(x):
                        pe.wait_ge(taken_x, x + 1)
                        pe.wait_ge(hot_x_made, x + 1)
                        window_sum(hot_x, p, SUM_X, DEG_X, True)(summed_x, True)

                    with pe.If(ends_sums(w)):
                        end(summed, True)
                        with pe.If(has_further(w)):
                            further_sum(further_start(w))
                            rest(pe, w, lambda x, window: further_sum(x))
                    with pe.Else():
                        end(summed, False)

                pre(0, 0)
                for g in range(2):
                    pre(g + 1, 1 - g)
                    group_sum(g, g)
                with pe.Fori(0, (NG - 4) // 2) as j:
                    for p in range(2):
                        pre(j * 2 + (p + 3), 1 - p)
                        group_sum(j * 2 + (p + 2), p)
                pre(NG - 1, 1)
                group_sum(NG - 2, 0)
                group_sum(NG - 1, 1)
        s3.close()
        held_kq.close()

        ring = ExitStack()
        RING = 4
        g_raw = [sb(f"g_raw{i}", [128, KC, 128], F32, ring) for i in range(RING)]
        g_hi = [sb(f"g_hi{i}", [128, KC, 128], F32R, ring) for i in range(RING)]
        g_lo = [sb(f"g_lo{i}", [128, KC, 128], F32R, ring) for i in range(RING)]
        NP = 6 * KC
        g_loaded = [sem(f"g_loaded{i}") for i in range(RING)]
        g_high, g_low, gate_done = sem("g_high"), sem("g_low"), sem("gate_done")

        def load_piece(sp, q):
            if q >= RING:
                sp.wait_ge(g_low, q - RING + 1)
            sp.dma_start(g_raw[q % RING][:, :, :], gate_blocks[q]).then_inc(g_loaded[q % RING], 16)

        def pieces_high(act, *qs):
            for q in qs:
                if q < NP:
                    act.wait_ge(g_loaded[q % RING], 16 * (q // RING + 1))
                    if q >= RING:
                        act.wait_ge(gate_done, (q - RING) // 2 + 1)
                    nc.scalar.copy(g_hi[q % RING][:, :, :], g_raw[q % RING][:, :, :]).then_inc(g_high, 1)

        def pieces_low(dve, *qs):
            for q in qs:
                if q < NP:
                    dve.wait_ge(g_high, q + 1)
                    nc.vector.tensor_tensor(g_lo[q % RING][:, :, :], g_raw[q % RING][:, :, :],
                                            g_hi[q % RING][:, :, :], ALU.subtract).then_inc(g_low, 1)

        s4 = ExitStack()
        tr_hi = sb("tr_hi", [128, KC, N], F32R, s4)
        tr_lo = sb("tr_lo", [128, KC, N], F32R, s4)
        ag_hi = sb("ag_hi", [128, KC, N], F32R, s4)
        ag_lo = sb("ag_lo", [128, KC, N], F32R, s4)
        w2_hi, w2_lo = w_hi[0], w_lo[0]
        b2_loaded, sums_turned, sums_high, sums_low = (sem(n) for n in (
            "b2_loaded", "sums_turned", "sums_high", "sums_low"))
        agg_ready, agg_high, agg_low, xn_high = sem("agg_ready"), sem("agg_high"), sem("agg_low"), sem("xn_high")

        with nc.Block() as block:
            @block.sync
            def _(sp):
                sp.dma_start(b2_row, b2.unsqueeze(0)).then_inc(b2_loaded, 16)
                for q in range(RING):
                    load_piece(sp, q)

            def xn_parts(j):
                s = {KC: 0, 2 * KC: 1, 3 * KC - 1: 2}.get(j)
                if s is None:
                    return []
                step = KC if s < 2 else 1
                return [(slice(k, k + step), slice(SLICES[s][0], sum(SLICES[s]))) for k in range(0, KC, step)]

            def bank_nodes(t):
                return bank[t % 4][:, 0:KC * TP].rearrange("p (k n) -> p k n", k=KC)

            @block.scalar
            def _(act):
                for t in range(NT):
                    act.wait_ge(sums_turned, t + 1)
                    nc.scalar.copy(tr_hi[:, :, t * TP:(t + 1) * TP], bank_nodes(t)).then_inc(sums_high, 1)
                pieces_high(act, *range(RING))
                for j, (c, s) in enumerate(MJ):
                    a, n = SLICES[s]
                    act.wait_ge(agg_ready, j + 1)
                    nc.scalar.copy(ag_hi[:, c, a:a + n], bank[j % 4][:, 0:n]).then_inc(agg_high, 1)
                    for kk, at in xn_parts(j):
                        nc.scalar.copy(tr_hi[:, kk, at], xn[:, kk, at]).then_inc(xn_high, 1)

            @block.vector
            def _(dve):
                for t in range(NT):
                    dve.wait_ge(sums_high, t + 1)
                    s = slice(t * TP, (t + 1) * TP)
                    nc.vector.tensor_tensor(tr_lo[:, :, s], bank_nodes(t), tr_hi[:, :, s],
                                            ALU.subtract).then_inc(sums_low, 1)
                pieces_low(dve, *range(RING))
                xn_made = 0
                for j, (c, s) in enumerate(MJ):
                    a, n = SLICES[s]
                    dve.wait_ge(agg_high, j + 1)
                    nc.vector.tensor_tensor(ag_lo[:, c, a:a + n], bank[j % 4][:, 0:n], ag_hi[:, c, a:a + n],
                                            ALU.subtract).then_inc(agg_low, 1)
                    for kk, at in xn_parts(j):
                        xn_made += 1
                        dve.wait_ge(xn_high, xn_made)
                        nc.vector.tensor_tensor(tr_lo[:, kk, at], xn[:, kk, at], tr_hi[:, kk, at], ALU.subtract)

            @block.tensor
            def _(pe):
                for t in range(NT):
                    if t >= 4:
                        pe.wait_ge(sums_low, t - 3)
                    for k in range(KC):
                        last = nc.tensor.transpose(bank[t % 4][:, k * TP:(k + 1) * TP],
                                                   nodes[:, t, k * 128:(k + 1) * 128], ident[0:TP, 0:TP])
                    last.then_inc(sums_turned, 1)
                pe.wait_ge(sums_low, NT)
                pe.wait_ge(b2_loaded, 16)
                for j, (c, s) in enumerate(MJ):
                    a, n = SLICES[s]
                    if j >= 4:
                        pe.wait_ge(agg_low, j - 3)
                    cc = slice(c * 128, (c + 1) * 128)
                    nc.tensor.matmul(bank[j % 4][:, 0:n], b2_row[:, cc], deg_slice(a, n),
                                     start=True, stop=False)
                    for k in range(KC):
                        last = product3(bank[j % 4][:, 0:n], (w2_hi[:, k, cc], w2_lo[:, k, cc]),
                                        (tr_hi[:, k, a:a + n], tr_lo[:, k, a:a + n]), False, k == KC - 1)
                    last.then_inc(agg_ready, 1)
        held_w.close()
        held_x.close()

        s4b = ExitStack()
        w1_all = sb("w1_all", [128, NX, KC, HX], side="right")
        experts_loaded = [sem(f"experts_loaded{i}") for i in range(3)]
        issued = [0, 0, 0]

        def load_expert(sp, i, dst, src):
            if issued[i % 3]:
                sp.wait_ge(experts_loaded[i % 3], 16 * issued[i % 3])
            sp.dma_start(dst, src).then_inc(experts_loaded[i % 3], 16)
            issued[i % 3] += 1

        gate_r = [sb(f"gate_r{i}", [128, N], F32, s4b) for i in range(2)]
        gate_z = [sb(f"gate_z{i}", [128, N], F32, s4b) for i in range(2)]
        wide = SLICES[0][1]
        cand = [sb(f"cand{i}", [128, wide], F32, s4b) for i in range(2)]
        new = [sb(f"new{i}", [128, wide], F32, s4b) for i in range(2)]
        mixd = [sb(f"mixd{i}", [128, wide], F32, s4b) for i in range(2)]
        JB = 6
        FILLS = [(0, 4), (4, 4), (8, 2)]
        LOGITS = bank[7]
        wg_loaded, rows_turned, rows_copied, logits_ready, stats5, std5 = (sem(n) for n in (
            "wg_loaded", "rows_turned", "rows_copied", "logits_ready", "stats5", "std5"))
        fill_bank = lambda c, i: bank[6] if c < KC - 1 or i == 0 else bank[i - 1]
        gate_ready, gate_taken, cand_made, new_made, x1_made = (
            sem(n) for n in ("gate_ready", "gate_taken",
                             "cand_made", "new_made", "x1_made"))

        with nc.Block() as block:
            @block.sync
            def _(sp):
                sp.dma_start(wg_sb[:, :, :], wg.rearrange("(k p) e -> p k e", p=128)).then_inc(wg_loaded, 16)
                for q in range(RING, NP):
                    load_piece(sp, q)
                    if q % 2 and q // 2 - RING // 2 < NX:
                        e = q // 2 - RING // 2
                        load_expert(sp, e, w1_all[:, e, :, :], we1[e].rearrange("(k p) h -> p k h", p=128))

            @block.scalar
            def _(act):
                def copy_rows(c, i):
                    t0, n = FILLS[i]
                    act.wait_ge(rows_turned, 3 * c + i + 1)
                    nc.scalar.copy(nodes[:, t0:t0 + n, c * 128:(c + 1) * 128],
                                   fill_bank(c, i)[0:TP, 0:n * 128].rearrange("p (t f) -> p t f", f=128)
                                   ).then_inc(rows_copied, 1)

                for c in range(KC):
                    for gate, dst in ((0, gate_r[c % 2]), (1, gate_z[c % 2])):
                        for s, (a, n) in enumerate(SLICES):
                            job = 12 * c + 3 * gate + s
                            act.wait_ge(gate_ready, job + 1)
                            if c >= 2:
                                act.wait_ge(x1_made, 3 * (c - 1))
                            nc.scalar.activation(dst[:, a:a + n], bank[job % JB][:, 0:n], ACT.Sigmoid,
                                                 bias=brz[:, gate, c:c + 1]).then_inc(gate_taken, 1)
                            if gate == 1 and c:
                                copy_rows(c - 1, s)
                        pieces_high(act, 6 * c + 4 + 2 * gate, 6 * c + 5 + 2 * gate)
                    for s, (a, n) in enumerate(SLICES):
                        i = 3 * c + s
                        act.wait_ge(cand_made, i + 1)
                        if i >= 2:
                            act.wait_ge(x1_made, i - 1)
                        nc.scalar.activation(new[i % 2][:, 0:n], cand[i % 2][:, 0:n], ACT.Tanh).then_inc(new_made, 1)
                    pieces_high(act, 6 * c + 8, 6 * c + 9)
                for i in range(3):
                    copy_rows(KC - 1, i)
                act.wait_ge(stats5, 1)
                nc.scalar.activation(rstd[:, :], mv[:, :, 1], ACT.Sqrt, bias=epsc[0:TP, :]).then_inc(std5, 1)

            @block.vector
            def _(dve):
                L = dve_chain.link

                def candidate(c, s):
                    a, n = SLICES[s]
                    i, job = 3 * c + s, 12 * c + 6 + 2 * s
                    dve.wait_ge(gate_ready, job + 2)
                    dve.wait_ge(gate_taken, 6 * c + 6)
                    L(dve, nc.vector.scalar_tensor_tensor(
                        cand[i % 2][:, 0:n], bank[(job + 1) % JB][:, 0:n], COL["bhn"][:, c:c + 1],
                        gate_r[c % 2][:, a:a + n], ALU.add, ALU.mult))
                    nc.vector.scalar_tensor_tensor(
                        cand[i % 2][:, 0:n], bank[job % JB][:, 0:n], COL["bin"][:, c:c + 1],
                        cand[i % 2][:, 0:n], ALU.add, ALU.add).then_inc(cand_made, 1)

                def combine(c, s):
                    a, n = SLICES[s]
                    i = 3 * c + s
                    dve.wait_ge(new_made, i + 1)
                    m, nw = mixd[i % 2][:, 0:n], new[i % 2][:, 0:n]
                    L(dve, nc.vector.tensor_tensor(m, tr_hi[:, c, a:a + n], nw, ALU.subtract))
                    L(dve, nc.vector.tensor_tensor(m, m, tr_lo[:, c, a:a + n], ALU.add))
                    L(dve, nc.vector.tensor_tensor(m, m, gate_z[c % 2][:, a:a + n], ALU.mult))
                    L(dve, nc.vector.tensor_tensor(m, m, nw, ALU.add))
                    nc.vector.scalar_tensor_tensor(base[:, c, a:a + n], m, gscale[:, c:c + 1], base[:, c, a:a + n],
                                                   ALU.mult, ALU.add).then_inc(x1_made, 1)

                def chunk_stats(c, i):
                    dve.wait_ge(rows_copied, 3 * c + i + 1)
                    for t in range(FILLS[i][0], sum(FILLS[i])):
                        ins = nc.vector.bn_stats(stat[:, t, c, :], nodes[:, t, c * 128:(c + 1) * 128])
                    dve_chain.link(dve, ins)

                for c in range(KC):
                    pieces_low(dve, 6 * c + 4, 6 * c + 5)
                    pieces_low(dve, 6 * c + 6, 6 * c + 7)
                    if c:
                        for i in range(3):
                            chunk_stats(c - 1, i)
                    if c < KC - 1:
                        candidate(c, 0)
                        candidate(c, 1)
                        combine(c, 0)
                        candidate(c, 2)
                        combine(c, 1)
                        combine(c, 2)
                    else:
                        for s in range(len(SLICES)):
                            candidate(c, s)
                            combine(c, s)
                    pieces_low(dve, 6 * c + 8, 6 * c + 9)
                for i in range(3):
                    chunk_stats(KC - 1, i)
                for t in range(NT):
                    ins = nc.vector.bn_aggr(mv[:, t, :], stat[:, t, :, :])
                ins.then_inc(stats5, 1)
                dve.wait_ge(stats5, 1)
                L(dve, nc.vector.tensor_scalar(tmp_t[:, :], mv[:, :, 1], EPS, None, ALU.add))
                dve.wait_ge(std5, 1)
                newton_rsqrt(dve, rstd[:, :], tmp_t[:, :], tmp_s[:, :], stat[:, :, 0, 0])
                nc.vector.tensor_copy(rows[:, :, D], rstd[:, :])
                nc.vector.scalar_tensor_tensor(rows[:, :, D + 1], mv[:, :, 0], -1.0, rstd[:, :], ALU.mult, ALU.mult)

            @block.tensor
            def _(pe):
                pe.wait_ge(wg_loaded, 16)
                for k in range(KC):
                    nc.tensor.matmul(LOGITS[0:TP, NT * NX:(NT + 1) * NX], ones[:, 0:TP], wg_sb[:, k, :],
                                     start=(k == 0), stop=False)

                def free(job):
                    job -= JB
                    if job >= 0:
                        c, i = divmod(job, 12)
                        if i < 6:
                            pe.wait_ge(gate_taken, 6 * c + i + 1)
                        else:
                            pe.wait_ge(cand_made, 3 * c + (i - 6) // 2 + 1)

                def operand(q, k):
                    return g_hi[q % RING][:, k, :], g_lo[q % RING][:, k, :]

                def turn_rows(c, i):
                    t0, n = FILLS[i]
                    pe.wait_ge(x1_made, 3 * c + (2 if i == 0 else 3))
                    if i or c:
                        pe.wait_ge(rows_copied, 3 * c + i if c < KC - 1 or i == 0 else 3 * c)
                    for t in range(t0, t0 + n):
                        last = nc.tensor.transpose(fill_bank(c, i)[0:TP, (t - t0) * 128:(t - t0 + 1) * 128],
                                                   base[:, c, t * TP:(t + 1) * TP], ident[:, :])
                    last.then_inc(rows_turned, 1)
                    for t in range(t0, t0 + n):
                        last = nc.tensor.matmul(LOGITS[0:TP, t * NX:(t + 1) * NX], base[:, c, t * TP:(t + 1) * TP],
                                                wg_sb[:, c, :], start=False, stop=(c == KC - 1 and t == NT - 1))
                    if c == KC - 1 and i == 2:
                        last.then_inc(logits_ready, 1)

                for c in range(KC):
                    for gate in range(2):
                        q = 6 * c + 2 * gate
                        pe.wait_ge(g_low, q + 2)
                        for s, (a, n) in enumerate(SLICES):
                            job = 12 * c + 3 * gate + s
                            free(job)
                            for k in range(KC):
                                product3(bank[job % JB][:, 0:n], operand(q, k),
                                         (ag_hi[:, k, a:a + n], ag_lo[:, k, a:a + n]), k == 0, False)
                        for s, (a, n) in enumerate(SLICES):
                            job = 12 * c + 3 * gate + s
                            for k in range(KC):
                                last = product3(bank[job % JB][:, 0:n], operand(q + 1, k),
                                                (tr_hi[:, k, a:a + n], tr_lo[:, k, a:a + n]), False, k == KC - 1)
                            last.then_inc(gate_ready, 1)
                            if gate == 1 and c:
                                turn_rows(c - 1, s)
                            if s == len(SLICES) - 1:
                                pe.nop().then_inc(gate_done, 1)
                    q = 6 * c + 4
                    pe.wait_ge(g_low, q + 2)
                    for s, (a, n) in enumerate(SLICES):
                        for part, (hi, lo) in enumerate(((ag_hi, ag_lo), (tr_hi, tr_lo))):
                            job = 12 * c + 6 + 2 * s + part
                            free(job)
                            for k in range(KC):
                                last = product3(bank[job % JB][:, 0:n], operand(q + part, k),
                                                (hi[:, k, a:a + n], lo[:, k, a:a + n]), k == 0, k == KC - 1)
                            last.then_inc(gate_ready, 1)
                    pe.nop().then_inc(gate_done, 1)
                for i in range(3):
                    turn_rows(KC - 1, i)
        s4b.close()
        s4.close()
        ring.close()

        s5 = ExitStack()
        w2_all = sb("w2_all", [128, NX, HX // 128, D], F32, s5)
        bias_all = sb("bias_all", [TS, NX * (HX + D)], F32, s5)
        b1_all, b2_all = bias_all[:, 0:NX * HX], bias_all[:, NX * HX:]
        bg_sb = sb("bg_sb", [TP, NX], F32, s5)
        before = sb("before", [128, 128], F32, s5)
        R3 = lambda n: sb(n, [TP, NT, NX], F32, s5)
        logit, prob, is_max, hot_e, place = R3("logit"), R3("prob"), R3("is_max"), R3("hot_e"), R3("place")
        e_less = sb("e_less", [TP, NX], F32, s5)
        best = sb("best", [TP, NT], F32, s5)
        score = sb("score", [TP, NT], F32, s5)
        slot_f = sb("slot_f", [TP, NT], F32, s5)
        slot = sb("slot", [TP, NT], I32, s5)
        held = sb("held", [TP, NX], F32, s5)
        MT = -(-N // TS)
        steps = sb("steps", [TP, NX, MT], F32, s5)
        over = sb("over", [TP, NX, MT], F32, s5)
        upto = sb("upto", [TP, NX, NX], F32, s5)
        parts = sb("parts", [TP, NX, NX], F32, s5)
        tiles = sb("tiles", [TP, NX], F32, s5)
        cum = sb("cum", [TP, NX], F32, s5)
        first = sb("first", [TP, NX], F32, s5)
        tile_no = sb("tile_no", [1, NST, NX], F32, s5)
        past = sb("past", [1, NST, NX], F32, s5)
        tile_ef = sb("tile_ef", [1, NST], F32, s5)
        tile_e = sb("tile_e", [1, NST], I32, s5)
        FR = 5
        row_in = [sb(f"row_in{i}", [TS, ROW], F32, s5) for i in range(FR)]
        node_i = [sb(f"node_i{i}", [TS, 1], I32, s5) for i in range(FR)]
        spare = sb("spare", [TS, NST], F32, s5)
        is_spare = [sb(f"is_spare{i}", [TS, 1], F32, s5) for i in range(2)]
        y = [sb(f"y{i}", [TS, D], F32, s5) for i in range(2)]
        yt = [sb(f"yt{i}", [128, KC, TS], F32, s5) for i in range(2)]
        pre_hid = [sb(f"pre_hid{i}", [TS, HX], F32, s5) for i in range(2)]
        hid = [sb(f"hid{i}", [128, HX // 128, TS], F32, s5) for i in range(2)]
        fo = [sb(f"fo{i}", [TS, D], F32, s5) for i in range(2)]
        bg_loaded, consts5, shifted, exp_made, held_made, counts_ready, slots_made, scattered = (
            sem(n) for n in ("bg_loaded", "consts5", "shifted", "exp_made", "held_made",
                             "counts_ready", "slots_made", "scattered"))
        row_loaded = [sem(f"row_loaded{i}") for i in range(FR)]
        y_made, y_turned, yt_made, pre_ready5, pre_made, hid_turned, hid_made, f_ready, f_made = (sem(n) for n in (
            "y_made", "y_turned", "yt_made", "pre_ready5", "pre_made", "hid_turned", "hid_made", "f_ready", "f_made"))
        tiles_made, bias_in, bias_spread, bias_made = (sem(n) for n in (
            "tiles_made", "bias_in", "bias_spread", "bias_made"))
        NB = NX * (HX + D) // 512
        out_stored = [sem(f"out_stored{i}") for i in range(2)]

        def an_expert(eng, i):
            return eng.value_load(tile_e[0:1, i:i + 1], min_val=0, max_val=NX - 1)

        with nc.Block() as block:
            @block.sync
            def _(sp):
                sp.dma_start(bg_sb[:, :], bg.unsqueeze(0).to_broadcast([TP, NX])).then_inc(bg_loaded, 16)
                sp.dma_start(b1_all[0:1, :], be1.rearrange("e h -> (e h)").unsqueeze(0)).then_inc(bias_in, 16)
                sp.dma_start(b2_all[0:1, :], be2.rearrange("e h -> (e h)").unsqueeze(0)).then_inc(bias_in, 16)
                for e in range(NX):
                    load_expert(sp, NX + e, w2_all[:, e, :, :], we2[e].rearrange("(k p) h -> p k h", p=128))
                sp.wait_ge(scattered, 16 * NT)
                for i in range(NST):
                    if i >= FR:
                        sp.wait_ge(f_made, i - FR + 1)
                    sp.dma_start(row_in[i % FR][:, :], slot_in[i * TS:(i + 1) * TS, :]).then_inc(row_loaded[i % FR], 16)
                sp.wait_ge(out_stored[0], 16 * ((NST + 1) // 2))
                sp.wait_ge(out_stored[1], 16 * (NST // 2))

            @block.gpsimd
            def _(pool):
                exact = dict(allow_small_or_imprecise_dtypes=True)
                nc.gpsimd.iota(e_less[:, :], pattern=[[1, NX]], base=-NX, channel_multiplier=0, **exact)
                nc.gpsimd.iota(tile_no[:, :, :], pattern=[[1, NST], [0, NX]], base=0, channel_multiplier=0, **exact)
                nc.gpsimd.iota(steps[:, :, :], pattern=[[0, NX], [TS, MT]], base=0, channel_multiplier=0, **exact)
                nc.gpsimd.iota(score[:, :], pattern=[[TP, NT]], base=1, channel_multiplier=1, **exact)
                nc.gpsimd.iota(spare[:, :], pattern=[[TS, NST]], base=N + 1, channel_multiplier=1, **exact)
                pool_chain.link(pool, nc.gpsimd.memset(place[:, 0, :], 0.0))
                nc.gpsimd.tensor_copy(rows[:, :, D + 3], score[:, :])
                nc.gpsimd.affine_select(out=upto[:, :, :], in_=ones[0:TP, 0:NX * NX].rearrange("p (a b) -> p a b", a=NX),
                                        compare_op=ALU.is_ge, fill=0.0, base=0, pattern=[[1, NX], [-1, NX]],
                                        channel_multiplier=0)
                nc.gpsimd.affine_select(out=before[:, :], in_=ones[:, :], compare_op=ALU.is_gt, fill=0.0,
                                        base=0, pattern=[[1, 128]], channel_multiplier=-1).then_inc(consts5, 1)
                pool.wait_ge(slots_made, 1)
                pool.wait_ge(table_zeroed, 16 * NST)
                for t in range(NT):
                    pool.indirect_dma_start(out=slot_in, out_offset=bass.IndirectOffsetOnAxis(ap=slot[:, t:t + 1], axis=0),
                                            in_=rows[:, t, :], in_offset=None).then_inc(scattered, 16)
                for i in range(NST):
                    pool.wait_ge(f_made, i + 1)
                    pool.indirect_dma_start(out=out, out_offset=bass.IndirectOffsetOnAxis(ap=node_i[i % FR][:, 0:1], axis=0),
                                            in_=fo[i % 2][:, :], in_offset=None).then_inc(out_stored[i % 2], 16)

            @block.scalar
            def _(act):
                act.wait_ge(shifted, 1)
                nc.scalar.activation(prob[:, :, :], logit[:, :, :], ACT.Exp).then_inc(exp_made, 1)

                for i in range(NB):
                    act.wait_ge(bias_spread, i + 1)
                    nc.scalar.copy(bias_all[:, i * 512:(i + 1) * 512], bank[i % 2][0:TS, :]).then_inc(bias_made, 1)

                def norm(i):
                    act.wait_ge(row_loaded[i % FR], 16 * (i // FR + 1))
                    if i >= 2:
                        act.wait_ge(y_turned, i - 1)
                    r = row_in[i % FR]
                    nc.scalar.activation(y[i % 2][:, :], r[:, 0:D], ACT.Identity, scale=r[:, D:D + 1],
                                         bias=r[:, D + 1:D + 2]).then_inc(y_made, 1)

                def turned(i):
                    act.wait_ge(y_turned, i + 1)
                    if i >= 2:
                        act.wait_ge(pre_ready5, i - 1)
                    nc.scalar.copy(yt[i % 2][:, :, :].rearrange("p k n -> p (k n)"), bank[i % 2][:, :]).then_inc(yt_made, 1)

                norm(0)
                norm(1)
                turned(0)
                for i in range(NST):
                    if i + 1 < NST:
                        turned(i + 1)
                    if i + 2 < NST:
                        norm(i + 2)
                    act.wait_ge(hid_turned, i + 1)
                    if i >= 2:
                        act.wait_ge(f_ready, i - 1)
                    nc.scalar.activation(hid[i % 2][:, :, :].rearrange("p k n -> p (k n)"), bank[6 + i % 2][:, 0:HX],
                                         ACT.Relu).then_inc(hid_made, 1)

            @block.vector
            def _(dve):
                L = dve_chain.link

                def over_e(ap):
                    return ap.unsqueeze(2).to_broadcast([TP, NT, NX])

                def over_t(ap):
                    return ap.unsqueeze(1).to_broadcast([TP, NT, NX])

                TT = nc.vector.tensor_tensor
                L(dve, TT(logit[:, :, :], over_e(mv[:, :, 0]), over_t(LOGITS[0:TP, NT * NX:(NT + 1) * NX]), ALU.mult))
                L(dve, TT(logit[:, :, :], LOGITS[0:TP, 0:NT * NX].rearrange("p (t e) -> p t e", e=NX), logit[:, :, :],
                          ALU.subtract))
                L(dve, TT(logit[:, :, :], logit[:, :, :], over_e(rstd[:, :]), ALU.mult))
                dve.wait_ge(bg_loaded, 16)
                L(dve, TT(logit[:, :, :], logit[:, :, :], over_t(bg_sb[:, :]), ALU.add))
                L(dve, nc.vector.tensor_reduce(best[:, :], logit[:, :, :], AX_X, ALU.max))
                TT(logit[:, :, :], logit[:, :, :], over_e(best[:, :]), ALU.subtract).then_inc(shifted, 1)
                dve.wait_ge(shifted, 1)
                dve.wait_ge(consts5, 1)
                L(dve, nc.vector.scalar_tensor_tensor(is_max[:, :, :], logit[:, :, :], 0.0, over_t(e_less[:, :]),
                                                      ALU.is_equal, ALU.mult))
                L(dve, nc.vector.tensor_reduce(best[:, :], is_max[:, :, :], AX_X, ALU.min))
                L(dve, TT(hot_e[:, :, :], over_t(e_less[:, :]), over_e(best[:, :]), ALU.is_equal))
                nc.vector.tensor_reduce(held[:, :], hot_e[:, :, :].rearrange("p t e -> p e t"), AX_X,
                                        ALU.add).then_inc(held_made, 1)
                for t in range(1, NT):
                    L(dve, TT(place[:, t, :], place[:, t - 1, :], hot_e[:, t - 1, :], ALU.add))
                dve.wait_ge(counts_ready, 1)
                L(dve, TT(over[:, :, :], bank[6][0:TP, 0:NX].unsqueeze(2).to_broadcast([TP, NX, MT]), steps[:, :, :],
                          ALU.is_gt))
                L(dve, nc.vector.tensor_reduce(tiles[:, :], over[:, :, :], AX_X, ALU.add))
                L(dve, TT(parts[:, :, :], tiles[:, :].unsqueeze(1).to_broadcast([TP, NX, NX]), upto[:, :, :], ALU.mult))
                L(dve, nc.vector.tensor_reduce(cum[:, :], parts[:, :, :], AX_X, ALU.add))
                L(dve, TT(first[:, :], cum[:, :], tiles[:, :], ALU.subtract))
                L(dve, nc.vector.scalar_tensor_tensor(first[:, :], first[:, :], float(TS), bank[6][0:TP, NX:2 * NX],
                                                      ALU.mult, ALU.add))
                L(dve, TT(place[:, :, :], place[:, :, :], over_t(first[:, :]), ALU.add))
                L(dve, TT(place[:, :, :], place[:, :, :], hot_e[:, :, :], ALU.mult))
                L(dve, nc.vector.tensor_reduce(slot_f[:, :], place[:, :, :], AX_X, ALU.add))
                dve.wait_ge(exp_made, 1)
                L(dve, nc.vector.tensor_reduce(score[:, :], prob[:, :, :], AX_X, ALU.add))
                nc.vector.reciprocal(rows[:, :, D + 2], score[:, :])
                nc.vector.tensor_copy(slot[:, :], slot_f[:, :]).then_inc(slots_made, 1)
                L(dve, TT(past[:, :, :], tile_no[:, :, :], cum[0:1, :].unsqueeze(1).to_broadcast([1, NST, NX]), ALU.is_ge))
                L(dve, nc.vector.tensor_reduce(tile_ef[:, :], past[:, :, :], AX_X, ALU.add))
                nc.vector.tensor_scalar(tile_e[:, :], tile_ef[:, :], float(NX - 1), None, ALU.min).then_inc(tiles_made, 1)
                dve.wait_ge(tiles_made, 1)
                dve.wait_ge(bias_made, NB)

                def result(i, e):
                    r = row_in[i % FR]
                    dve.wait_ge(f_ready, i + 1)
                    if i >= 2:
                        dve.wait_ge(out_stored[i % 2], 16 * (i // 2))
                    L(dve, TT(fo[i % 2][:, :], bank[4 + i % 2][0:TS, :], b2_all[:, bass.ds(e * D, D)], ALU.add))
                    nc.vector.scalar_tensor_tensor(fo[i % 2][:, :], fo[i % 2][:, :], r[:, D + 2:D + 3], r[:, 0:D],
                                                   ALU.mult, ALU.add).then_inc(f_made, 1)

                e_last = None
                for i in range(NST):
                    e = an_expert(dve, i)
                    dve.wait_ge(row_loaded[i % FR], 16 * (i // FR + 1))
                    if i >= FR:
                        dve.wait_ge(out_stored[(i - FR) % 2], 16 * ((i - FR) // 2 + 1))
                    node1 = row_in[i % FR][:, D + 3:D + 4]
                    L(dve, nc.vector.scalar_tensor_tensor(is_spare[i % 2][:, :], node1, 0.0, spare[:, i:i + 1],
                                                          ALU.is_equal, ALU.mult))
                    nc.vector.scalar_tensor_tensor(node_i[i % FR][:, :], node1, -1.0, is_spare[i % 2][:, :],
                                                   ALU.add, ALU.add)
                    dve.wait_ge(pre_ready5, i + 1)
                    if i >= 2:
                        dve.wait_ge(hid_turned, i - 1)
                    TT(pre_hid[i % 2][:, :], bank[2 + i % 2][0:TS, 0:HX], b1_all[:, bass.ds(e * HX, HX)],
                       ALU.add).then_inc(pre_made, 1)
                    if i:
                        result(i - 1, e_last)
                    e_last = e
                result(NST - 1, e_last)

            @block.tensor
            def _(pe):
                pe.wait_ge(held_made, 1)
                pe.wait_ge(consts5, 1)
                nc.tensor.matmul(bank[6][0:TP, 0:NX], ones[0:TP, 0:TP], held[:, :], start=True, stop=True)
                nc.tensor.matmul(bank[6][0:TP, NX:2 * NX], before[0:TP, 0:TP], held[:, :],
                                 start=True, stop=True).then_inc(counts_ready, 1)

                def turn_y(i):
                    pe.wait_ge(y_made, i + 1)
                    if i >= 2:
                        pe.wait_ge(yt_made, i - 1)
                    for k in range(KC):
                        last = nc.tensor.transpose(bank[i % 2][:, k * TS:(k + 1) * TS],
                                                   y[i % 2][:, k * 128:(k + 1) * 128], ident[0:TS, 0:TS])
                    last.then_inc(y_turned, 1)

                def first_layer(i, e):
                    pe.wait_ge(yt_made, i + 1)
                    if i >= 2:
                        pe.wait_ge(pre_made, i - 1)
                    for k in range(KC):
                        last = nc.tensor.matmul(bank[2 + i % 2][0:TS, 0:HX], yt[i % 2][:, k, :], w1_of(e, k),
                                                start=(k == 0), stop=(k == KC - 1))
                    last.then_inc(pre_ready5, 1)

                def w1_of(e, k):
                    return w1_all[:, :, :, :].rearrange("p e k h -> p (e k h)")[:, bass.ds(e * (KC * HX) + k * HX, HX)]

                def turn_hid(i):
                    pe.wait_ge(pre_made, i + 1)
                    if i >= 2:
                        pe.wait_ge(hid_made, i - 1)
                    for m in range(HX // 128):
                        last = nc.tensor.transpose(bank[6 + i % 2][:, m * TS:(m + 1) * TS],
                                                   pre_hid[i % 2][:, m * 128:(m + 1) * 128], ident[0:TS, 0:TS])
                    last.then_inc(hid_turned, 1)

                def second_layer(i, e):
                    pe.wait_ge(hid_made, i + 1)
                    if i >= 2:
                        pe.wait_ge(f_made, i - 1)
                    w2_of = w2_all[:, :, :, :].rearrange("p e k h -> p (e k h)")
                    for m in range(HX // 128):
                        last = nc.tensor.matmul(bank[4 + i % 2][0:TS, :], hid[i % 2][:, m, :],
                                                w2_of[:, bass.ds(e * (HX // 128 * D) + m * D, D)],
                                                start=(m == 0), stop=(m == HX // 128 - 1))
                    last.then_inc(f_ready, 1)

                pe.wait_ge(bias_in, 32)
                for i in range(NB):
                    if i >= 2:
                        pe.wait_ge(bias_made, i - 1)
                    nc.tensor.matmul(bank[i % 2][0:TS, :], ones[0:1, 0:TS], bias_all[0:1, i * 512:(i + 1) * 512],
                                     start=True, stop=True).then_inc(bias_spread, 1)
                pe.wait_ge(tiles_made, 1)
                for i in range(3):
                    pe.wait_ge(experts_loaded[i], 16 * len(range(i, 2 * NX, 3)))
                pe.wait_ge(bias_made, NB)
                turn_y(0)
                e_last = None
                for i in range(NST):
                    e = an_expert(pe, i)
                    first_layer(i, e)
                    if i + 1 < NST:
                        turn_y(i + 1)
                    if i:
                        second_layer(i - 1, e_last)
                    turn_hid(i)
                    e_last = e
                second_layer(NST - 1, e_last)
        s5.close()


def layouts(np, a):
    blocks = lambda w: w.T.reshape(KC, 128, w.shape[0]).transpose(1, 0, 2)
    ih, hh = blocks(a["L0_gnn_W_ih"]), blocks(a["L0_gnn_W_hh"])
    column = lambda v: v.reshape(KC, 128).T
    bih, bhh = a["L0_gnn_b_ih"].reshape(3, D), a["L0_gnn_b_hh"].reshape(3, D)
    return {
        "x_nodes": a["x"],
        "x_feat": a["x"].T,
        "src_blocks": a["src"].reshape(NG, TG, TP).transpose(0, 2, 1),
        "dst_cols": a["dst"].reshape(NG * TG, TP).T,
        "dst_groups": a["dst"].reshape(NG, EG),
        "edge_blocks": a["edge_attr_128"].reshape(NG, EG, ED).transpose(0, 2, 1),
        "w1a": a["L0_gnn_W1"][:, :D].T,
        "w1b": a["L0_gnn_W1"][:, D:].T,
        "wk": a["L0_mix_Wk"], "wv": a["L0_mix_Wv"], "wq": a["L0_mix_Wq"], "wp": a["L0_mix_Wp"],
        "w2": a["L0_gnn_W2"].T,
        "gate_blocks": np.stack([w[:, :, g * D + c * 128:g * D + (c + 1) * 128]
                                 for c in range(KC) for g in range(3) for w in (ih, hh)]),
        "wg": a["L0_ffn_Wg"], "we1": a["L0_ffn_W1"], "we2": a["L0_ffn_W2"],
        "b1": a["L0_gnn_b1"], "bk": a["L0_mix_bk"], "bv": a["L0_mix_bv"], "b2": a["L0_gnn_b2"],
        "cols": np.stack([column(v) for v in (
            a["L0_mix_bq"], a["L0_mix_bp"], bih[0], bih[1], bih[2], bhh[0], bhh[1], bhh[2], a["L0_gnn_gamma"],
            a["L0_gnn_beta"], a["L0_gnn_run_mean"], a["L0_gnn_run_var"])], axis=1),
        "bg": a["L0_ffn_bg"],
        "be1": a["L0_ffn_b1"], "be2": a["L0_ffn_b2"],
    }


def kernel(**inputs):
    import numpy as _np
    import concourse.bacc as _bacc
    from concourse.bass_utils import run_bass_kernel_spmd as _run

    nc = _bacc.Bacc("TRN2", target_bir_lowering=False, num_devices=1)
    arrays, aps = {}, {}
    for name, a in layouts(_np, {k: _np.asarray(v) for k, v in inputs.items()}).items():
        a = _np.ascontiguousarray(a)
        arrays[f"in_{name}"] = a
        aps[name] = nc.dram_tensor(f"in_{name}", a.shape, mybir.dt.from_np(a.dtype), kind="ExternalInput").ap()
    aps["proj"] = nc.dram_tensor("proj_table", (N, D), F32, kind="Internal").ap()
    aps["slot_in"] = nc.dram_tensor("slot_table", (NSLOT, ROW), F32, kind="Internal").ap()
    aps["out"] = nc.dram_tensor("out_x", (N + NSLOT, D), F32, kind="ExternalOutput").ap()
    build(nc, **aps)
    r = _run(nc, [arrays], core_ids=[0])
    return r.results[0]["out_x"][:N]
```
